# Optimizing a Trainium2 kernel written in Bass

```python
import numpy as np
import jax
import jax.numpy as jnp

def _softmax(x, axis=-1):
    return jax.nn.softmax(x, axis=axis)

def _gelu(x):
    return jax.nn.gelu(x, approximate=True)

def _silu(x):
    return jax.nn.silu(x)

def _sigmoid(x):
    return jax.nn.sigmoid(x)

def _layernorm(x, axis=-1, eps=1e-05):
    m = jnp.mean(x, axis=axis, keepdims=True)
    v = jnp.var(x, axis=axis, keepdims=True)
    return (x - m) / jnp.sqrt(v + eps)

def _scatter_add(tgt, idx, src, axis=0):
    return tgt.at[idx].add(src)

def _segment_sum(src, seg, n):
    return jax.ops.segment_sum(src, seg, n)
kernel_name = 'mk_sandwich_d2_jaxref_r8_db4dc8'

def setup_inputs(seed: int=0):
    np.random.seed(seed)
    _w = jnp.asarray

    def _L0_attn_setup():
        import jax, jax.numpy as jnp
        import numpy as np
        import math
        B, S, E = (2, 256, 128)
        H, DK, DV = (16, 64, 64)

        def _rope(q, k):
            D = q.shape[-1]
            theta = 10000.0 ** (jnp.arange(0, D, 2, dtype=jnp.float32) / D)
            pos = jnp.arange(q.shape[-2], dtype=jnp.float32)
            freqs = pos[:, None] * (1.0 / theta)[None, :]
            emb = jnp.concatenate([freqs, freqs], axis=-1)
            cos = jnp.cos(emb)[None, None]
            sin = jnp.sin(emb)[None, None]

            def rotate(x):
                x1 = x[..., ::2]
                x2 = x[..., 1::2]
                return jnp.stack([-x2, x1], axis=-1).reshape(x.shape)
            return (q * cos + rotate(q) * sin, k * cos + rotate(k) * sin)
        key = jax.random.key(seed)
        ks = jax.random.split(key, 9)
        sE = 1.0 / math.sqrt(E)
        sV = 1.0 / math.sqrt(H * DV)
        return {'x': jax.random.normal(ks[0], (B, S, E), dtype=jnp.float32), 'wq': jax.random.uniform(ks[1], (H * DK, E), jnp.float32, -sE, sE), 'bq': jax.random.uniform(ks[2], (H * DK,), jnp.float32, -sE, sE), 'wk': jax.random.uniform(ks[3], (H * DK, E), jnp.float32, -sE, sE), 'bk': jax.random.uniform(ks[4], (H * DK,), jnp.float32, -sE, sE), 'wv': jax.random.uniform(ks[5], (H * DV, E), jnp.float32, -sE, sE), 'bv': jax.random.uniform(ks[6], (H * DV,), jnp.float32, -sE, sE), 'wo': jax.random.uniform(ks[7], (E, H * DV), jnp.float32, -sV, sV), 'bo': jax.random.uniform(ks[8], (E,), jnp.float32, -sV, sV)}
    _L0_attn_in = _L0_attn_setup()

    def _L0_ffn_setup():
        import jax, jax.numpy as jnp
        import numpy as np
        from jax import lax
        HIDDEN = 128
        INTER = 64
        E = 64
        K = 6
        G = 8
        TG = 4
        NSH = 2
        ISH = INTER * NSH

        def _moe_forward(hidden_states, gate_w, gate_bias, eg_w, eu_w, ed_w, sg_w, su_w, sd_w):
            B, S, H = hidden_states.shape
            x = hidden_states.reshape(-1, H)
            T = x.shape[0]
            shared = jax.nn.silu(x @ sg_w.T) * (x @ su_w.T) @ sd_w.T
            logits = x @ gate_w.T
            scores = jax.nn.sigmoid(logits) + gate_bias
            group_scores = scores.reshape(T, G, E // G).max(axis=-1)
            _, sel_groups = lax.top_k(group_scores, TG)
            group_mask = jnp.zeros((T, G), scores.dtype).at[jnp.arange(T)[:, None], sel_groups].set(1.0)
            mask = jnp.repeat(group_mask, E // G, axis=1)
            masked_scores = scores * mask
            topk_w, topk_i = lax.top_k(masked_scores, K)
            topk_w = topk_w / (topk_w.sum(axis=-1, keepdims=True) + 1e-08)
            comb = jnp.zeros((T, E), x.dtype).at[jnp.arange(T)[:, None], topk_i].add(topk_w)
            h = jax.nn.silu(jnp.einsum('th,eih->eti', x, eg_w)) * jnp.einsum('th,eih->eti', x, eu_w)
            routed = jnp.einsum('eti,ehi,te->th', h, ed_w, comb)
            return (shared + routed).reshape(B, S, H)
        key = jax.random.key(seed)
        ks = jax.random.split(key, 9)
        s = 0.02
        return {'hidden_states': jax.random.normal(ks[0], (1, 128, HIDDEN), jnp.float32), 'gate_w': jax.random.normal(ks[1], (E, HIDDEN), jnp.float32) * s, 'gate_bias': jnp.zeros((E,), jnp.float32), 'eg_w': jax.random.normal(ks[2], (E, INTER, HIDDEN), jnp.float32) * s, 'eu_w': jax.random.normal(ks[3], (E, INTER, HIDDEN), jnp.float32) * s, 'ed_w': jax.random.normal(ks[4], (E, HIDDEN, INTER), jnp.float32) * s, 'sg_w': jax.random.normal(ks[5], (ISH, HIDDEN), jnp.float32) * s, 'su_w': jax.random.normal(ks[6], (ISH, HIDDEN), jnp.float32) * s, 'sd_w': jax.random.normal(ks[7], (HIDDEN, ISH), jnp.float32) * s}
    _L0_ffn_in = _L0_ffn_setup()

    def _L1_attn_setup():
        import jax, jax.numpy as jnp
        import numpy as np
        from jax import lax
        D_MODEL, D_STATE, D_CONV, EXPAND = (128, 16, 4, 2)
        D_INNER = EXPAND * D_MODEL
        B, L = (2, 256)
        key = jax.random.key(seed)
        ks = jax.random.split(key, 8)
        s_in = 1.0 / np.sqrt(D_MODEL)
        s_xp = 1.0 / np.sqrt(D_INNER)
        x = jax.random.normal(ks[0], (B, L, D_MODEL), dtype=jnp.float32)
        W_in = jax.random.uniform(ks[1], (2 * D_INNER, D_MODEL), minval=-s_in, maxval=s_in)
        conv_w = jax.random.uniform(ks[2], (D_INNER, 1, D_CONV), minval=-0.5, maxval=0.5)
        conv_b = jax.random.uniform(ks[3], (D_INNER,), minval=-0.5, maxval=0.5)
        W_xproj = jax.random.uniform(ks[4], (1 + 2 * D_STATE, D_INNER), minval=-s_xp, maxval=s_xp)
        W_dt = jax.random.uniform(ks[5], (D_INNER, 1), minval=-1.0, maxval=1.0)
        b_dt = jax.random.uniform(ks[6], (D_INNER,), minval=-1.0, maxval=1.0)
        A_log = jnp.log(jnp.broadcast_to(jnp.arange(1, D_STATE + 1, dtype=jnp.float32), (D_INNER, D_STATE)))
        D = jnp.ones((D_INNER,), dtype=jnp.float32)
        W_out = jax.random.uniform(ks[7], (D_MODEL, D_INNER), minval=-s_xp, maxval=s_xp)
        return {'x': x, 'W_in': W_in, 'conv_w': conv_w, 'conv_b': conv_b, 'W_xproj': W_xproj, 'W_dt': W_dt, 'b_dt': b_dt, 'A_log': A_log, 'D': D, 'W_out': W_out}
    _L1_attn_in = _L1_attn_setup()

    def _L1_ffn_setup():
        import jax, jax.numpy as jnp
        import numpy as np
        D_MODEL = 128
        EXPERT_DIM = 64
        N_EXPERTS = 8
        TOP_K = 2

        def _sq_relu(h):
            return jnp.square(jax.nn.relu(h))
        key = jax.random.key(seed)
        ks = jax.random.split(key, 6)
        s = 0.02
        x = jax.random.normal(ks[0], (2, 256, D_MODEL), dtype=jnp.float32)
        Ws1 = jax.random.normal(ks[1], (D_MODEL, EXPERT_DIM), dtype=jnp.float32) * s
        Ws2 = jax.random.normal(ks[2], (EXPERT_DIM, D_MODEL), dtype=jnp.float32) * s
        W1 = jax.random.normal(ks[3], (N_EXPERTS, D_MODEL, EXPERT_DIM), dtype=jnp.float32) * s
        W2 = jax.random.normal(ks[4], (N_EXPERTS, EXPERT_DIM, D_MODEL), dtype=jnp.float32) * s
        Wr = jax.random.normal(ks[5], (D_MODEL, N_EXPERTS), dtype=jnp.float32) * s
        return {'x': x, 'Ws1': Ws1, 'Ws2': Ws2, 'W1': W1, 'W2': W2, 'Wr': Wr}
    _L1_ffn_in = _L1_ffn_setup()
    _d = {'L0_attn_x': _L0_attn_in['x'], 'L0_attn_wq': _L0_attn_in['wq'], 'L0_attn_bq': _L0_attn_in['bq'], 'L0_attn_wk': _L0_attn_in['wk'], 'L0_attn_bk': _L0_attn_in['bk'], 'L0_attn_wv': _L0_attn_in['wv'], 'L0_attn_bv': _L0_attn_in['bv'], 'L0_attn_wo': _L0_attn_in['wo'], 'L0_attn_bo': _L0_attn_in['bo'], 'L0_ffn_gate_w': _L0_ffn_in['gate_w'], 'L0_ffn_gate_bias': _L0_ffn_in['gate_bias'], 'L0_ffn_eg_w': _L0_ffn_in['eg_w'], 'L0_ffn_eu_w': _L0_ffn_in['eu_w'], 'L0_ffn_ed_w': _L0_ffn_in['ed_w'], 'L0_ffn_sg_w': _L0_ffn_in['sg_w'], 'L0_ffn_su_w': _L0_ffn_in['su_w'], 'L0_ffn_sd_w': _L0_ffn_in['sd_w'], 'L1_attn_W_in': _L1_attn_in['W_in'], 'L1_attn_conv_w': _L1_attn_in['conv_w'], 'L1_attn_conv_b': _L1_attn_in['conv_b'], 'L1_attn_W_xproj': _L1_attn_in['W_xproj'], 'L1_attn_W_dt': _L1_attn_in['W_dt'], 'L1_attn_b_dt': _L1_attn_in['b_dt'], 'L1_attn_A_log': _L1_attn_in['A_log'], 'L1_attn_D': _L1_attn_in['D'], 'L1_attn_W_out': _L1_attn_in['W_out'], 'L1_ffn_Ws1': _L1_ffn_in['Ws1'], 'L1_ffn_Ws2': _L1_ffn_in['Ws2'], 'L1_ffn_W1': _L1_ffn_in['W1'], 'L1_ffn_W2': _L1_ffn_in['W2'], 'L1_ffn_Wr': _L1_ffn_in['Wr']}
    _x0 = _d['L0_attn_x']
    _d['L0_attn_x'] = jax.random.normal(jax.random.fold_in(jax.random.key(seed), 1), (8, 512, 128), dtype=_x0.dtype)
    del _x0
    return _d

def reference(L0_attn_x, L0_attn_wq, L0_attn_bq, L0_attn_wk, L0_attn_bk, L0_attn_wv, L0_attn_bv, L0_attn_wo, L0_attn_bo, L0_ffn_gate_w, L0_ffn_gate_bias, L0_ffn_eg_w, L0_ffn_eu_w, L0_ffn_ed_w, L0_ffn_sg_w, L0_ffn_su_w, L0_ffn_sd_w, L1_attn_W_in, L1_attn_conv_w, L1_attn_conv_b, L1_attn_W_xproj, L1_attn_W_dt, L1_attn_b_dt, L1_attn_A_log, L1_attn_D, L1_attn_W_out, L1_ffn_Ws1, L1_ffn_Ws2, L1_ffn_W1, L1_ffn_W2, L1_ffn_Wr):

    def _L0_attn_ref(x, wq, bq, wk, bk, wv, bv, wo, bo):
        import jax, jax.numpy as jnp
        import numpy as np
        import math
        B, S, E = (2, 256, 128)
        H, DK, DV = (16, 64, 64)

        def _rope(q, k):
            D = q.shape[-1]
            theta = 10000.0 ** (jnp.arange(0, D, 2, dtype=jnp.float32) / D)
            pos = jnp.arange(q.shape[-2], dtype=jnp.float32)
            freqs = pos[:, None] * (1.0 / theta)[None, :]
            emb = jnp.concatenate([freqs, freqs], axis=-1)
            cos = jnp.cos(emb)[None, None]
            sin = jnp.sin(emb)[None, None]

            def rotate(x):
                x1 = x[..., ::2]
                x2 = x[..., 1::2]
                return jnp.stack([-x2, x1], axis=-1).reshape(x.shape)
            return (q * cos + rotate(q) * sin, k * cos + rotate(k) * sin)
        Bx, Sx, Ex = x.shape
        q = (x @ wq.T + bq).reshape(Bx, Sx, H, DK).transpose(0, 2, 1, 3)
        k = (x @ wk.T + bk).reshape(Bx, Sx, H, DK).transpose(0, 2, 1, 3)
        v = (x @ wv.T + bv).reshape(Bx, Sx, H, DV).transpose(0, 2, 1, 3)
        q, k = _rope(q, k)
        scores = jnp.einsum('bhqd,bhkd->bhqk', q, k)
        causal = jnp.triu(jnp.ones((Sx, Sx), dtype=bool), k=1)
        scores = jnp.where(causal[None, None], -jnp.inf, scores)
        attn = jax.nn.softmax(scores / math.sqrt(DK), axis=-1)
        out = jnp.einsum('bhqk,bhkd->bhqd', attn, v)
        out = out.transpose(0, 2, 1, 3).reshape(Bx, Sx, H * DV)
        return out @ wo.T + bo

    def _L0_ffn_ref(hidden_states, gate_w, gate_bias, eg_w, eu_w, ed_w, sg_w, su_w, sd_w):
        import jax, jax.numpy as jnp
        import numpy as np
        from jax import lax
        HIDDEN = 128
        INTER = 64
        E = 64
        K = 6
        G = 8
        TG = 4
        NSH = 2
        ISH = INTER * NSH

        def _moe_forward(hidden_states, gate_w, gate_bias, eg_w, eu_w, ed_w, sg_w, su_w, sd_w):
            B, S, H = hidden_states.shape
            x = hidden_states.reshape(-1, H)
            T = x.shape[0]
            shared = jax.nn.silu(x @ sg_w.T) * (x @ su_w.T) @ sd_w.T
            logits = x @ gate_w.T
            scores = jax.nn.sigmoid(logits) + gate_bias
            group_scores = scores.reshape(T, G, E // G).max(axis=-1)
            _, sel_groups = lax.top_k(group_scores, TG)
            group_mask = jnp.zeros((T, G), scores.dtype).at[jnp.arange(T)[:, None], sel_groups].set(1.0)
            mask = jnp.repeat(group_mask, E // G, axis=1)
            masked_scores = scores * mask
            topk_w, topk_i = lax.top_k(masked_scores, K)
            topk_w = topk_w / (topk_w.sum(axis=-1, keepdims=True) + 1e-08)
            comb = jnp.zeros((T, E), x.dtype).at[jnp.arange(T)[:, None], topk_i].add(topk_w)
            h = jax.nn.silu(jnp.einsum('th,eih->eti', x, eg_w)) * jnp.einsum('th,eih->eti', x, eu_w)
            routed = jnp.einsum('eti,ehi,te->th', h, ed_w, comb)
            return (shared + routed).reshape(B, S, H)
        return _moe_forward(hidden_states, gate_w, gate_bias, eg_w, eu_w, ed_w, sg_w, su_w, sd_w)

    def _L1_attn_ref(x, W_in, conv_w, conv_b, W_xproj, W_dt, b_dt, A_log, D, W_out):
        import jax, jax.numpy as jnp
        import numpy as np
        from jax import lax
        D_MODEL, D_STATE, D_CONV, EXPAND = (128, 16, 4, 2)
        D_INNER = EXPAND * D_MODEL
        B, L = (2, 256)
        b, l, _ = x.shape
        d_state = A_log.shape[1]
        d_conv = conv_w.shape[-1]
        xz = x @ W_in.T
        x_in, z = jnp.split(xz, 2, axis=-1)
        lhs = jnp.pad(x_in.transpose(0, 2, 1), ((0, 0), (0, 0), (d_conv - 1, 0)))
        conv = lax.conv_general_dilated(lhs, conv_w, window_strides=(1,), padding='VALID', dimension_numbers=('NCW', 'OIW', 'NCW'), feature_group_count=conv_w.shape[0])
        x_conv = jax.nn.silu(conv.transpose(0, 2, 1) + conv_b)
        ssm_in = x_conv @ W_xproj.T
        dt_raw = ssm_in[..., :1]
        B_ssm = ssm_in[..., 1:1 + d_state]
        C_ssm = ssm_in[..., 1 + d_state:]
        delta = jax.nn.softplus(dt_raw @ W_dt.T + b_dt)
        A = -jnp.exp(A_log)
        deltaA = jnp.exp(delta[..., None] * A)
        deltaB_u = delta[..., None] * B_ssm[:, :, None, :] * x_conv[..., None]

        def step(h, inp):
            dA, dBu, c = inp
            h = dA * h + dBu
            y = jnp.einsum('bds,bs->bd', h, c)
            return (h, y)
        h0 = jnp.zeros((b, deltaA.shape[2], d_state), dtype=x.dtype)
        _, ys = lax.scan(step, h0, (deltaA.transpose(1, 0, 2, 3), deltaB_u.transpose(1, 0, 2, 3), C_ssm.transpose(1, 0, 2)))
        y = ys.transpose(1, 0, 2) + x_conv * D
        y = y * jax.nn.silu(z)
        return y @ W_out.T

    def _L1_ffn_ref(x, Ws1, Ws2, W1, W2, Wr):
        import jax, jax.numpy as jnp
        import numpy as np
        D_MODEL = 128
        EXPERT_DIM = 64
        N_EXPERTS = 8
        TOP_K = 2

        def _sq_relu(h):
            return jnp.square(jax.nn.relu(h))
        shape = x.shape
        xf = x.reshape(-1, D_MODEL)
        out_shared = _sq_relu(xf @ Ws1) @ Ws2
        logits = xf @ Wr
        top_vals, top_idx = jax.lax.top_k(logits, TOP_K)
        rw = jax.nn.softmax(top_vals.astype(jnp.float32), axis=-1).astype(x.dtype)
        onehot = jax.nn.one_hot(top_idx, N_EXPERTS, dtype=x.dtype)
        prob = jnp.einsum('tk,tke->te', rw, onehot)
        prob = jnp.trunc(prob)
        h = _sq_relu(jnp.einsum('td,edf->tef', xf, W1))
        y = jnp.einsum('tef,efd->ted', h, W2)
        out_routed = jnp.einsum('ted,te->td', y, prob)
        return (out_shared + out_routed).reshape(shape)
    x = L0_attn_x
    x = x + _layernorm(_L0_attn_ref(_layernorm(x, axis=-1), L0_attn_wq, L0_attn_bq, L0_attn_wk, L0_attn_bk, L0_attn_wv, L0_attn_bv, L0_attn_wo, L0_attn_bo), axis=-1)
    x = x + _layernorm(_L0_ffn_ref(_layernorm(x, axis=-1), L0_ffn_gate_w, L0_ffn_gate_bias, L0_ffn_eg_w, L0_ffn_eu_w, L0_ffn_ed_w, L0_ffn_sg_w, L0_ffn_su_w, L0_ffn_sd_w), axis=-1)
    x = x + _layernorm(_L1_attn_ref(_layernorm(x, axis=-1), L1_attn_W_in, L1_attn_conv_w, L1_attn_conv_b, L1_attn_W_xproj, L1_attn_W_dt, L1_attn_b_dt, L1_attn_A_log, L1_attn_D, L1_attn_W_out), axis=-1)
    x = x + _layernorm(_L1_ffn_ref(_layernorm(x, axis=-1), L1_ffn_Ws1, L1_ffn_Ws2, L1_ffn_W1, L1_ffn_W2, L1_ffn_Wr), axis=-1)
    return x

_drawn_inputs = setup_inputs


def setup_inputs(seed=0):
    import zlib

    import numpy as np

    out = dict(_drawn_inputs(seed))
    spreads = {'L0_ffn_gate_bias': (0.0, 0.1), 'L1_attn_D': (1.0, 0.2)}
    factors = {'L0_attn_bk': 3.24,
     'L1_attn_W_xproj': 4.324,
     'L1_attn_W_dt': 8.0,
     'L1_attn_b_dt': 4.169,
     'L1_attn_A_log': 8.0}
    for name, (base, spread) in spreads.items():
        noise = np.random.default_rng([zlib.crc32(name.encode()), seed]).standard_normal(out[name].shape)
        drawn = base * np.exp(spread * noise) if base else spread * noise
        out[name] = jnp.asarray(drawn.astype(out[name].dtype))
    for name, factor in factors.items():
        out[name] = (out[name] * factor).astype(out[name].dtype)
    return out
```

```python
from contextlib import ExitStack

import concourse.bass as bass
from concourse import mybir

F32 = mybir.dt.float32
F32R = mybir.dt.float32r
ALU = mybir.AluOpType
ACT = mybir.ActivationFunctionType
AX = mybir.AxisListType

P = 128
NB = 8
S = 512
NT = S // P
D = 128
H = 16
DK = 64
NP = H // 2
E, G, TG, TK = 64, 8, 4, 6
NJ = 1 + E // 2
DI, DS, DC = 256, 16, 4
NI = DI // P
E2 = 8
NJ2 = 1 + E2 // 2
EPS = 1e-5
MASKED = -1e30
TOP = 3e38
TAKEN = -3e38

def columns(parts):
    at, where = 0, {}
    for name, n in parts:
        where[name] = (at, at + n)
        at += n
    return where, at


SMALL, NSMALL = columns([
    ("ident", P), ("cosq", S), ("sinq", S), ("cosk", S), ("sink", S), ("bqk", NP * 4), ("bv", NP), ("bo", 1),
    ("gbias", NT * E), ("convw", NI * DC), ("convb", NI), ("wx", NI * 33), ("wdt", NI), ("bdt", NI),
    ("alog", NI * DS), ("dskip", NI), ("wout", NI * D)])
ONCE, NONCE = columns([("eye", P), ("mask", P), ("sel", 1024), ("sel8", 512), ("i64", 32), ("gate", E), ("wr", E2)])
PART_OFF = [0, 512, 1024, 896]
PROB_OFF = [0, 128, 384, 768]


def layers_kernel(nc, x_in, small_in, once_in, wqk_in, wv_in, wo_in, wg_in, wu_in, wd_in, win_in, w1_in, w2_in, out):
    ctx = ExitStack()
    with ctx:
        def sb(name, shape, dt=F32):
            return ctx.enter_context(nc.sbuf_tensor(name, shape, dt))

        small = sb("small", [P, NSMALL])

        def sm(name):
            a, b = SMALL[name]
            return small[:, a:b]

        wv_h, wv_l = sb("wv_h", [P, H * DK], F32R), sb("wv_l", [P, H * DK], F32R)
        wo_h, wo_l = sb("wo_h", [P, NP, D], F32R), sb("wo_l", [P, NP, D], F32R)
        wg_h, wg_l = sb("wg_h", [P, NJ * P], F32R), sb("wg_l", [P, NJ * P], F32R)
        wu_h, wu_l = sb("wu_h", [P, NJ * P], F32R), sb("wu_l", [P, NJ * P], F32R)
        wd = sb("wd", [P, NJ, D])
        win_h, win_l = sb("win_h", [P, 2 * DI], F32R), sb("win_l", [P, 2 * DI], F32R)
        w1_h, w1_l = sb("w1_h", [P, NJ2 * P], F32R), sb("w1_l", [P, NJ2 * P], F32R)
        w2 = sb("w2", [P, NJ2, D])
        gate_h, gate_l = sb("gate_h", [P, E], F32R), sb("gate_l", [P, E], F32R)
        wr_h, wr_l = sb("wr_h", [P, E2], F32R), sb("wr_l", [P, E2], F32R)
        ident_r, mask_r = sb("ident_r", [P, P], F32R), sb("mask_r", [P, P], F32R)
        i64_r = sb("i64_r", [P, 32], F32R)
        sel_r, sel8_r = sb("sel_r", [P, 1024], F32R), sb("sel8_r", [P, 512], F32R)
        negA = sb("negA", [P, NI * DS])
        half_neg = sb("half_neg", [P, NT])
        ident = sm("ident")

        x = sb("x", [P, NT, D])
        xn = sb("xn", [P, NT, D])
        xT_h, xT_l = sb("xT_h", [P, S], F32R), sb("xT_l", [P, S], F32R)
        yT = xn[:, :, :].rearrange("p a b -> p (a b)")
        stats, mv = sb("stats", [P, NT, 6]), sb("mv", [P, NT, 2])
        ve, rstd = sb("ve", [P, NT]), sb("rstd", [P, NT])

        WORK, WORKR = 10800, 7168
        work, workr = sb("work", [P, WORK]), sb("workr", [P, WORKR], F32R)
        free, freer = [0], [0]

        def piece(*dims, dt=F32):
            n = 1
            for d in dims:
                n *= d
            space, at = (work, free) if dt == F32 else (workr, freer)
            assert at[0] + n <= (WORK if dt == F32 else WORKR), (at[0], n)
            a = space[:, at[0]:at[0] + n]
            at[0] += n
            if len(dims) == 2:
                a = a.rearrange("p (a b) -> p a b", b=dims[1])
            if len(dims) == 3:
                a = a.rearrange("p (a b c) -> p a b c", b=dims[1], c=dims[2])
            return a

        v = piece(NT, H * DK)
        wqk = piece(2, 2, 4 * P, dt=F32R)
        ropeA, ropeB = piece(2, S), piece(S)
        q_h, q_l, k_h, k_l = (piece(2, S, dt=F32R) for _ in range(4))
        prob = piece(2, 1280)
        probT = piece(2, 1280)
        o_h, o_l = piece(S, dt=F32R), piece(S, dt=F32R)
        nmax, rsum, rinv = piece(8), piece(8), piece(8)
        free[0] = freer[0] = 0
        sg = piece(2, S)
        hid = piece(3, S)
        sc = piece(NT, E)
        gm, gr = piece(NT, G + 4), piece(NT, G + 4)
        g8 = piece(NT, 8)
        gmask = piece(NT, G)
        ms, sr = piece(NT, E + 2), piece(NT, E + 2)
        s8 = piece(NT, 8)
        csum = piece(NT)
        comb = piece(NT, E)
        cs = piece(NT, P)
        combT = piece(S, dt=F32R)
        free[0] = freer[0] = 0
        xin = piece(NI, S + DC - 1)
        ca, cb = piece(NI, S), piece(NI, S)
        u, sz = piece(NI, S), piece(NI, S)
        xs, delta, du = piece(NI, S), piece(NI, S), piece(NI, S)
        bc_r = piece(S, dt=F32R)
        Bs, dBu = piece(2, S), piece(2, S)
        dA, hc, hs = xs, ca, [cb[:, 0, :], cb[:, 1, :], piece(S)]
        free[0] = freer[0] = 0
        r2, rp2, h2 = piece(2, S), piece(2, S), piece(2, S)
        lg = piece(NT, E2)
        v8 = piece(NT, 8)
        e2, gate2 = piece(NT), piece(NT)
        pr2 = piece(NT, E2)
        pT2 = piece(S, dt=F32R)
        free[0] = freer[0] = 0
        raw, raw2 = piece(NJ * P), piece(NJ * P)
        once = piece(NONCE)
        raw_h, raw_l = piece(1024, dt=F32R), piece(1024, dt=F32R)

        def on(name):
            a, b = ONCE[name]
            return once[:, a:b]


        bk = [ctx.enter_context(nc.psum_tensor(f"bank{i}", [P, S], F32)) for i in range(8)]
        wqk_split = nc.dram_tensor("wqk_split", (NP, P, 2, 4 * P), F32, kind="Internal").ap()

        names0 = ["w_in", "small_in_", "split_h", "split_l", "store_qk"]
        s0 = {n: ctx.enter_context(nc.semaphore(n)) for n in names0}
        jobs = []
        load_small = s0["small_in_"]
        NQK = NP * 4 * P // 1024
        with nc.Block() as block:
            loads = [(raw[:, 0:1024], wv_in, wv_h[:, :], wv_l[:, :]),
                     (raw[:, 1024:2048], wo_in, wo_h[:, :, :].rearrange("p a b -> p (a b)"), wo_l[:, :, :].rearrange("p a b -> p (a b)")),
                     (raw[:, 2048:2560], win_in, win_h[:, :], win_l[:, :]),
                     (raw[:, 2560:3200], w1_in, w1_h[:, :], w1_l[:, :]),
                     (raw2[:, :], wg_in, wg_h[:, :], wg_l[:, :]),
                     (raw[:, :], wu_in, wu_h[:, :], wu_l[:, :])]
            qk_loads = [(raw[:, 1024 * (c % 2):1024 * (c % 2) + 1024], wqk_in[:, 1024 * c:1024 * c + 1024]) for c in range(NQK)]
            NL = len(loads)

            @block.sync
            def _(sp):
                sp.dma_start(small[:, :], small_in).then_inc(s0["small_in_"], 16)
                sp.dma_start(once, once_in).then_inc(s0["small_in_"], 16)
                sp.wait_ge(s0["small_in_"], 32)
                for dst, src, _, _ in loads:
                    if src is wu_in:
                        sp.wait_ge(s0["split_l"], 4)
                    sp.dma_start(dst, src).then_inc(s0["w_in"], 16)
                sp.wait_ge(s0["w_in"], 16 * NL)
                sp.dma_start(wd[:, :, :].rearrange("p a b -> p (a b)"), wd_in).then_inc(s0["small_in_"], 16)
                sp.dma_start(w2[:, :, :].rearrange("p a b -> p (a b)"), w2_in).then_inc(s0["small_in_"], 16)
                for c, (dst, src) in enumerate(qk_loads):
                    sp.wait_ge(s0["split_l"], NL + c - 1 if c else NL)
                    sp.dma_start(dst, src).then_inc(s0["w_in"], 16)
                    sp.wait_ge(s0["w_in"], 16 * (NL + c + 1))
                    sp.wait_ge(s0["split_l"], NL + c + 1)
                    for h in range(2):
                        for part, t in ((0, raw_h), (1, raw_l)):
                            sp.dma_start(wqk_split[2 * c + h, :, part, :], t[:, 512 * h:512 * h + 512].bitcast(F32)).then_inc(s0["store_qk"], 16)
                    sp.wait_ge(s0["store_qk"], 64 * (c + 1))
                sp.wait_ge(s0["small_in_"], 64)

            @block.scalar
            def _(act):
                for n, (t, _, hi, _) in enumerate(loads):
                    act.wait_ge(s0["w_in"], 16 * (NL if n == NL - 1 else NL - 1))
                    nc.scalar.activation(hi, t, ACT.Copy).then_inc(s0["split_h"], 1)
                for c, (t, _) in enumerate(qk_loads):
                    act.wait_ge(s0["w_in"], 16 * (NL + c + 1))
                    if c:
                        act.wait_ge(s0["store_qk"], 64 * c)
                    nc.scalar.activation(raw_h, t, ACT.Copy).then_inc(s0["split_h"], 1)
                act.wait_ge(s0["small_in_"], 32)
                nc.scalar.activation(negA[:, :], sm("alog"), ACT.Exp).then_inc(s0["split_h"], 1)
                act.wait_ge(s0["split_h"], NL + NQK + 1)
                nc.scalar.mul(negA[:, :], negA[:, :], -1.0)

            @block.vector
            def _(dve):
                for n, (t, _, hi, lo) in enumerate(loads):
                    dve.wait_ge(s0["split_h"], n + 1)
                    nc.vector.tensor_tensor(lo, t, hi.bitcast(F32), ALU.subtract).then_inc(s0["split_l"], 1)
                for c, (t, _) in enumerate(qk_loads):
                    dve.wait_ge(s0["split_h"], NL + c + 1)
                    if c:
                        dve.wait_ge(s0["store_qk"], 64 * c)
                    nc.vector.tensor_tensor(raw_l, t, raw_h.bitcast(F32), ALU.subtract).then_inc(s0["split_l"], 1)
                dve.wait_ge(s0["small_in_"], 32)
                nc.vector.tensor_copy(gate_h[:, :], on("gate")).then_inc(s0["split_l"], 1)
                nc.vector.tensor_copy(wr_h[:, :], on("wr")).then_inc(s0["split_l"], 1)
                dve.wait_ge(s0["split_l"], NL + NQK + 2)
                nc.vector.tensor_tensor(gate_l[:, :], on("gate"), gate_h[:, :].bitcast(F32), ALU.subtract)
                nc.vector.tensor_tensor(wr_l[:, :], on("wr"), wr_h[:, :].bitcast(F32), ALU.subtract)
                for t, name in ((ident_r, "eye"), (mask_r, "mask"), (i64_r, "i64"), (sel_r, "sel"), (sel8_r, "sel8")):
                    nc.vector.tensor_copy(t[:, :], on(name))

            @block.gpsimd
            def _(pool):
                nc.gpsimd.memset(half_neg[:, :], -0.5)

        names = """x_in_ x_out pow_ask pow_done xn_ready xn_turned xT_h_done xT_l_done sub_done y_copied y_turned
            dve_seq act_seq wqk0 wqk1 v_made v_kept_a v_kept_d proj_made rope_terms rope_sum rope_h_done rope_l_done
            s_made max_done exp_done rinv_done norm_done pt_made pt_kept_a pt_kept_d pv_made o_h_done o_l_done wo_made
            lg_made lg_exp comb_turned comb_ask combT_done gu_made silu_done act1_done c_made hid_done down_made
            xz_made xin_done sz_done conv_done u_done xp_made bc_done xs_done sp_exp sp_w1 sp_ln delta_done
            B_made C_made Bs_done dA_done dBu_done scan_done hc_done y_made y2_done
            l2_made l2_exp l2_ask p2_ask p2_turned pT2_done up2_made relu_done p2_made h2_done down2_made""".split()
        sem = {n: ctx.enter_context(nc.semaphore(n)) for n in names}
        first, last = sem[names[0]], sem[names[-1]]

        with nc.Fori(0, NB) as b:
            with nc.Block() as block:
                @block.sync
                def _(sp):
                    def load_wqk(p):
                        if p >= 2:
                            sp.wait_ge(sem["proj_made"], 4 * (p - 1))
                        sp.dma_start(wqk[:, p % 2, :, :].bitcast(F32), wqk_split[p]).then_inc(sem[f"wqk{p % 2}"], 16)

                    xb = x_in[bass.ds(b, 1)].rearrange("o (t p) d -> (o p) t d", p=P)
                    ob = out[bass.ds(b, 1)].rearrange("o (t p) d -> (o p) t d", p=P)
                    sp.dma_start(x[:, :, :], xb).then_inc(sem["x_in_"], 16)
                    for p in range(NP):
                        load_wqk(p)
                    sp.wait_ge(sem["x_out"], 1)
                    sp.dma_start(ob, x[:, :, :]).then_inc(sem["x_in_"], 16)
                    sp.wait_ge(sem["x_in_"], 32)

                @block.tensor
                def _(pe):
                    mm = nc.tensor.matmul

                    def mm3(o, wh, wl, mh, ml, start=True, stop=True):
                        mm(o, wh, mh, start=start, stop=False)
                        mm(o, wh, ml, start=False, stop=False)
                        return mm(o, wl, mh, start=False, stop=stop)

                    def turn_xn(k):
                        pe.wait_ge(sem["xn_ready"], k + 1)
                        for t in range(NT):
                            last = nc.tensor.transpose(bk[7][:, t * P:(t + 1) * P], xn[:, t, :], ident)
                        last.then_inc(sem["xn_turned"], 1)

                    def turn_y(k):
                        pe.wait_ge(sem["y_copied"], k + 1)
                        for t in range(NT):
                            last = nc.tensor.transpose(bk[7][:, t * P:(t + 1) * P], yT[:, t * P:(t + 1) * P], ident)
                        last.then_inc(sem["y_turned"], 1)

                    def wait_xT(k):
                        pe.wait_ge(sem["xT_h_done"], k + 1)
                        pe.wait_ge(sem["xT_l_done"], k + 1)

                    def attention():
                        wait_xT(0)
                        for n in range(2 * NT):
                            t, hf = divmod(n, 2)
                            if n >= 2:
                                pe.wait_ge(sem["v_kept_d" if n % 2 else "v_kept_a"], n // 2)
                            tt, cc = slice(t * P, (t + 1) * P), slice(hf * 512, hf * 512 + 512)
                            mm3(bk[3 + n % 2][:, :], xT_h[:, tt], xT_l[:, tt], wv_h[:, cc], wv_l[:, cc]).then_inc(sem["v_made"], 1)
                        pe.wait_ge(sem["v_kept_a"], NT)
                        pe.wait_ge(sem["v_kept_d"], NT)

                        def project(p, kind):
                            n = 4 * p + kind
                            if kind == 0:
                                pe.wait_ge(sem[f"wqk{p % 2}"], 16 * (p // 2 + 1))
                            if n:
                                pe.wait_ge(sem["rope_terms"], n)
                            c = slice(kind * P, kind * P + P)
                            mm3(bk[7][:, :], wqk[:, p % 2, 0, c], wqk[:, p % 2, 1, c], xT_h[:, :], xT_l[:, :]).then_inc(sem["proj_made"], 1)

                        def scores(n, qb):
                            p, r = n // 2, slice(DK * (n % 2), DK * (n % 2) + DK)
                            un = 4 * n + qb
                            if qb == 0:
                                pe.wait_ge(sem["rope_h_done"], 2 * p + 2)
                                pe.wait_ge(sem["rope_l_done"], 2 * p + 2)
                            if un >= 3:
                                pe.wait_ge(sem["exp_done"], un - 2)
                            q, N = slice(qb * P, (qb + 1) * P), P * (qb + 1)
                            o = bk[un % 3]
                            mm(o[:, 0:N], q_h[r, p % 2, q], k_h[r, p % 2, 0:N], start=True, stop=False)
                            mm(o[:, 0:N], q_h[r, p % 2, q], k_l[r, p % 2, 0:N], start=False, stop=False)
                            mm(o[:, 0:N], q_l[r, p % 2, q], k_h[r, p % 2, 0:N], start=False, stop=False)
                            mm(o[:, qb * P:N], ident_r[:, :], mask_r[:, :], start=False, stop=True).then_inc(sem["s_made"], 1)

                        def turn(n, g):
                            if g == 0:
                                pe.wait_ge(sem["norm_done"], 4 * (n + 1))
                                if n:
                                    pe.wait_ge(sem["pt_kept_a"], 2 * n)
                            elif g == 1:
                                if n:
                                    pe.wait_ge(sem["pt_kept_d"], n)
                            else:
                                pe.wait_ge(sem["pt_kept_a"], 2 * n + 1)
                            o = bk[3 + (3 * n + g) % 2]
                            at = 0
                            for kb in ((0,), (1, 3), (2,))[g]:
                                for qb in range(kb, NT):
                                    a = PROB_OFF[qb] + kb * P
                                    last = nc.tensor.transpose(o[:, at:at + P], prob[:, n % 2, a:a + P], ident)
                                    at += P
                            last.then_inc(sem["pt_made"], 1)

                        def weigh(p):
                            pe.wait_ge(sem["pt_kept_a"], 4 * (p + 1))
                            pe.wait_ge(sem["pt_kept_d"], 2 * (p + 1))
                            if p:
                                pe.wait_ge(sem["o_h_done"], p)
                                pe.wait_ge(sem["o_l_done"], p)
                            for kb in range(NT):
                                N = S - kb * P
                                for j in range(2):
                                    n = 2 * p + j
                                    last = mm(bk[5][DK * j:DK * j + DK, kb * P:S], v[:, kb, n * DK:n * DK + DK],
                                              probT[:, j, PART_OFF[kb]:PART_OFF[kb] + N], start=(kb == 0), stop=(kb == NT - 1),
                                              skip_group_check=True)
                            last.then_inc(sem["pv_made"], 1)

                        def project_out(p):
                            pe.wait_ge(sem["o_h_done"], p + 1)
                            pe.wait_ge(sem["o_l_done"], p + 1)
                            last = mm3(bk[6][:, :], wo_h[:, p, :], wo_l[:, p, :], o_h, o_l, start=(p == 0), stop=(p == NP - 1))
                            last.then_inc(sem["wo_made"], 1)

                        for kind in range(4):
                            project(0, kind)
                        for kind in range(2):
                            project(1, kind)
                        for qb in range(NT):
                            scores(0, qb)
                        for n in range(H):
                            pp = (n + 3) // 2 if n % 2 else (n + 2) // 2
                            kinds = (0, 1) if n % 2 else (2, 3)
                            more = pp < NP
                            if n + 1 < H:
                                scores(n + 1, 0)
                                scores(n + 1, 1)
                            if more:
                                project(pp, kinds[0])
                            if n + 1 < H:
                                scores(n + 1, 2)
                                scores(n + 1, 3)
                            if n % 2 == 0 and n:
                                weigh(n // 2 - 1)
                            turn(n, 0)
                            turn(n, 1)
                            if more:
                                project(pp, kinds[1])
                            if n % 2 == 1 and n > 1:
                                project_out((n - 3) // 2)
                            turn(n, 2)
                        weigh(NP - 1)
                        project_out(NP - 1)

                    def experts():
                        wait_xT(1)
                        for t in range(NT):
                            tt = slice(t * P, (t + 1) * P)
                            last = mm3(bk[7][:, t * E:(t + 1) * E], xT_h[:, tt], xT_l[:, tt], gate_h[:, :], gate_l[:, :])
                        last.then_inc(sem["lg_made"], 1)

                        def down(j):
                            pe.wait_ge(sem["hid_done"], j + 1)
                            mm(bk[6][:, :], wd[:, j, :], hid[:, j % 3, :], start=(j == 0), stop=(j == NJ - 1)).then_inc(sem["down_made"], 1)

                        for j in range(NJ):
                            c = slice(j * P, (j + 1) * P)
                            if j >= 2:
                                pe.wait_ge(sem["silu_done"], j - 1)
                                pe.wait_ge(sem["act1_done"], j - 1)
                            mm3(bk[j % 2][:, :], wg_h[:, c], wg_l[:, c], xT_h[:, :], xT_l[:, :]).then_inc(sem["gu_made"], 1)
                            mm3(bk[2 + j % 2][:, :], wu_h[:, c], wu_l[:, c], xT_h[:, :], xT_l[:, :]).then_inc(sem["gu_made"], 1)
                            if j == 1:
                                pe.wait_ge(sem["comb_ask"], 1)
                                for t in range(NT):
                                    last = nc.tensor.transpose(bk[7][:, t * P:(t + 1) * P], cs[:, t, :], ident)
                                last.then_inc(sem["comb_turned"], 1)
                                pe.wait_ge(sem["combT_done"], 1)
                            if j:
                                e0 = 2 * (j - 1)
                                g, el = divmod(e0, 16)
                                if j >= 3:
                                    pe.wait_ge(sem["hid_done"], j - 1)
                                rows = slice(32 * g, 32 * g + 32)
                                mm(bk[4 + j % 2][:, :], sel_r[rows, 64 * el:64 * el + P], combT[rows, :], start=True, stop=True,
                                   tile_position=(32 * g, 0)).then_inc(sem["c_made"], 1)
                            if j:
                                down(j - 1)
                        down(NJ - 1)

                    def mamba():
                        wait_xT(2)
                        for i in range(4):
                            c = slice(i * P, (i + 1) * P)
                            mm3(bk[i][:, :], win_h[:, c], win_l[:, c], xT_h[:, :], xT_l[:, :]).then_inc(sem["xz_made"], 1)
                        wx = sm("wx").rearrange("p (i n) -> p i n", n=33)
                        pe.wait_ge(sem["u_done"], NI)
                        for i in range(NI):
                            mm(bk[4][0:32, :], wx[:, i, 0:32], u[:, i, :], start=(i == 0), stop=(i == NI - 1))
                        for i in range(NI):
                            last = mm(bk[5][:, :], wx[:, i, 32:33].broadcast_to([P, P]), u[:, i, :], start=(i == 0), stop=(i == NI - 1))
                        last.then_inc(sem["xp_made"], 1)

                        def spread(s):
                            if s >= 2:
                                pe.wait_ge(sem["Bs_done"], s - 1)
                                pe.wait_ge(sem["hc_done"], 2 * (s - 1))
                            mm(bk[s % 2][:, :], i64_r[0:64, s:s + 1].broadcast_to([64, P]), bc_r[0:64, :], start=True, stop=True).then_inc(sem["B_made"], 1)
                            mm(bk[2 + s % 2][:, :], i64_r[0:64, DS + s:DS + s + 1].broadcast_to([64, P]), bc_r[0:64, :], start=True, stop=True).then_inc(sem["C_made"], 1)

                        pe.wait_ge(sem["bc_done"], 2)
                        pe.wait_ge(sem["xs_done"], NI)
                        spread(0)
                        for s in range(DS):
                            if s + 1 < DS:
                                spread(s + 1)
                            for i in range(NI):
                                m = NI * s + i
                                pe.wait_ge(sem["hc_done"], m + 1)
                                mm(bk[4 + i][:, :], ident, hc[:, m % 2, :], start=(s == 0), stop=(s == DS - 1)).then_inc(sem["y_made"], 1)
                        pe.wait_ge(sem["y2_done"], NI)
                        wout = sm("wout").rearrange("p (i n) -> p i n", n=D)
                        for i in range(NI):
                            last = mm(bk[6][:, :], wout[:, i, :], ca[:, i, :], start=(i == 0), stop=(i == NI - 1))
                        last.then_inc(sem["sub_done"], 1)

                    def experts2():
                        wait_xT(3)
                        for t in range(NT):
                            tt = slice(t * P, (t + 1) * P)
                            last = mm3(bk[7][:, t * E2:(t + 1) * E2], xT_h[:, tt], xT_l[:, tt], wr_h[:, :], wr_l[:, :])
                        last.then_inc(sem["l2_made"], 1)

                        def down(j):
                            pe.wait_ge(sem["h2_done"], j + 1)
                            k = P if j else 64
                            mm(bk[6][:, :], w2[0:k, j, :], h2[0:k, j % 2, :], start=(j == 0), stop=(j == NJ2 - 1)).then_inc(sem["down2_made"], 1)

                        for j in range(NJ2):
                            c = slice(j * P, (j + 1) * P)
                            if j >= 2:
                                pe.wait_ge(sem["relu_done"], j - 1)
                            mm3(bk[j % 2][:, :], w1_h[:, c], w1_l[:, c], xT_h[:, :], xT_l[:, :]).then_inc(sem["up2_made"], 1)
                            if j == 1:
                                pe.wait_ge(sem["p2_ask"], 1)
                                for t in range(NT):
                                    last = nc.tensor.transpose(bk[7][0:E2, t * P:(t + 1) * P], pr2[:, t, :], ident)
                                last.then_inc(sem["p2_turned"], 1)
                                pe.wait_ge(sem["pT2_done"], 1)
                            if j:
                                if j >= 3:
                                    pe.wait_ge(sem["h2_done"], j - 1)
                                mm(bk[2 + j % 2][:, :], sel8_r[0:E2, (j - 1) * P:j * P], pT2[0:E2, :], start=True, stop=True).then_inc(sem["p2_made"], 1)
                                down(j - 1)
                        down(NJ2 - 1)

                    turn_xn(0)
                    attention()
                    turn_y(0)
                    turn_xn(1)
                    experts()
                    turn_y(1)
                    turn_xn(2)
                    mamba()
                    turn_y(2)
                    turn_xn(3)
                    experts2()
                    turn_y(3)

                @block.scalar
                def _(act):
                    A = nc.scalar.activation

                    def keep_xT(k):
                        act.wait_ge(sem["xn_turned"], k + 1)
                        A(xT_h[:, :], bk[7][:, :], ACT.Copy).then_inc(sem["xT_h_done"], 1)

                    def keep_y(k):
                        name, n = (("wo_made", NP), ("down_made", NJ), ("sub_done", 1), ("down2_made", NJ2))[k]
                        act.wait_ge(sem[name], n)
                        if k == 0:
                            A(yT, bk[6][:, :], ACT.Identity, bias=sm("bo")).then_inc(sem["y_copied"], 1)
                        else:
                            A(yT, bk[6][:, :], ACT.Copy).then_inc(sem["y_copied"], 1)

                    def attention():
                        for n in range(0, 2 * NT, 2):
                            t = n // 2
                            act.wait_ge(sem["v_made"], n + 1)
                            A(v[:, t, 0:512], bk[3][:, :], ACT.Copy).then_inc(sem["v_kept_a"], 1)

                        def exps(n):
                            if n >= 2:
                                act.wait_ge(sem["pt_made"], 3 * (n - 1))
                            for qb in range(NT):
                                un = 4 * n + qb
                                N = P * (qb + 1)
                                if un >= 8 and qb == 0:
                                    act.wait_ge(sem["rinv_done"], n - 1)
                                act.wait_ge(sem["max_done"], un + 1)
                                A(prob[:, n % 2, PROB_OFF[qb]:PROB_OFF[qb] + N], bk[un % 3][:, 0:N], ACT.Exp,
                                  bias=nmax[:, un % 8:un % 8 + 1], accum_out=rsum[:, un % 8:un % 8 + 1]).then_inc(sem["exp_done"], 1)

                        def keep_turned(n, g):
                            if n >= 2 and g == 0:
                                act.wait_ge(sem["pv_made"], n // 2)
                            act.wait_ge(sem["pt_made"], 3 * n + g + 1)
                            A(probT[:, n % 2, 512 * g:512 * g + 512], bk[3 + (3 * n + g) % 2][:, :], ACT.Copy).then_inc(sem["pt_kept_a"], 1)

                        def keep_o(p):
                            if p:
                                act.wait_ge(sem["wo_made"], p)
                            act.wait_ge(sem["pv_made"], p + 1)
                            A(o_h, bk[5][:, :], ACT.Identity, bias=sm("bv")[:, p:p + 1]).then_inc(sem["o_h_done"], 1)

                        exps(0)
                        for n in range(H):
                            if n + 1 < H:
                                exps(n + 1)
                            if n % 2 == 0 and n:
                                keep_o(n // 2 - 1)
                            keep_turned(n, 0)
                            keep_turned(n, 1)
                        keep_o(NP - 1)

                    def experts():
                        act.wait_ge(sem["lg_made"], 1)
                        A(sc.rearrange("p a b -> p (a b)"), bk[7][:, 0:NT * E], ACT.Exp, scale=-1.0).then_inc(sem["lg_exp"], 1)
                        for j in range(NJ):
                            if j >= 2:
                                act.wait_ge(sem["act1_done"], j - 1)
                            act.wait_ge(sem["gu_made"], 2 * j + 1)
                            A(sg[:, j % 2, :], bk[j % 2][:, :], ACT.Silu).then_inc(sem["silu_done"], 1)

                    def mamba():
                        for i in range(NI):
                            act.wait_ge(sem["xz_made"], i + 1)
                            A(xin[:, i, DC - 1:], bk[i][:, :], ACT.Copy).then_inc(sem["xin_done"], 1)
                        for i in range(NI):
                            act.wait_ge(sem["xz_made"], NI + i + 1)
                            A(sz[:, i, :], bk[NI + i][:, :], ACT.Silu).then_inc(sem["sz_done"], 1)
                        for i in range(NI):
                            act.wait_ge(sem["conv_done"], i + 1)
                            A(u[:, i, :], cb[:, i, :], ACT.Silu, bias=sm("convb")[:, i:i + 1]).then_inc(sem["u_done"], 1)
                        act.wait_ge(sem["xs_done"], NI)
                        A(ca, xs, ACT.Abs).then_inc(sem["act_seq"], 1)
                        act.wait_ge(sem["act_seq"], 1)
                        A(cb, ca, ACT.Exp, scale=-1.0).then_inc(sem["sp_exp"], 1)
                        act.wait_ge(sem["sp_w1"], 1)
                        A(delta, ca, ACT.Ln).then_inc(sem["sp_ln"], 1)
                        act.wait_ge(sem["delta_done"], 1)
                        for s in range(DS):
                            act.wait_ge(sem["B_made"], s + 1)
                            if s >= 2:
                                act.wait_ge(sem["dBu_done"], NI * (s - 1))
                            A(Bs[:, s % 2, :], bk[s % 2][:, :], ACT.Copy).then_inc(sem["Bs_done"], 1)
                            for i in range(NI):
                                m = NI * s + i
                                if m >= 2:
                                    act.wait_ge(sem["scan_done"], m - 1)
                                A(dA[:, m % 2, :], delta[:, i, :], ACT.Exp, scale=negA[:, i * DS + s:i * DS + s + 1]).then_inc(sem["dA_done"], 1)

                    def experts2():
                        act.wait_ge(sem["l2_ask"], 1)
                        A(gate2, e2, ACT.Exp).then_inc(sem["l2_exp"], 1)
                        for j in range(NJ2):
                            act.wait_ge(sem["up2_made"], j + 1)
                            if j >= 2:
                                act.wait_ge(sem["h2_done"], j - 1)
                            A(r2[:, j % 2, :], bk[j % 2][:, :], ACT.Relu).then_inc(sem["relu_done"], 1)

                    keep_xT(0)
                    attention()
                    keep_y(0)
                    keep_xT(1)
                    experts()
                    keep_y(1)
                    keep_xT(2)
                    mamba()
                    keep_y(2)
                    keep_xT(3)
                    experts2()
                    keep_y(3)

                @block.vector
                def _(dve):
                    V = nc.vector
                    seq = [0]

                    def link(ins):
                        seq[0] += 1
                        ins.then_inc(sem["dve_seq"], 1)
                        dve.wait_ge(sem["dve_seq"], seq[0])

                    asked = [0]

                    def norm_scale(rows):
                        for t in range(NT):
                            ins = V.bn_stats(stats[:, t, :], rows(t))
                        link(ins)
                        for t in range(NT):
                            ins = V.bn_aggr(mv[:, t, :], stats[:, t, :])
                        link(ins)
                        V.tensor_scalar(ve[:, :], mv[:, :, 1], EPS, None, ALU.add).then_inc(sem["pow_ask"], 1)
                        asked[0] += 1
                        dve.wait_ge(sem["pow_done"], asked[0])

                    def norm_x(k):
                        norm_scale(lambda t: x[:, t, :])
                        for t in range(NT):
                            ins = V.tensor_scalar(xn[:, t, :], x[:, t, :], mv[:, t, 0:1], rstd[:, t:t + 1], ALU.subtract, ALU.mult)
                        ins.then_inc(sem["xn_ready"], 1)
                        dve.wait_ge(sem["xT_h_done"], k + 1)
                        V.tensor_tensor(xT_l[:, :], bk[7][:, :], xT_h[:, :].bitcast(F32), ALU.subtract).then_inc(sem["xT_l_done"], 1)

                    def add_y(k):
                        dve.wait_ge(sem["y_turned"], k + 1)
                        norm_scale(lambda t: bk[7][:, t * P:(t + 1) * P])
                        for t in range(NT):
                            ins = V.tensor_scalar(xn[:, t, :], bk[7][:, t * P:(t + 1) * P], mv[:, t, 0:1], rstd[:, t:t + 1],
                                                  ALU.subtract, ALU.mult)
                        link(ins)
                        ins = V.tensor_tensor(x[:, :, :], x[:, :, :], xn[:, :, :], ALU.add)
                        if k < 3:
                            link(ins)
                        else:
                            ins.then_inc(sem["x_out"], 1)

                    def attention():
                        for n in range(1, 2 * NT, 2):
                            dve.wait_ge(sem["v_made"], n + 1)
                            V.tensor_copy(v[:, n // 2, 512:1024], bk[4][:, :]).then_inc(sem["v_kept_d"], 1)

                        def rope_term(p, kind):
                            n = 4 * p + kind
                            m = n // 2
                            dve.wait_ge(sem["proj_made"], n + 1)
                            tab = sm(("cosq", "sinq", "cosk", "sink")[kind])
                            bias = sm("bqk")[:, 4 * p + kind:4 * p + kind + 1]
                            if kind % 2 == 0 and m >= 2:
                                dve.wait_ge(sem["rope_l_done"], m - 1)
                            if kind % 2 == 1 and m >= 1:
                                dve.wait_ge(sem["rope_sum"], m)
                            dst = ropeB if kind % 2 else ropeA[:, m % 2, :]
                            V.scalar_tensor_tensor(dst, bk[7][:, :], bias, tab, ALU.add, ALU.mult).then_inc(sem["rope_terms"], 1)

                        def rope_high(m):
                            p = m // 2
                            dve.wait_ge(sem["rope_sum"], m + 1)
                            if p >= 2:
                                dve.wait_ge(sem["s_made"], 8 * (p - 1))
                            V.tensor_copy((k_h if m % 2 else q_h)[:, p % 2, :], ropeA[:, m % 2, :]).then_inc(sem["rope_h_done"], 1)

                        def row_max(n, qb):
                            un = 4 * n + qb
                            dve.wait_ge(sem["s_made"], un + 1)
                            V.tensor_reduce(nmax[:, un % 8:un % 8 + 1], bk[un % 3][:, 0:P * (qb + 1)], AX.X, ALU.max, negate=True)\
                             .then_inc(sem["max_done"], 1)

                        def row_inv(n):
                            dve.wait_ge(sem["exp_done"], 4 * (n + 1))
                            if n >= 2:
                                dve.wait_ge(sem["norm_done"], 4 * (n - 1))
                            a = 4 * (n % 2)
                            V.reciprocal(rinv[:, a:a + 4], rsum[:, a:a + 4]).then_inc(sem["rinv_done"], 1)

                        def keep_turned(n):
                            if n >= 2:
                                dve.wait_ge(sem["pv_made"], n // 2)
                            dve.wait_ge(sem["pt_made"], 3 * n + 3)
                            V.tensor_copy(probT[:, n % 2, 1024:1280], bk[3 + (3 * n + 2) % 2][:, 0:256]).then_inc(sem["pt_kept_d"], 1)

                        def keep_o(p):
                            dve.wait_ge(sem["o_h_done"], p + 1)
                            V.scalar_tensor_tensor(o_l, bk[5][:, :], sm("bv")[:, p:p + 1], o_h.bitcast(F32), ALU.add, ALU.subtract)\
                             .then_inc(sem["o_l_done"], 1)

                        for m in range(2):
                            rope_term(0, 2 * m)
                            rope_term(0, 2 * m + 1)
                            rope_high(m)
                        rope_term(1, 0)
                        rope_term(1, 1)
                        for qb in range(NT):
                            row_max(0, qb)
                        rope_high(2)
                        row_inv(0)
                        for n in range(H):
                            pp = (n + 3) // 2 if n % 2 else (n + 2) // 2
                            kinds = (0, 1) if n % 2 else (2, 3)
                            more = pp < NP
                            if n + 1 < H:
                                row_max(n + 1, 0)
                                row_max(n + 1, 1)
                            if more:
                                rope_term(pp, kinds[0])
                            if n + 1 < H:
                                row_max(n + 1, 2)
                                row_max(n + 1, 3)
                            if n % 2 == 0 and n:
                                keep_o(n // 2 - 1)
                            if n + 1 < H:
                                row_inv(n + 1)
                            if more:
                                rope_term(pp, kinds[1])
                            keep_turned(n)
                            if more:
                                rope_high(2 * pp + kinds[0] // 2)
                        keep_o(NP - 1)

                    def experts():
                        s2 = sc.rearrange("p a b -> p (a b)")
                        V.memset(gm[:, :, G:], TOP)
                        V.memset(ms[:, :, E:], TOP)
                        dve.wait_ge(sem["lg_exp"], 1)
                        link(V.tensor_scalar(s2, s2, 1.0, None, ALU.add))
                        link(V.reciprocal(s2, s2))
                        link(V.tensor_tensor(s2, s2, sm("gbias"), ALU.add))
                        link(V.tensor_reduce(gm[:, :, 0:G], sc.rearrange("p a (g e) -> p a g e", e=E // G), AX.X, ALU.max))
                        for t in range(NT):
                            ins = V.max(g8[:, t, :], gm[:, t, :])
                        link(ins)
                        for t in range(NT):
                            ins = V.match_replace(gr[:, t, :], g8[:, t, :], gm[:, t, :], TAKEN)
                        link(ins)
                        link(V.tensor_scalar(gmask, gr[:, :, 0:G], TAKEN, None, ALU.is_equal))
                        ins = None
                        for t in range(NT):
                            ins = V.tensor_tensor(ms[:, t, 0:E].rearrange("p (g e) -> p g e", e=E // G),
                                                  sc[:, t, :].rearrange("p (g e) -> p g e", e=E // G),
                                                  gmask[:, t, :].rearrange("p (g o) -> p g o", o=1).broadcast_to([P, G, E // G]), ALU.mult)
                        link(ins)
                        for t in range(NT):
                            ins = V.max(s8[:, t, :], ms[:, t, :])
                        link(ins)
                        for t in range(NT):
                            ins = V.match_replace(sr[:, t, :], s8[:, t, :], ms[:, t, :], TAKEN)
                        link(ins)
                        link(V.scalar_tensor_tensor(comb, sr[:, :, 0:E], TAKEN, ms[:, :, 0:E], ALU.is_equal, ALU.mult))
                        link(V.tensor_reduce(csum, comb, AX.X, ALU.add))
                        link(V.tensor_scalar(csum, csum, 1e-8, None, ALU.add))
                        link(V.reciprocal(csum, csum))
                        link(V.tensor_tensor(comb, comb, csum.rearrange("p (a o) -> p a o", o=1).broadcast_to([P, NT, E]), ALU.mult))
                        for t in range(NT):
                            c4 = cs[:, t, :].rearrange("p (g h e) -> p g h e", h=2, e=16)
                            ins = V.tensor_copy(c4[:, :, 0, :].bitcast(F32R), comb[:, t, :].rearrange("p (g e) -> p g e", e=16))
                        link(ins)
                        for t in range(NT):
                            c4 = cs[:, t, :].rearrange("p (g h e) -> p g h e", h=2, e=16)
                            ins = V.tensor_tensor(c4[:, :, 1, :], comb[:, t, :].rearrange("p (g e) -> p g e", e=16), c4[:, :, 0, :], ALU.subtract)
                        ins.then_inc(sem["comb_ask"], 1)

                        def gated(j):
                            dve.wait_ge(sem["silu_done"], j + 1)
                            dve.wait_ge(sem["gu_made"], 2 * j + 2)
                            if j >= 3:
                                dve.wait_ge(sem["down_made"], j - 2)
                            ins = V.tensor_tensor(hid[:, j % 3, :], sg[:, j % 2, :], bk[2 + j % 2][:, :], ALU.mult)
                            ins.then_inc(sem["act1_done"], 1)

                        def weighted(j):
                            dve.wait_ge(sem["act1_done"], j + 1)
                            dve.wait_ge(sem["c_made"], j)
                            V.tensor_tensor(hid[:, j % 3, :], hid[:, j % 3, :], bk[4 + j % 2][:, :], ALU.mult).then_inc(sem["hid_done"], 1)

                        gated(0)
                        dve.wait_ge(sem["act1_done"], 1)
                        V.nop().then_inc(sem["hid_done"], 1)
                        dve.wait_ge(sem["comb_turned"], 1)
                        V.tensor_copy(combT, bk[7][:, :]).then_inc(sem["combT_done"], 1)
                        gated(1)
                        for j in range(2, NJ):
                            gated(j)
                            weighted(j - 1)
                        weighted(NJ - 1)

                    def mamba():
                        cw = sm("convw").rearrange("p (i c) -> p i c", c=DC)
                        link(V.memset(xin[:, :, 0:DC - 1], 0.0))
                        dve.wait_ge(sem["xin_done"], NI)
                        for i in range(NI):
                            ins = V.tensor_scalar(ca[:, i, :], xin[:, i, 0:S], cw[:, i, 0:1], None, ALU.mult)
                        link(ins)
                        for c in range(1, DC):
                            src, dst = (ca, cb) if c % 2 else (cb, ca)
                            for i in range(NI):
                                ins = V.scalar_tensor_tensor(dst[:, i, :], xin[:, i, c:c + S], cw[:, i, c:c + 1], src[:, i, :], ALU.mult, ALU.add)
                                if c == DC - 1:
                                    ins.then_inc(sem["conv_done"], 1)
                            if c < DC - 1:
                                link(ins)
                        dve.wait_ge(sem["xp_made"], 1)
                        V.tensor_copy(bc_r[0:32, :], bk[4][0:32, :]).then_inc(sem["bc_done"], 1)
                        for i in range(NI):
                            V.tensor_scalar(xs[:, i, :], bk[5][:, :], sm("wdt")[:, i:i + 1], sm("bdt")[:, i:i + 1], ALU.mult, ALU.add)\
                             .then_inc(sem["xs_done"], 1)
                        dve.wait_ge(sem["bc_done"], 1)
                        V.tensor_tensor(bc_r[32:64, :], bk[4][0:32, :], bc_r[0:32, :].bitcast(F32), ALU.subtract).then_inc(sem["bc_done"], 1)
                        dve.wait_ge(sem["sp_exp"], 1)
                        V.tensor_scalar(ca, cb, 1.0, None, ALU.add).then_inc(sem["sp_w1"], 1)
                        dve.wait_ge(sem["sp_w1"], 1)
                        link(V.scalar_tensor_tensor(cb, ca, 1.0, cb, ALU.subtract, ALU.subtract))
                        dve.wait_ge(sem["sp_ln"], 1)
                        link(V.tensor_tensor(delta, delta, cb, ALU.subtract))
                        link(V.scalar_tensor_tensor(delta, xs, 0.0, delta, ALU.max, ALU.add))
                        V.tensor_tensor(du, delta, u, ALU.mult).then_inc(sem["delta_done"], 1)

                        def scan(m):
                            dve.wait_ge(sem["dA_done"], m + 1)
                            dve.wait_ge(sem["dBu_done"], m + 1)
                            if m >= 3:
                                dve.wait_ge(sem["hc_done"], m - 2)
                            V.tensor_tensor_scan(hs[m % 3], dA[:, m % 2, :], dBu[:, m % 2, :], 0.0, ALU.mult, ALU.add)\
                             .then_inc(sem["scan_done"], 1)

                        def read_out(m):
                            dve.wait_ge(sem["scan_done"], m + 1)
                            dve.wait_ge(sem["C_made"], m // NI + 1)
                            if m >= 2:
                                dve.wait_ge(sem["y_made"], m - 1)
                            V.tensor_tensor(hc[:, m % 2, :], hs[m % 3], bk[2 + (m // NI) % 2][:, :], ALU.mult).then_inc(sem["hc_done"], 1)

                        scan(0)
                        for m in range(1, NI * DS):
                            scan(m)
                            read_out(m - 1)
                        read_out(NI * DS - 1)
                        for i in range(NI):
                            dve.wait_ge(sem["y_made"], NI * (DS - 1) + i + 1)
                            ins = V.scalar_tensor_tensor(cb[:, i, :], u[:, i, :], sm("dskip")[:, i:i + 1], bk[4 + i][:, :], ALU.mult, ALU.add)
                        link(ins)
                        dve.wait_ge(sem["sz_done"], NI)
                        for i in range(NI):
                            V.tensor_tensor(ca[:, i, :], cb[:, i, :], sz[:, i, :], ALU.mult).then_inc(sem["y2_done"], 1)

                    def experts2():
                        dve.wait_ge(sem["l2_made"], 1)
                        link(V.tensor_copy(lg.rearrange("p a b -> p (a b)"), bk[7][:, 0:NT * E2]))
                        for t in range(NT):
                            ins = V.max(v8[:, t, :], lg[:, t, :])
                        link(ins)
                        V.tensor_tensor(e2, v8[:, :, 1], v8[:, :, 0], ALU.subtract).then_inc(sem["l2_ask"], 1)
                        dve.wait_ge(sem["l2_exp"], 1)
                        link(V.tensor_scalar(gate2, gate2, 1.0, None, ALU.add))
                        link(V.reciprocal(gate2, gate2))
                        link(V.tensor_scalar(gate2, gate2, 1.0, None, ALU.is_ge))
                        link(V.tensor_tensor(pr2, lg, v8[:, :, 0:1].broadcast_to([P, NT, E2]), ALU.is_equal))
                        V.tensor_tensor(pr2, pr2, gate2.rearrange("p (a o) -> p a o", o=1).broadcast_to([P, NT, E2]), ALU.mult)\
                         .then_inc(sem["p2_ask"], 1)

                        def hidden(j):
                            dve.wait_ge(sem["relu_done"], j + 1)
                            if j >= 2:
                                dve.wait_ge(sem["down2_made"], j - 1)
                            r = r2[:, j % 2, :]
                            if j:
                                dve.wait_ge(sem["p2_made"], j)
                                link(V.tensor_tensor(rp2[:, j % 2, :], r, bk[2 + j % 2][:, :], ALU.mult))
                                V.tensor_tensor(h2[:, j % 2, :], rp2[:, j % 2, :], r, ALU.mult).then_inc(sem["h2_done"], 1)
                            else:
                                V.tensor_tensor(h2[:, 0, :], r, r, ALU.mult).then_inc(sem["h2_done"], 1)

                        hidden(0)
                        dve.wait_ge(sem["p2_turned"], 1)
                        V.tensor_copy(pT2[0:E2, :], bk[7][0:E2, :]).then_inc(sem["pT2_done"], 1)
                        for j in range(1, NJ2):
                            hidden(j)

                    dve.wait_ge(sem["x_in_"], 16)
                    norm_x(0)
                    attention()
                    add_y(0)
                    norm_x(1)
                    experts()
                    add_y(1)
                    norm_x(2)
                    mamba()
                    add_y(2)
                    norm_x(3)
                    experts2()
                    add_y(3)

                @block.gpsimd
                def _(pool):
                    Q = nc.gpsimd
                    asked = [0]

                    def power():
                        asked[0] += 1
                        pool.wait_ge(sem["pow_ask"], asked[0])
                        Q.tensor_tensor(rstd[:, :], ve[:, :], half_neg[:, :], ALU.pow).then_inc(sem["pow_done"], 1)

                    def attention():
                        def rope_sum(m):
                            pool.wait_ge(sem["rope_terms"], 2 * m + 2)
                            a = ropeA[:, m % 2, :]
                            Q.tensor_tensor(a, a, ropeB, ALU.add).then_inc(sem["rope_sum"], 1)

                        def rope_low(m):
                            p = m // 2
                            pool.wait_ge(sem["rope_h_done"], m + 1)
                            hi, lo = (k_h, k_l) if m % 2 else (q_h, q_l)
                            Q.tensor_tensor(lo[:, p % 2, :], ropeA[:, m % 2, :], hi[:, p % 2, :].bitcast(F32), ALU.subtract)\
                             .then_inc(sem["rope_l_done"], 1)

                        def normalise(n):
                            pool.wait_ge(sem["rinv_done"], n + 1)
                            for qb in range(NT):
                                a = prob[:, n % 2, PROB_OFF[qb]:PROB_OFF[qb] + P * (qb + 1)]
                                c = 4 * (n % 2) + qb
                                Q.tensor_scalar(a, a, rinv[:, c:c + 1], 0.0, ALU.mult, ALU.add).then_inc(sem["norm_done"], 1)

                        for m in range(2):
                            rope_sum(m)
                            rope_low(m)
                        rope_sum(2)
                        rope_low(2)
                        normalise(0)
                        for n in range(H):
                            pp = (n + 3) // 2 if n % 2 else (n + 2) // 2
                            m = 2 * pp + (0 if n % 2 else 1)
                            if n + 1 < H:
                                normalise(n + 1)
                            if pp < NP:
                                rope_sum(m)
                                rope_low(m)

                    def mamba():
                        pool.wait_ge(sem["delta_done"], 1)
                        for s in range(DS):
                            for i in range(NI):
                                m = NI * s + i
                                pool.wait_ge(sem["Bs_done"], s + 1)
                                if m >= 2:
                                    pool.wait_ge(sem["scan_done"], m - 1)
                                Q.tensor_tensor(dBu[:, m % 2, :], du[:, i, :], Bs[:, s % 2, :], ALU.mult).then_inc(sem["dBu_done"], 1)

                    power()
                    attention()
                    for _ in range(4):
                        power()
                    mamba()
                    for _ in range(3):
                        power()
            nc.all_engine_barrier(sems_to_clear=range(first.num, last.num + 1))


def kernel(**inputs):
    import numpy as np
    import concourse.bacc as bacc
    from concourse.bass_utils import run_bass_kernel_spmd as run

    a = {k: np.asarray(t) for k, t in inputs.items()}
    f32 = np.float32

    half = DK // 2
    theta = (f32(10000.0) ** (np.arange(0, DK, 2, dtype=f32) / f32(DK))).astype(f32)
    freqs = (np.arange(S, dtype=f32)[:, None] * (f32(1.0) / theta)[None, :]).astype(f32)
    emb = np.concatenate([freqs, freqs], axis=-1).T
    sign = np.where(np.arange(DK) % 2 == 0, f32(-1), f32(1))[:, None]
    cos, sin = np.tile(np.cos(emb), (2, 1)), np.tile(np.sin(emb) * sign, (2, 1))
    scale = f32(DK ** -0.5)
    r = np.arange(P)
    sel = (np.arange(1024)[None, :] // 64 == (r % 16)[:, None]).astype(f32)
    sel8 = (np.arange(512)[None, :] // 64 == r[:, None]).astype(f32)
    small = {
        "ident": np.eye(P, dtype=f32), "eye": np.eye(P, dtype=f32), "mask": np.where(r[None, :] > r[:, None], f32(MASKED), f32(0)),
        "cosq": cos * scale, "sinq": sin * scale, "cosk": cos, "sink": sin, "sel": sel, "sel8": sel8,
        "i64": ((r % 32)[:, None] == np.arange(32)[None, :]).astype(f32),
    }

    swap = np.arange(H * DK) ^ 1

    def by_pair(w):
        return w.T.reshape(D, NP, P)

    wq, wk, bq, bk_ = a["L0_attn_wq"], a["L0_attn_wk"], a["L0_attn_bq"], a["L0_attn_bk"]
    wqk = np.stack([by_pair(w) for w in (wq, wq[swap], wk, wk[swap])], axis=2).reshape(D, NP * 4 * P)
    small["bqk"] = np.stack([t.reshape(NP, P).T for t in (bq, bq[swap], bk_, bk_[swap])], axis=2)
    small["bv"] = a["L0_attn_bv"].reshape(NP, P).T
    small["bo"] = a["L0_attn_bo"].reshape(D, 1)
    small["gbias"] = np.broadcast_to(a["L0_ffn_gate_bias"], (P, NT, E))
    small["convw"] = a["L1_attn_conv_w"].reshape(NI, P, DC).transpose(1, 0, 2)
    small["convb"] = a["L1_attn_conv_b"].reshape(NI, P).T
    wx = a["L1_attn_W_xproj"]
    small["wx"] = np.concatenate([wx[1:], wx[:1]], axis=0).T.reshape(NI, P, 33).transpose(1, 0, 2)
    small["wdt"] = a["L1_attn_W_dt"].reshape(NI, P).T
    small["bdt"] = a["L1_attn_b_dt"].reshape(NI, P).T
    small["alog"] = a["L1_attn_A_log"].reshape(NI, P, DS).transpose(1, 0, 2)
    small["dskip"] = a["L1_attn_D"].reshape(NI, P).T
    small["wout"] = a["L1_attn_W_out"].T.reshape(NI, P, D).transpose(1, 0, 2)
    small["gate"] = a["L0_ffn_gate_w"].T
    small["wr"] = a["L1_ffn_Wr"]
    packed, packed_once = (np.concatenate([np.ascontiguousarray(small[n]).reshape(P, -1) for n in names], axis=1)
                           for names in (SMALL, ONCE))

    def up(shared, w):
        return np.concatenate([shared, w.transpose(2, 0, 1).reshape(D, -1)], axis=1)

    wd = np.concatenate([a["L0_ffn_sd_w"].T, a["L0_ffn_ed_w"].transpose(0, 2, 1).reshape(-1, D)], axis=0)
    w1 = np.concatenate([a["L1_ffn_Ws1"], np.zeros((D, 64), f32), a["L1_ffn_W1"].transpose(1, 0, 2).reshape(D, -1)], axis=1)
    w2 = np.concatenate([a["L1_ffn_Ws2"], np.zeros((64, D), f32), a["L1_ffn_W2"].reshape(-1, D)], axis=0)
    arrays = {
        "x": a["L0_attn_x"], "small": packed, "once": packed_once, "wqk": wqk, "wv": a["L0_attn_wv"].T,
        "wo": a["L0_attn_wo"].T.reshape(NP, P, D).transpose(1, 0, 2).reshape(P, NP * D),
        "wg": up(a["L0_ffn_sg_w"].T, a["L0_ffn_eg_w"]), "wu": up(a["L0_ffn_su_w"].T, a["L0_ffn_eu_w"]),
        "wd": wd.reshape(NJ, P, D).transpose(1, 0, 2).reshape(P, NJ * D),
        "win": a["L1_attn_W_in"].T, "w1": w1, "w2": w2.reshape(NJ2, P, D).transpose(1, 0, 2).reshape(P, NJ2 * D),
    }

    nc = bacc.Bacc("TRN2", target_bir_lowering=False, num_devices=1)
    feeds, args = {}, []
    for name, t in arrays.items():
        t = np.ascontiguousarray(t)
        feeds[f"in_{name}"] = t
        args.append(nc.dram_tensor(f"in_{name}", t.shape, mybir.dt.from_np(t.dtype), kind="ExternalInput").ap())
    args.append(nc.dram_tensor("out_x", (NB, S, D), F32, kind="ExternalOutput").ap())
    layers_kernel(nc, *args)
    r = run(nc, [feeds], core_ids=[0])
    return r.results[0]["out_x"]
```

```python
from contextlib import ExitStack

import concourse.bass as bass
from concourse import mybir

F32 = mybir.dt.float32
F32R = mybir.dt.float32r
ALU = mybir.AluOpType
ACT = mybir.ActivationFunctionType
AX = mybir.AxisListType

P = 128
NB = 8
S = 512
NT = S // P
D = 128
H = 16
DK = 64
NP = H // 2
E, G, TG, TK = 64, 8, 4, 6
WUCH = 8
NJ = 1 + E // 2
DI, DS, DC = 256, 16, 4
NI = DI // P
E2 = 8
NJ2 = 1 + E2 // 2
EPS = 1e-5
MASKED = -1e30
TOP = 3e38
TAKEN = -3e38

def columns(parts):
    at, where = 0, {}
    for name, n in parts:
        where[name] = (at, at + n)
        at += n
    return where, at


SMALL, NSMALL = columns([
    ("ident", P), ("cos", S), ("sin", S), ("bqk", NP * 4), ("bv", NP), ("bo", 1),
    ("gbias", E), ("convw", NI * DC), ("convb", NI), ("wx", NI * 33), ("wdt", NI), ("bdt", NI),
    ("alog", NI * DS), ("dskip", NI), ("wout", NI * D)])
ONCE, NONCE = columns([("eye", P), ("mask", P), ("sel", 1024), ("i64", 32), ("gate", E), ("wr", E2)])
PART_OFF = [0, 512, 1024, 896]
PROB_OFF = [0, 128, 384, 768]


def layers_kernel(nc, x_in, small_in, once_in, wqk_in, wv_in, wo_in, wg_in, wu_in, wd_in, win_in, w1_in, w2_in, out):
    ctx = ExitStack()
    with ctx:
        def sb(name, shape, dt=F32):
            return ctx.enter_context(nc.sbuf_tensor(name, shape, dt))

        small = sb("small", [P, NSMALL])

        def sm(name):
            a, b = SMALL[name]
            return small[:, a:b]

        wv_h, wv_l = sb("wv_h", [P, H * DK], F32R), sb("wv_l", [P, H * DK], F32R)
        wo_h, wo_l = sb("wo_h", [P, NP, D], F32R), sb("wo_l", [P, NP, D], F32R)
        wg_h = sb("wg_h", [P, NJ * P], F32R)
        wu_h = sb("wu_h", [P, NJ * P], F32R)
        win_h, win_l = sb("win_h", [P, 2 * DI], F32R), sb("win_l", [P, 2 * DI], F32R)
        w1_h, w1_l = sb("w1_h", [P, NJ2 * P], F32R), sb("w1_l", [P, NJ2 * P], F32R)
        w2 = sb("w2", [P, NJ2, D])
        gate_h, gate_l = sb("gate_h", [P, E], F32R), sb("gate_l", [P, E], F32R)
        wr_h, wr_l = sb("wr_h", [P, E2], F32R), sb("wr_l", [P, E2], F32R)
        ident_r, mask_r = sb("ident_r", [P, P], F32R), sb("mask_r", [P, P], F32R)
        i64_r = sb("i64_r", [P, 32], F32R)
        sel_r = sb("sel_r", [P, 1024], F32R)
        negA = sb("negA", [P, NI * DS])
        half_neg = sb("half_neg", [P, NT])
        ident = sm("ident")

        x0, xA, xB = (sb(n, [P, NT, D]) for n in ("x0", "xA", "xB"))

        class Lane:
            def __init__(lane, n, bank):
                lane.name, lane.bank = n, bank
                lane.xn = sb("xn_" + n, [P, NT, D])
                lane.yT = lane.xn[:, :, :].rearrange("p a b -> p (a b)")
                lane.xT_h, lane.xT_l = sb("xT_h_" + n, [P, S], F32R), sb("xT_l_" + n, [P, S], F32R)
                lane.stats, lane.mv = sb("stats_" + n, [P, NT, 6]), sb("mv_" + n, [P, NT, 2])
                lane.ve, lane.rstd = sb("ve_" + n, [P, NT]), sb("rstd_" + n, [P, NT])

        bk = [ctx.enter_context(nc.psum_tensor(f"bank{i}", [P, S], F32)) for i in range(8)]
        laneA, laneB = Lane("a", bk[4]), Lane("b", bk[5])

        WORK, WORKR, WORKB, WORKBR = 10776, 7168, 10246, S
        spaces = {("A", F32): sb("work", [P, WORK]), ("A", F32R): sb("workr", [P, WORKR], F32R),
                  ("B", F32): sb("work_b", [P, WORKB]), ("B", F32R): sb("workr_b", [P, WORKBR], F32R)}
        sizes = {("A", F32): WORK, ("A", F32R): WORKR, ("B", F32): WORKB, ("B", F32R): WORKBR}
        at = {k: 0 for k in spaces}

        def piece(*dims, dt=F32, lane="A"):
            n = 1
            for d in dims:
                n *= d
            k = (lane, dt)
            assert at[k] + n <= sizes[k], (k, at[k], n)
            a = spaces[k][:, at[k]:at[k] + n]
            at[k] += n
            if len(dims) == 2:
                a = a.rearrange("p (a b) -> p a b", b=dims[1])
            if len(dims) == 3:
                a = a.rearrange("p (a b c) -> p a b c", b=dims[1], c=dims[2])
            return a

        def again(lane, f32=0, f32r=0):
            at[(lane, F32)], at[(lane, F32R)] = f32, f32r

        v = piece(NT, H * DK)
        wqk = piece(2, 2, 4 * P, dt=F32R)
        ropeA, ropeB = piece(2, S), piece(S)
        q_h, q_l, k_h, k_l = (piece(2, S, dt=F32R) for _ in range(4))
        prob = piece(2, 1280)
        probT = piece(2, 1280)
        o_h, o_l = piece(S, dt=F32R), piece(S, dt=F32R)
        nmax, rsum, rinv = piece(8), piece(8), piece(8)
        again("A", 0, 2 * 2 * 4 * P)
        wd = piece(NJ, D)
        wg_l = piece(NJ * P, dt=F32R)
        wu_l = spaces[("A", F32R)][:, 0:2 * WUCH * P].rearrange("p (a b) -> p a b", b=WUCH * P)
        sg = piece(2, S)
        hid = piece(3, S)
        sc = piece(NT, E)
        gm, gr = piece(NT, G + 4), piece(NT, G + 4)
        g8 = piece(NT, 8)
        gmask = piece(NT, G)
        ms, sr = piece(NT, E + 2), piece(NT, E + 2)
        s8 = piece(NT, 8)
        csum = piece(NT)
        comb = piece(NT, E)
        cs = piece(NT, P)
        combT = piece(S, dt=F32R)
        xin = piece(NI, S + DC - 1, lane="B")
        ca, cb, u, sz, xs, delta, du, dBu, Cs = (piece(NI, S, lane="B") for _ in range(9))
        y1 = laneB.yT
        bc_r = piece(S, dt=F32R, lane="B")
        Bs = spaces[("B", F32)][:, 0:NI * S].rearrange("p (a b) -> p a b", b=S)
        dA, hc, hs = xs, ca, cb
        again("B")
        r2, rp2, h2 = (piece(2, S, lane="B") for _ in range(3))
        lg = piece(NT, E2, lane="B")
        v8 = piece(NT, 8, lane="B")
        e2, gate2 = piece(NT, lane="B"), piece(NT, lane="B")
        pr2 = piece(NT, E2, lane="B")
        pT2 = piece(S, dt=F32R, lane="B")
        again("A")
        raw, raw2 = piece(NJ * P), piece(NJ * P)
        once = piece(NONCE)
        raw_h, raw_l = piece(1024, dt=F32R), piece(1024, dt=F32R)

        def on(name):
            a, b = ONCE[name]
            return once[:, a:b]


        wqk_split = nc.dram_tensor("wqk_split", (NP, P, 2, 4 * P), F32, kind="Internal").ap()
        wg_low, wu_low = (nc.dram_tensor(n, (P, NJ * P), F32, kind="Internal").ap() for n in ("wg_low", "wu_low"))
        flat = "p a b -> p (a b)"
        SCALE = DK ** -0.5

        names0 = ["w_in", "store_low", "small_in_", "split_h", "split_l", "store_qk"]
        s0 = {n: ctx.enter_context(nc.semaphore(n)) for n in names0}
        NQK = NP * 4 * P // 1024
        with nc.Block() as block:
            loads = [(raw[:, 0:1024], wv_in, wv_h[:, :], wv_l[:, :]),
                     (raw[:, 1024:2048], wo_in, wo_h[:, :, :].rearrange("p a b -> p (a b)"), wo_l[:, :, :].rearrange("p a b -> p (a b)")),
                     (raw[:, 2048:2560], win_in, win_h[:, :], win_l[:, :]),
                     (raw[:, 2560:3200], w1_in, w1_h[:, :], w1_l[:, :]),
                     (raw2[:, :], wg_in, wg_h[:, :], wg_l),
                     (raw[:, :], wu_in, wu_h[:, :], wg_l)]
            qk_loads = [(raw[:, 1024 * (c % 2):1024 * (c % 2) + 1024], wqk_in[:, 1024 * c:1024 * c + 1024]) for c in range(NQK)]
            NL = len(loads)

            @block.sync
            def _(sp):
                sp.dma_start(small[:, :], small_in).then_inc(s0["small_in_"], 16)
                sp.dma_start(once, once_in).then_inc(s0["small_in_"], 16)
                sp.wait_ge(s0["small_in_"], 32)
                for dst, src, _, _ in loads:
                    if src is wu_in:
                        sp.wait_ge(s0["split_l"], 4)
                    sp.dma_start(dst, src).then_inc(s0["w_in"], 16)
                sp.wait_ge(s0["split_l"], NL - 1)
                sp.dma_start(wg_low, wg_l.bitcast(F32)).then_inc(s0["store_low"], 16)
                sp.wait_ge(s0["w_in"], 16 * NL)
                sp.wait_ge(s0["split_l"], NL)
                sp.dma_start(wu_low, wg_l.bitcast(F32)).then_inc(s0["store_low"], 16)
                sp.dma_start(w2[:, :, :].rearrange("p a b -> p (a b)"), w2_in).then_inc(s0["small_in_"], 16)
                for c, (dst, src) in enumerate(qk_loads):
                    sp.wait_ge(s0["split_l"], NL + c - 1 if c else NL)
                    sp.dma_start(dst, src).then_inc(s0["w_in"], 16)
                    sp.wait_ge(s0["w_in"], 16 * (NL + c + 1))
                    sp.wait_ge(s0["split_l"], NL + c + 1)
                    for h in range(2):
                        for part, t in ((0, raw_h), (1, raw_l)):
                            sp.dma_start(wqk_split[2 * c + h, :, part, :], t[:, 512 * h:512 * h + 512].bitcast(F32)).then_inc(s0["store_qk"], 16)
                    sp.wait_ge(s0["store_qk"], 64 * (c + 1))
                sp.wait_ge(s0["small_in_"], 48)
                sp.wait_ge(s0["store_low"], 32)

            @block.scalar
            def _(act):
                for n, (t, _, hi, _) in enumerate(loads):
                    act.wait_ge(s0["w_in"], 16 * (NL if n == NL - 1 else NL - 1))
                    nc.scalar.activation(hi, t, ACT.Copy).then_inc(s0["split_h"], 1)
                for c, (t, _) in enumerate(qk_loads):
                    act.wait_ge(s0["w_in"], 16 * (NL + c + 1))
                    if c:
                        act.wait_ge(s0["store_qk"], 64 * c)
                    th, tr = (w.rearrange("p (a k n) -> p a k n", k=2, n=2 * P) for w in (raw_h, t))
                    nc.scalar.activation(th[:, :, 0, :], tr[:, :, 0, :], ACT.Copy, scale=SCALE)
                    nc.scalar.activation(th[:, :, 1, :], tr[:, :, 1, :], ACT.Copy).then_inc(s0["split_h"], 1)
                act.wait_ge(s0["small_in_"], 32)
                nc.scalar.activation(negA[:, :], sm("alog"), ACT.Exp).then_inc(s0["split_h"], 1)
                act.wait_ge(s0["split_h"], NL + NQK + 1)
                nc.scalar.mul(negA[:, :], negA[:, :], -1.0)

            @block.vector
            def _(dve):
                for n, (t, _, hi, lo) in enumerate(loads):
                    dve.wait_ge(s0["split_h"], n + 1)
                    if n == NL - 1:
                        dve.wait_ge(s0["store_low"], 16)
                    nc.vector.tensor_tensor(lo, t, hi.bitcast(F32), ALU.subtract).then_inc(s0["split_l"], 1)
                for c, (t, _) in enumerate(qk_loads):
                    dve.wait_ge(s0["split_h"], NL + c + 1)
                    if c:
                        dve.wait_ge(s0["store_qk"], 64 * c)
                    tl, tr, th = (w.rearrange("p (a k n) -> p a k n", k=2, n=2 * P) for w in (raw_l, t, raw_h))
                    for k, factor in ((0, SCALE), (1, 1.0)):
                        ins = nc.vector.scalar_tensor_tensor(tl[:, :, k, :], tr[:, :, k, :], factor, th[:, :, k, :].bitcast(F32),
                                                             ALU.mult, ALU.subtract)
                    ins.then_inc(s0["split_l"], 1)
                dve.wait_ge(s0["small_in_"], 32)
                nc.vector.tensor_copy(gate_h[:, :], on("gate")).then_inc(s0["split_l"], 1)
                nc.vector.tensor_copy(wr_h[:, :], on("wr")).then_inc(s0["split_l"], 1)
                dve.wait_ge(s0["split_l"], NL + NQK + 2)
                nc.vector.tensor_tensor(gate_l[:, :], on("gate"), gate_h[:, :].bitcast(F32), ALU.subtract)
                nc.vector.tensor_tensor(wr_l[:, :], on("wr"), wr_h[:, :].bitcast(F32), ALU.subtract)
                for t, name in ((ident_r, "eye"), (mask_r, "mask"), (i64_r, "i64"), (sel_r, "sel")):
                    nc.vector.tensor_copy(t[:, :], on(name))
                bq = sm("bqk").rearrange("p (a k) -> p a k", k=4)[:, :, 0:2]
                nc.vector.tensor_scalar(bq, bq, SCALE, None, ALU.mult)

            @block.gpsimd
            def _(pool):
                nc.gpsimd.memset(half_neg[:, :], -0.5)

        names = """x_in_ wv_in x_out out_done pow_ask pow_done xn_ready_a xn_turned_a xT_h_done_a xT_l_done_a y_copied_a y_turned_a
            xn_ready_b xn_turned_b xT_h_done_b xT_l_done_b y_copied_b y_turned_b
            dve_seq act_seq wqk0 wqk1 wg_low_in wu_low_in wd_in_ v_made v_kept_a v_kept_d proj_made rope_terms rope_sum rope_h_done rope_l_done
            s_made max_done exp_done rinv_done norm_done pt_made pt_kept_a pt_kept_d pv_made o_h_done o_l_done wo_made
            lg_made lg_exp comb_turned comb_ask combT_done g_made u_made silu_done act1_done c_made hid_done down_made
            xz_made xin_done sz_done conv_done u_done xp_made bc_done xs_done sp_exp sp_w1 sp_ln delta_done
            spread_made spread_kept dA_done dBu_done scan_done hc_done y_made y1_done y2_done out_made
            l2_made l2_exp l2_ask p2_ask p2_turned pT2_done up2_made relu_done p2_made h2_done down2_made""".split()
        sem = {n: ctx.enter_context(nc.semaphore(n)) for n in names}
        first, last_sem = sem[names[0]], sem[names[-1]]
        NU = NI * DS
        SLOTS = 3 * H
        SPREAD, DECAY, SCAN, READ, SUM = 11, 12, 13, 14, 15
        WCH = 11

        def turn(A, B, x_src, out_dst):
            with nc.Block() as block:
                @block.sync
                def _(sp):
                    if A:
                        sp.dma_start(x0[:, :, :], x_src.rearrange("o (t p) d -> (o p) t d", p=P)).then_inc(sem["x_in_"], 16)
                        for p in range(NP):
                            if p >= 2:
                                sp.wait_ge(sem["proj_made"], 4 * (p - 1))
                            sp.dma_start(wqk[:, p % 2, :, :].bitcast(F32), wqk_split[p]).then_inc(sem[f"wqk{p % 2}"], 16)

                        def load_wu(c):
                            w = slice(c * WUCH * P, min((c + 1) * WUCH, NJ) * P)
                            if c >= 2:
                                sp.wait_ge(sem["u_made"], WUCH * (c - 1))
                            sp.dma_start(wu_l[:, c % 2, 0:w.stop - w.start].bitcast(F32), wu_low[:, w]).then_inc(sem["wu_low_in"], 16)

                        sp.wait_ge(sem["proj_made"], 4 * NP)
                        load_wu(0)
                        sp.wait_ge(sem["pv_made"], NP)
                        sp.wait_ge(sem["wo_made"], NP)
                        for c in range(NJ // WCH):
                            w = slice(c * WCH * P, (c + 1) * WCH * P)
                            sp.dma_start(wg_l[:, w].bitcast(F32), wg_low[:, w]).then_inc(sem["wg_low_in"], 16)
                            sp.wait_ge(sem["wg_low_in"], 16 * (c + 1))
                            sp.dma_start(wd[:, c * WCH:(c + 1) * WCH, :].rearrange(flat), wd_in[:, w]).then_inc(sem["wd_in_"], 16)
                            sp.wait_ge(sem["wd_in_"], 16 * (c + 1))
                            if c == 0:
                                sp.wait_ge(sem["wu_low_in"], 16)
                                load_wu(1)
                        for c in range(2, -(-NJ // WUCH)):
                            sp.wait_ge(sem["wu_low_in"], 16 * c)
                            load_wu(c)
                    if B:
                        sp.wait_ge(sem["x_out"], 1)
                        sp.dma_start(out_dst.rearrange("o (t p) d -> (o p) t d", p=P), xB[:, :, :]).then_inc(sem["out_done"], 16)
                        sp.wait_ge(sem["out_done"], 16)

                @block.tensor
                def _(pe):
                    mm = nc.tensor.matmul

                    def mm3(o, wh, wl, mh, ml, start=True, stop=True):
                        mm(o, wh, mh, start=start, stop=False)
                        mm(o, wh, ml, start=False, stop=False)
                        return mm(o, wl, mh, start=False, stop=stop)

                    def turn_xn(L, k):
                        pe.wait_ge(sem["xn_ready_" + L.name], k + 1)
                        for t in range(NT):
                            last = nc.tensor.transpose(L.bank[:, t * P:(t + 1) * P], L.xn[:, t, :], ident)
                        last.then_inc(sem["xn_turned_" + L.name], 1)

                    def turn_y(L, k):
                        if k:
                            pe.wait_ge(sem["y_copied_" + L.name], k)
                        for t in range(NT):
                            last = nc.tensor.transpose(L.bank[:, t * P:(t + 1) * P], L.yT[:, t * P:(t + 1) * P], ident)
                        last.then_inc(sem["y_turned_" + L.name], 1)

                    def wait_xT(L, k):
                        pe.wait_ge(sem["xT_h_done_" + L.name], k + 1)
                        pe.wait_ge(sem["xT_l_done_" + L.name], k + 1)

                    def xz(i):
                        if i == 0:
                            wait_xT(laneB, 0)
                        if i >= NI:
                            pe.wait_ge(sem["xin_done"], i - NI + 1)
                        c = slice(i * P, (i + 1) * P)
                        mm3(bk[(7, 5)[i % NI]][:, :], win_h[:, c], win_l[:, c], laneB.xT_h[:, :], laneB.xT_l[:, :])\
                            .then_inc(sem["xz_made"], 1)

                    def xproj():
                        wx = sm("wx").rearrange("p (i n) -> p i n", n=33)
                        pe.wait_ge(sem["sz_done"], NI)
                        pe.wait_ge(sem["u_done"], NI)
                        for i in range(NI):
                            mm(bk[7][0:32, :], wx[:, i, 0:32], u[:, i, :], start=(i == 0), stop=(i == NI - 1))
                        for i in range(NI):
                            last = mm(bk[5][:, :], wx[:, i, 32:33].broadcast_to([P, P]), u[:, i, :], start=(i == 0), stop=(i == NI - 1))
                        last.then_inc(sem["xp_made"], 1)

                    def spread(m):
                        if m == 0:
                            pe.wait_ge(sem["bc_done"], 2)
                            pe.wait_ge(sem["xs_done"], NI)
                        else:
                            pe.wait_ge(sem["spread_kept"], m)
                        row = m // 2 + (DS if m % 2 else 0)
                        mm(bk[5][:, :], i64_r[0:64, row:row + 1].broadcast_to([64, P]), bc_r[0:64, :], start=True, stop=True)\
                            .then_inc(sem["spread_made"], 1)

                    def sum_states(s):
                        pe.wait_ge(sem["hc_done"], NI * s + 1)
                        mm(bk[7][:, :], ident, hc[:, 0, :], start=(s == 0), stop=(s == DS - 1)).then_inc(sem["y_made"], 1)

                    def slot(k):
                        if not B:
                            return
                        if k == 5:
                            xproj()
                        if 0 <= k - SUM < NU and (k - SUM) % NI == 0:
                            sum_states((k - SUM) // NI)
                        if 0 <= k - SPREAD < NU:
                            spread(k - SPREAD)

                    def out_proj():
                        pe.wait_ge(sem["y2_done"], NI)
                        wout = sm("wout").rearrange("p (i n) -> p i n", n=D)
                        for i in range(NI):
                            last = mm(bk[3][:, :], wout[:, i, :], ca[:, i, :], start=(i == 0), stop=(i == NI - 1))
                        last.then_inc(sem["out_made"], 1)

                    def logits2():
                        wait_xT(laneB, 1)
                        for t in range(NT):
                            tt = slice(t * P, (t + 1) * P)
                            last = mm3(bk[5][:, t * E2:(t + 1) * E2], laneB.xT_h[:, tt], laneB.xT_l[:, tt], wr_h[:, :], wr_l[:, :])
                        last.then_inc(sem["l2_made"], 1)

                    def turn_p2():
                        pe.wait_ge(sem["p2_ask"], 1)
                        for t in range(NT):
                            last = nc.tensor.transpose(bk[5][0:E2, t * P:(t + 1) * P], pr2[:, t, :], ident)
                        last.then_inc(sem["p2_turned"], 1)

                    def up2(j):
                        c = slice(j * P, (j + 1) * P)
                        if j == 0:
                            wait_xT(laneB, 1)
                        else:
                            pe.wait_ge(sem["relu_done"], j)
                        mm3(bk[3][:, :], w1_h[:, c], w1_l[:, c], laneB.xT_h[:, :], laneB.xT_l[:, :]).then_inc(sem["up2_made"], 1)
                        if j:
                            pe.wait_ge(sem["pT2_done"], 1)
                            if j >= 2:
                                pe.wait_ge(sem["h2_done"], j)
                            mm(bk[5][:, :], sel_r[0:E2, (j - 1) * P:j * P], pT2[0:E2, :], start=True, stop=True)\
                                .then_inc(sem["p2_made"], 1)

                    def down2(j):
                        pe.wait_ge(sem["h2_done"], j + 1)
                        k = P if j else 64
                        mm(bk[7][:, :], w2[0:k, j, :], h2[0:k, j % 2, :], start=(j == 0), stop=(j == NJ2 - 1))\
                            .then_inc(sem["down2_made"], 1)

                    def step_b(t):
                        if not B:
                            return
                        if t == 1:
                            turn_xn(laneB, 1)
                        if t == 3:
                            logits2()
                        if t == 4:
                            up2(0)
                        if t == 6:
                            down2(0)
                        if t == 7:
                            turn_p2()
                        for j in range(1, NJ2):
                            if t == 6 + 3 * j:
                                up2(j)
                            if t == 8 + 3 * j:
                                down2(j)
                        if t == 22:
                            turn_y(laneB, 2)

                    def values(n):
                        t, hf = divmod(n, 2)
                        if n >= 4:
                            pe.wait_ge(sem["v_kept_d" if n % 2 else "v_kept_a"], (n - 4) // 2 + 1)
                        tt, cc = slice(t * P, (t + 1) * P), slice(hf * 512, hf * 512 + 512)
                        mm3(bk[n % 4][:, :], laneA.xT_h[:, tt], laneA.xT_l[:, tt], wv_h[:, cc], wv_l[:, cc]).then_inc(sem["v_made"], 1)

                    def project(p, kind):
                        n = 4 * p + kind
                        if kind == 0:
                            pe.wait_ge(sem[f"wqk{p % 2}"], 16 * (p // 2 + 1))
                        if n:
                            pe.wait_ge(sem["rope_terms"], n)
                        c = slice(kind * P, kind * P + P)
                        mm3(bk[4][:, :], wqk[:, p % 2, 0, c], wqk[:, p % 2, 1, c], laneA.xT_h[:, :], laneA.xT_l[:, :])\
                            .then_inc(sem["proj_made"], 1)

                    def scores(n, qb):
                        p, r = n // 2, slice(DK * (n % 2), DK * (n % 2) + DK)
                        un = 4 * n + qb
                        if qb == 0:
                            pe.wait_ge(sem["rope_h_done"], 2 * p + 2)
                            pe.wait_ge(sem["rope_l_done"], 2 * p + 2)
                        if un >= 2:
                            pe.wait_ge(sem["exp_done"], un - 1)
                        q, N = slice(qb * P, (qb + 1) * P), P * (qb + 1)
                        o = bk[un % 2]
                        mm(o[:, 0:N], q_h[r, p % 2, q], k_h[r, p % 2, 0:N], start=True, stop=False)
                        mm(o[:, 0:N], q_h[r, p % 2, q], k_l[r, p % 2, 0:N], start=False, stop=False)
                        mm(o[:, 0:N], q_l[r, p % 2, q], k_h[r, p % 2, 0:N], start=False, stop=False)
                        mm(o[:, qb * P:N], ident_r[:, :], mask_r[:, :], start=False, stop=True).then_inc(sem["s_made"], 1)

                    def turn_probs(n, g):
                        if g == 0:
                            pe.wait_ge(sem["norm_done"], 4 * (n + 1))
                            if n:
                                pe.wait_ge(sem["pt_kept_a"], 2 * n)
                        elif g == 1:
                            if n:
                                pe.wait_ge(sem["pt_kept_d"], n)
                        else:
                            pe.wait_ge(sem["pt_kept_a"], 2 * n + 1)
                        o = bk[2 + (3 * n + g) % 2]
                        at = 0
                        for kb in ((0,), (1, 3), (2,))[g]:
                            for qb in range(kb, NT):
                                a = PROB_OFF[qb] + kb * P
                                last = nc.tensor.transpose(o[:, at:at + P], prob[:, n % 2, a:a + P], ident)
                                at += P
                        last.then_inc(sem["pt_made"], 1)

                    def weigh(p, terms):
                        pe.wait_ge(sem["pt_kept_a"], 4 * (p + 1))
                        pe.wait_ge(sem["pt_kept_d"], 2 * (p + 1))
                        pe.wait_ge(sem["rope_terms"], terms)
                        if p:
                            pe.wait_ge(sem["o_h_done"], p)
                            pe.wait_ge(sem["o_l_done"], p)
                        for kb in range(NT):
                            N = S - kb * P
                            for j in range(2):
                                n = 2 * p + j
                                last = mm(bk[4][DK * j:DK * j + DK, kb * P:S], v[:, kb, n * DK:n * DK + DK],
                                          probT[:, j, PART_OFF[kb]:PART_OFF[kb] + N], start=(kb == 0), stop=(kb == NT - 1),
                                          skip_group_check=True)
                        last.then_inc(sem["pv_made"], 1)

                    def project_out(p):
                        pe.wait_ge(sem["o_h_done"], p + 1)
                        pe.wait_ge(sem["o_l_done"], p + 1)
                        last = mm3(bk[6][:, :], wo_h[:, p, :], wo_l[:, p, :], o_h, o_l, start=(p == 0), stop=(p == NP - 1))
                        last.then_inc(sem["wo_made"], 1)

                    def begin_a():
                        pe.wait_ge(sem["v_kept_a"], NT)
                        pe.wait_ge(sem["v_kept_d"], NT)
                        for n in range(8):
                            project(n // 4, n % 4)
                        for qb in range(NT):
                            scores(0, qb)

                    def head(n):
                        pp, kinds = (n // 2 + 2, (0, 1)) if n % 2 == 0 else (n // 2 + 2, (2, 3))
                        more = pp < NP
                        if n + 1 < H:
                            scores(n + 1, 0)
                            scores(n + 1, 1)
                        if more:
                            if n % 2 == 1 and n > 1:
                                pe.wait_ge(sem["o_h_done"], n // 2)
                                pe.wait_ge(sem["o_l_done"], n // 2)
                            project(pp, kinds[0])
                        slot(3 * n)
                        if n + 1 < H:
                            scores(n + 1, 2)
                            scores(n + 1, 3)
                        if n % 2 == 0 and n:
                            weigh(n // 2 - 1, 4 * pp + 1 if more else 4 * NP)
                        slot(3 * n + 1)
                        turn_probs(n, 0)
                        turn_probs(n, 1)
                        slot(3 * n + 2)
                        if more:
                            if n % 2 == 0 and n:
                                pe.wait_ge(sem["o_h_done"], n // 2)
                                pe.wait_ge(sem["o_l_done"], n // 2)
                            project(pp, kinds[1])
                        if n % 2 == 1 and n > 1:
                            project_out((n - 3) // 2)
                        turn_probs(n, 2)

                    def expert_logits():
                        wait_xT(laneA, 1)
                        for t in range(NT):
                            tt = slice(t * P, (t + 1) * P)
                            last = mm3(bk[4][:, t * E:(t + 1) * E], laneA.xT_h[:, tt], laneA.xT_l[:, tt], gate_h[:, :], gate_l[:, :])
                        last.then_inc(sem["lg_made"], 1)

                    def down(j):
                        pe.wait_ge(sem["hid_done"], j + 1)
                        if j % WCH == 0:
                            pe.wait_ge(sem["wd_in_"], 16 * (j // WCH + 1))
                        mm(bk[6][:, :], wd[:, j, :], hid[:, j % 3, :], start=(j == 0), stop=(j == NJ - 1)).then_inc(sem["down_made"], 1)

                    def experts(j):
                        c = slice(j * P, (j + 1) * P)
                        if j >= 2:
                            pe.wait_ge(sem["silu_done"], j - 1)
                        if j % WCH == 0:
                            pe.wait_ge(sem["wg_low_in"], 16 * (j // WCH + 1))
                        mm3(bk[j % 2][:, :], wg_h[:, c], wg_l[:, c], laneA.xT_h[:, :], laneA.xT_l[:, :]).then_inc(sem["g_made"], 1)
                        if j:
                            pe.wait_ge(sem["act1_done"], j)
                        if j % WUCH == 0:
                            pe.wait_ge(sem["wu_low_in"], 16 * (j // WUCH + 1))
                        lo = slice(j % WUCH * P, (j % WUCH + 1) * P)
                        mm3(bk[2][:, :], wu_h[:, c], wu_l[:, j // WUCH % 2, lo], laneA.xT_h[:, :], laneA.xT_l[:, :]).then_inc(sem["u_made"], 1)
                        if j == 1:
                            pe.wait_ge(sem["comb_ask"], 1)
                            for t in range(NT):
                                last = nc.tensor.transpose(bk[4][:, t * P:(t + 1) * P], cs[:, t, :], ident)
                            last.then_inc(sem["comb_turned"], 1)
                            pe.wait_ge(sem["combT_done"], 1)
                        if j >= 2:
                            down(j - 2)
                        if j:
                            g, el = divmod(2 * (j - 1), 16)
                            if j >= 2:
                                pe.wait_ge(sem["hid_done"], j)
                            rows = slice(32 * g, 32 * g + 32)
                            mm(bk[4][:, :], sel_r[rows, 64 * el:64 * el + P], combT[rows, :], start=True, stop=True,
                               tile_position=(32 * g, 0)).then_inc(sem["c_made"], 1)

                    if B:
                        turn_y(laneB, 0)
                    if A:
                        turn_xn(laneA, 0)
                        wait_xT(laneA, 0)
                        for n in range(4):
                            values(n)
                    if B:
                        turn_xn(laneB, 0)
                    if A:
                        for n in range(4, 2 * NT):
                            values(n)
                    if B:
                        xz(0)
                        xz(1)
                    if A:
                        begin_a()
                    if B:
                        xz(2)
                        xz(3)
                    for n in range(H):
                        if A:
                            head(n)
                        else:
                            for k in range(3 * n, 3 * n + 3):
                                slot(k)
                    if A:
                        weigh(NP - 1, 4 * NP)
                        project_out(NP - 1)
                    if B:
                        out_proj()
                    if A:
                        turn_y(laneA, 1)
                    if B:
                        turn_y(laneB, 1)
                    if A:
                        turn_xn(laneA, 1)
                        expert_logits()
                    for j in range(NJ):
                        if A:
                            experts(j)
                        step_b(j)
                    if A:
                        down(NJ - 2)
                        down(NJ - 1)

                @block.scalar
                def _(act):
                    ac = nc.scalar.activation

                    def keep_xT(L, k):
                        act.wait_ge(sem["xn_turned_" + L.name], k + 1)
                        ac(L.xT_h[:, :], L.bank[:, :], ACT.Copy).then_inc(sem["xT_h_done_" + L.name], 1)

                    def keep_xin():
                        for i in range(NI):
                            act.wait_ge(sem["xz_made"], i + 1)
                            ac(xin[:, i, DC - 1:], bk[(7, 5)[i]][:, :], ACT.Copy).then_inc(sem["xin_done"], 1)

                    def slot(k):
                        if not B:
                            return
                        if k == 4:
                            for i in range(NI):
                                act.wait_ge(sem["xz_made"], NI + i + 1)
                                ac(sz[:, i, :], bk[(7, 5)[i]][:, :], ACT.Silu).then_inc(sem["sz_done"], 1)
                            for i in range(NI):
                                act.wait_ge(sem["conv_done"], i + 1)
                                ac(u[:, i, :], cb[:, i, :], ACT.Silu, bias=sm("convb")[:, i:i + 1]).then_inc(sem["u_done"], 1)
                        if k == 7:
                            act.wait_ge(sem["xs_done"], NI)
                            ac(ca, xs, ACT.Abs).then_inc(sem["act_seq"], 1)
                            act.wait_ge(sem["act_seq"], 1)
                            ac(cb, ca, ACT.Exp, scale=-1.0).then_inc(sem["sp_exp"], 1)
                        if k == 9:
                            act.wait_ge(sem["sp_w1"], 1)
                            ac(delta, ca, ACT.Ln).then_inc(sem["sp_ln"], 1)
                        m = k - SPREAD
                        if 0 <= m < NU:
                            s = m // 2
                            act.wait_ge(sem["spread_made"], m + 1)
                            if m % 2 == 0:
                                if s >= 2:
                                    act.wait_ge(sem["dBu_done"], NI * (s - 1))
                                if s == 0:
                                    act.wait_ge(sem["conv_done"], NI)
                                dst = Bs
                            else:
                                if s >= 2:
                                    act.wait_ge(sem["hc_done"], NI * (s - 1))
                                dst = Cs
                            ac(dst[:, s % 2, :], bk[5][:, :], ACT.Copy).then_inc(sem["spread_kept"], 1)
                        m = k - DECAY
                        if 0 <= m < NU:
                            s, i = divmod(m, NI)
                            if m == 0:
                                act.wait_ge(sem["delta_done"], 1)
                            if m >= 2:
                                act.wait_ge(sem["scan_done"], m - 1)
                            ac(dA[:, m % 2, :], delta[:, i, :], ACT.Exp, scale=negA[:, i * DS + s:i * DS + s + 1])\
                                .then_inc(sem["dA_done"], 1)

                    def step_b(t):
                        if not B:
                            return
                        if t == 1:
                            keep_xT(laneB, 1)
                        if t == 5:
                            act.wait_ge(sem["l2_ask"], 1)
                            ac(gate2, e2, ACT.Exp).then_inc(sem["l2_exp"], 1)
                        for j in range(NJ2):
                            if t == (6 + 3 * j if j else 4):
                                act.wait_ge(sem["up2_made"], j + 1)
                                if j >= 2:
                                    act.wait_ge(sem["h2_done"], j - 1)
                                ac(r2[:, j % 2, :], bk[3][:, :], ACT.Relu).then_inc(sem["relu_done"], 1)
                        if t == 21:
                            act.wait_ge(sem["down2_made"], NJ2)
                            ac(laneB.yT, bk[7][:, :], ACT.Copy).then_inc(sem["y_copied_b"], 1)

                    def keep_v(n):
                        act.wait_ge(sem["v_made"], n + 1)
                        ac(v[:, n // 2, 0:512], bk[n % 4][:, :], ACT.Copy).then_inc(sem["v_kept_a"], 1)

                    def exps(n, qbs):
                        for qb in qbs:
                            un = 4 * n + qb
                            N = P * (qb + 1)
                            if qb == 0 and n >= 2:
                                act.wait_ge(sem["pt_made"], 3 * (n - 1))
                                act.wait_ge(sem["rinv_done"], n - 1)
                            act.wait_ge(sem["max_done"], un + 1)
                            ac(prob[:, n % 2, PROB_OFF[qb]:PROB_OFF[qb] + N], bk[un % 2][:, 0:N], ACT.Exp,
                               bias=nmax[:, un % 8:un % 8 + 1], accum_out=rsum[:, un % 8:un % 8 + 1]).then_inc(sem["exp_done"], 1)

                    def keep_turned(n, g):
                        if n >= 2 and g == 0:
                            act.wait_ge(sem["pv_made"], n // 2)
                        act.wait_ge(sem["pt_made"], 3 * n + g + 1)
                        ac(probT[:, n % 2, 512 * g:512 * g + 512], bk[2 + (3 * n + g) % 2][:, :], ACT.Copy).then_inc(sem["pt_kept_a"], 1)

                    def keep_o(p):
                        if p:
                            act.wait_ge(sem["wo_made"], p)
                        act.wait_ge(sem["pv_made"], p + 1)
                        ac(o_h, bk[4][:, :], ACT.Identity, bias=sm("bv")[:, p:p + 1]).then_inc(sem["o_h_done"], 1)

                    def head(n):
                        if n + 1 < H:
                            exps(n + 1, (0, 1))
                        slot(3 * n)
                        if n + 1 < H:
                            exps(n + 1, (2, 3))
                        if n % 2 == 0 and n:
                            keep_o(n // 2 - 1)
                        slot(3 * n + 1)
                        keep_turned(n, 0)
                        keep_turned(n, 1)
                        slot(3 * n + 2)

                    if A:
                        keep_xT(laneA, 0)
                        keep_v(0)
                        keep_v(2)
                    if B:
                        keep_xT(laneB, 0)
                    if A:
                        keep_v(4)
                        keep_v(6)
                    if B:
                        keep_xin()
                    if A:
                        exps(0, range(NT))
                    for n in range(H):
                        if A:
                            head(n)
                        else:
                            for k in range(3 * n, 3 * n + 3):
                                slot(k)
                    if A:
                        keep_o(NP - 1)
                        act.wait_ge(sem["wo_made"], NP)
                        ac(laneA.yT, bk[6][:, :], ACT.Identity, bias=sm("bo")).then_inc(sem["y_copied_a"], 1)
                    if B:
                        act.wait_ge(sem["out_made"], 1)
                        ac(laneB.yT, bk[3][:, :], ACT.Copy).then_inc(sem["y_copied_b"], 1)
                    if A:
                        keep_xT(laneA, 1)
                        act.wait_ge(sem["lg_made"], 1)
                        ac(sc.rearrange(flat), bk[4][:, 0:NT * E], ACT.Exp, scale=-1.0).then_inc(sem["lg_exp"], 1)
                    for j in range(NJ):
                        if A:
                            if j >= 2:
                                act.wait_ge(sem["act1_done"], j - 1)
                            act.wait_ge(sem["g_made"], j + 1)
                            ac(sg[:, j % 2, :], bk[j % 2][:, :], ACT.Silu).then_inc(sem["silu_done"], 1)
                        step_b(j)
                    if A:
                        act.wait_ge(sem["down_made"], NJ)
                        if B:
                            act.wait_ge(sem["x_out"], 1)
                        ac(laneB.yT, bk[6][:, :], ACT.Copy).then_inc(sem["y_copied_a"], 1)

                @block.vector
                def _(dve):
                    V = nc.vector
                    seq = [0]

                    def link(ins):
                        seq[0] += 1
                        ins.then_inc(sem["dve_seq"], 1)
                        dve.wait_ge(sem["dve_seq"], seq[0])

                    asked = [0]

                    def ask_norm(L, rows):
                        for t in range(NT):
                            ins = V.bn_stats(L.stats[:, t, :], rows(t))
                        link(ins)
                        for t in range(NT):
                            ins = V.bn_aggr(L.mv[:, t, :], L.stats[:, t, :])
                        link(ins)
                        V.tensor_scalar(L.ve[:, :], L.mv[:, :, 1], EPS, None, ALU.add).then_inc(sem["pow_ask"], 1)
                        asked[0] += 1
                        return asked[0]

                    def ask_x(L, x):
                        return ask_norm(L, lambda t: x[:, t, :])

                    def norm_x(L, x, turn):
                        dve.wait_ge(sem["pow_done"], turn)
                        for t in range(NT):
                            ins = V.tensor_scalar(L.xn[:, t, :], x[:, t, :], L.mv[:, t, 0:1], L.rstd[:, t:t + 1], ALU.subtract, ALU.mult)
                        ins.then_inc(sem["xn_ready_" + L.name], 1)

                    def keep_xT(L, k):
                        dve.wait_ge(sem["xT_h_done_" + L.name], k + 1)
                        V.tensor_tensor(L.xT_l[:, :], L.bank[:, :], L.xT_h[:, :].bitcast(F32), ALU.subtract)\
                            .then_inc(sem["xT_l_done_" + L.name], 1)

                    def ask_y(L, k):
                        dve.wait_ge(sem["y_turned_" + L.name], k + 1)
                        return ask_norm(L, lambda t: L.bank[:, t * P:(t + 1) * P])

                    def add_y(L, dst, src, turn):
                        dve.wait_ge(sem["pow_done"], turn)
                        for t in range(NT):
                            ins = V.tensor_scalar(L.xn[:, t, :], L.bank[:, t * P:(t + 1) * P], L.mv[:, t, 0:1], L.rstd[:, t:t + 1],
                                                  ALU.subtract, ALU.mult)
                        link(ins)
                        return V.tensor_tensor(dst[:, :, :], src[:, :, :], L.xn[:, :, :], ALU.add)

                    cw = sm("convw").rearrange("p (i c) -> p i c", c=DC)

                    def conv(c):
                        if c == 0:
                            dve.wait_ge(sem["xin_done"], NI)
                        src, dst = (ca, cb) if c % 2 else (cb, ca)
                        for i in range(NI):
                            if c == 0:
                                ins = V.tensor_scalar(ca[:, i, :], xin[:, i, 0:S], cw[:, i, 0:1], None, ALU.mult)
                            else:
                                ins = V.scalar_tensor_tensor(dst[:, i, :], xin[:, i, c:c + S], cw[:, i, c:c + 1], src[:, i, :],
                                                             ALU.mult, ALU.add)
                            if c == DC - 1:
                                ins.then_inc(sem["conv_done"], 1)
                        if c < DC - 1:
                            link(ins)

                    def slot(k):
                        if not B:
                            return
                        if k < DC:
                            conv(k)
                        if k == 6:
                            dve.wait_ge(sem["xp_made"], 1)
                            V.tensor_copy(bc_r[0:32, :], bk[7][0:32, :]).then_inc(sem["bc_done"], 1)
                            for i in range(NI):
                                V.tensor_scalar(xs[:, i, :], bk[5][:, :], sm("wdt")[:, i:i + 1], sm("bdt")[:, i:i + 1], ALU.mult, ALU.add)\
                                 .then_inc(sem["xs_done"], 1)
                        if k == 7:
                            dve.wait_ge(sem["bc_done"], 1)
                            V.tensor_tensor(bc_r[32:64, :], bk[7][0:32, :], bc_r[0:32, :].bitcast(F32), ALU.subtract).then_inc(sem["bc_done"], 1)
                        if k == 8:
                            dve.wait_ge(sem["sp_exp"], 1)
                            V.tensor_scalar(ca, cb, 1.0, None, ALU.add).then_inc(sem["sp_w1"], 1)
                            dve.wait_ge(sem["sp_w1"], 1)
                            link(V.scalar_tensor_tensor(cb, ca, 1.0, cb, ALU.subtract, ALU.subtract))
                        if k == 10:
                            dve.wait_ge(sem["sp_ln"], 1)
                            link(V.tensor_tensor(delta, delta, cb, ALU.subtract))
                            link(V.scalar_tensor_tensor(delta, xs, 0.0, delta, ALU.max, ALU.add))
                            V.tensor_tensor(du, delta, u, ALU.mult).then_inc(sem["delta_done"], 1)
                        m = k - SCAN
                        if 0 <= m < NU:
                            dve.wait_ge(sem["dA_done"], m + 1)
                            dve.wait_ge(sem["dBu_done"], m + 1)
                            if m >= 2:
                                dve.wait_ge(sem["hc_done"], m - 1)
                            V.tensor_tensor_scan(hs[:, m % 2, :], dA[:, m % 2, :], dBu[:, m % 2, :], 0.0, ALU.mult, ALU.add)\
                             .then_inc(sem["scan_done"], 1)
                        m = k - READ
                        if 0 <= m < NU:
                            s, i = divmod(m, NI)
                            dve.wait_ge(sem["scan_done"], m + 1)
                            dve.wait_ge(sem["spread_kept"], 2 * s + 2)
                            if s:
                                dve.wait_ge(sem["y1_done" if i else "y_made"], s)
                            V.tensor_tensor(hc[:, i, :], hs[:, m % 2, :], Cs[:, s % 2, :], ALU.mult).then_inc(sem["hc_done"], 1)
                        m = k - SUM
                        if 0 <= m < NU and m % 2:
                            s = m // 2
                            dve.wait_ge(sem["hc_done"], m + 1)
                            if s:
                                dve.wait_ge(sem["y1_done"], s)
                                V.tensor_tensor(y1, y1, hc[:, 1, :], ALU.add).then_inc(sem["y1_done"], 1)
                            else:
                                V.tensor_copy(y1, hc[:, 1, :]).then_inc(sem["y1_done"], 1)

                    def gate_y():
                        dve.wait_ge(sem["y_made"], DS)
                        dve.wait_ge(sem["y1_done"], DS)
                        for i in range(NI):
                            ins = V.scalar_tensor_tensor(cb[:, i, :], u[:, i, :], sm("dskip")[:, i:i + 1], y1 if i else bk[7][:, :], ALU.mult, ALU.add)
                        link(ins)
                        dve.wait_ge(sem["sz_done"], NI)
                        for i in range(NI):
                            V.tensor_tensor(ca[:, i, :], cb[:, i, :], sz[:, i, :], ALU.mult).then_inc(sem["y2_done"], 1)

                    def hidden2(j):
                        dve.wait_ge(sem["relu_done"], j + 1)
                        if j >= 2:
                            dve.wait_ge(sem["down2_made"], j - 1)
                        r = r2[:, j % 2, :]
                        if j:
                            dve.wait_ge(sem["p2_made"], j)
                            link(V.tensor_tensor(rp2[:, j % 2, :], r, bk[5][:, :], ALU.mult))
                            V.tensor_tensor(h2[:, j % 2, :], rp2[:, j % 2, :], r, ALU.mult).then_inc(sem["h2_done"], 1)
                        else:
                            V.tensor_tensor(h2[:, 0, :], r, r, ALU.mult).then_inc(sem["h2_done"], 1)

                    b_turn = [0]

                    def step_b(t):
                        if not B:
                            return
                        if t == 0:
                            norm_x(laneB, xB, b_turn[0])
                        if t == 2:
                            keep_xT(laneB, 1)
                        if t == 4:
                            dve.wait_ge(sem["l2_made"], 1)
                            link(V.tensor_copy(lg.rearrange(flat), bk[5][:, 0:NT * E2]))
                            for i in range(NT):
                                ins = V.max(v8[:, i, :], lg[:, i, :])
                            link(ins)
                            V.tensor_tensor(e2, v8[:, :, 1], v8[:, :, 0], ALU.subtract).then_inc(sem["l2_ask"], 1)
                        if t == 5:
                            hidden2(0)
                        if t == 6:
                            dve.wait_ge(sem["l2_exp"], 1)
                            link(V.tensor_scalar(gate2, gate2, 1.0, None, ALU.add))
                            link(V.reciprocal(gate2, gate2))
                            link(V.tensor_scalar(gate2, gate2, 1.0, None, ALU.is_ge))
                            link(V.tensor_tensor(pr2, lg, v8[:, :, 0:1].broadcast_to([P, NT, E2]), ALU.is_equal))
                            V.tensor_tensor(pr2, pr2, gate2.rearrange("p (a o) -> p a o", o=1).broadcast_to([P, NT, E2]), ALU.mult)\
                             .then_inc(sem["p2_ask"], 1)
                        if t == 8:
                            dve.wait_ge(sem["p2_turned"], 1)
                            V.tensor_copy(pT2[0:E2, :], bk[5][0:E2, :]).then_inc(sem["pT2_done"], 1)
                        for j in range(1, NJ2):
                            if t == 7 + 3 * j:
                                hidden2(j)
                        if t == 23:
                            b_turn[0] = ask_y(laneB, 2)
                        if t == 24:
                            add_y(laneB, xB, xB, b_turn[0]).then_inc(sem["x_out"], 1)

                    def keep_v(n):
                        dve.wait_ge(sem["v_made"], n + 1)
                        V.tensor_copy(v[:, n // 2, 512:1024], bk[n % 4][:, :]).then_inc(sem["v_kept_d"], 1)

                    def rope_term(p, kind):
                        n = 4 * p + kind
                        m = n // 2
                        dve.wait_ge(sem["proj_made"], n + 1)
                        tab = sm("sin" if kind % 2 else "cos")
                        bias = sm("bqk")[:, 4 * p + kind:4 * p + kind + 1]
                        if kind % 2 == 0 and m >= 2:
                            dve.wait_ge(sem["rope_l_done"], m - 1)
                        if kind % 2 == 1 and m >= 1:
                            dve.wait_ge(sem["rope_sum"], m)
                        dst = ropeB if kind % 2 else ropeA[:, m % 2, :]
                        V.scalar_tensor_tensor(dst, bk[4][:, :], bias, tab, ALU.add, ALU.mult).then_inc(sem["rope_terms"], 1)

                    def rope_high(m):
                        p = m // 2
                        dve.wait_ge(sem["rope_sum"], m + 1)
                        if p >= 2:
                            dve.wait_ge(sem["s_made"], 8 * (p - 1))
                        V.tensor_copy((k_h if m % 2 else q_h)[:, p % 2, :], ropeA[:, m % 2, :]).then_inc(sem["rope_h_done"], 1)

                    def row_max(n, qb):
                        un = 4 * n + qb
                        dve.wait_ge(sem["s_made"], un + 1)
                        V.tensor_reduce(nmax[:, un % 8:un % 8 + 1], bk[un % 2][:, 0:P * (qb + 1)], AX.X, ALU.max, negate=True)\
                         .then_inc(sem["max_done"], 1)

                    def row_inv(n):
                        dve.wait_ge(sem["exp_done"], 4 * (n + 1))
                        if n >= 2:
                            dve.wait_ge(sem["norm_done"], 4 * (n - 1))
                        a = 4 * (n % 2)
                        V.reciprocal(rinv[:, a:a + 4], rsum[:, a:a + 4]).then_inc(sem["rinv_done"], 1)

                    def keep_turned(n):
                        if n >= 2:
                            dve.wait_ge(sem["pv_made"], n // 2)
                        dve.wait_ge(sem["pt_made"], 3 * n + 3)
                        V.tensor_copy(probT[:, n % 2, 1024:1280], bk[2 + (3 * n + 2) % 2][:, 0:256]).then_inc(sem["pt_kept_d"], 1)

                    def keep_o(p):
                        dve.wait_ge(sem["o_h_done"], p + 1)
                        V.scalar_tensor_tensor(o_l, bk[4][:, :], sm("bv")[:, p:p + 1], o_h.bitcast(F32), ALU.add, ALU.subtract)\
                         .then_inc(sem["o_l_done"], 1)

                    def begin_a():
                        for m in range(4):
                            rope_term(m // 2, 2 * (m % 2))
                            rope_term(m // 2, 2 * (m % 2) + 1)
                            rope_high(m)
                        for qb in range(NT):
                            row_max(0, qb)
                        row_inv(0)

                    def head(n):
                        pp, kinds = n // 2 + 2, ((0, 1) if n % 2 == 0 else (2, 3))
                        more = pp < NP
                        if n + 1 < H:
                            row_max(n + 1, 0)
                            row_max(n + 1, 1)
                        if more:
                            rope_term(pp, kinds[0])
                        slot(3 * n)
                        if n + 1 < H:
                            row_max(n + 1, 2)
                            row_max(n + 1, 3)
                        if n % 2 == 0 and n:
                            keep_o(n // 2 - 1)
                        slot(3 * n + 1)
                        if n + 1 < H:
                            row_inv(n + 1)
                        slot(3 * n + 2)
                        if more:
                            rope_term(pp, kinds[1])
                        keep_turned(n)
                        if more:
                            rope_high(2 * pp + kinds[0] // 2)

                    def route():
                        s2 = sc.rearrange(flat)
                        V.memset(gm[:, :, G:], TOP)
                        V.memset(ms[:, :, E:], TOP)
                        dve.wait_ge(sem["lg_exp"], 1)
                        link(V.tensor_scalar(s2, s2, 1.0, None, ALU.add))
                        link(V.reciprocal(s2, s2))
                        link(V.tensor_tensor(sc, sc, sm("gbias").rearrange("p (o e) -> p o e", o=1).broadcast_to([P, NT, E]), ALU.add))
                        link(V.tensor_reduce(gm[:, :, 0:G], sc.rearrange("p a (g e) -> p a g e", e=E // G), AX.X, ALU.max))
                        for t in range(NT):
                            ins = V.max(g8[:, t, :], gm[:, t, :])
                        link(ins)
                        for t in range(NT):
                            ins = V.match_replace(gr[:, t, :], g8[:, t, :], gm[:, t, :], TAKEN)
                        link(ins)
                        link(V.tensor_scalar(gmask, gr[:, :, 0:G], TAKEN, None, ALU.is_equal))
                        for t in range(NT):
                            ins = V.tensor_tensor(ms[:, t, 0:E].rearrange("p (g e) -> p g e", e=E // G),
                                                  sc[:, t, :].rearrange("p (g e) -> p g e", e=E // G),
                                                  gmask[:, t, :].rearrange("p (g o) -> p g o", o=1).broadcast_to([P, G, E // G]), ALU.mult)
                        link(ins)
                        for t in range(NT):
                            ins = V.max(s8[:, t, :], ms[:, t, :])
                        link(ins)
                        for t in range(NT):
                            ins = V.match_replace(sr[:, t, :], s8[:, t, :], ms[:, t, :], TAKEN)
                        link(ins)
                        link(V.scalar_tensor_tensor(comb, sr[:, :, 0:E], TAKEN, ms[:, :, 0:E], ALU.is_equal, ALU.mult))
                        link(V.tensor_reduce(csum, comb, AX.X, ALU.add))
                        link(V.tensor_scalar(csum, csum, 1e-8, None, ALU.add))
                        link(V.reciprocal(csum, csum))
                        link(V.tensor_tensor(comb, comb, csum.rearrange("p (a o) -> p a o", o=1).broadcast_to([P, NT, E]), ALU.mult))
                        for t in range(NT):
                            c4 = cs[:, t, :].rearrange("p (g h e) -> p g h e", h=2, e=16)
                            ins = V.tensor_copy(c4[:, :, 0, :].bitcast(F32R), comb[:, t, :].rearrange("p (g e) -> p g e", e=16))
                        link(ins)
                        for t in range(NT):
                            c4 = cs[:, t, :].rearrange("p (g h e) -> p g h e", h=2, e=16)
                            ins = V.tensor_tensor(c4[:, :, 1, :], comb[:, t, :].rearrange("p (g e) -> p g e", e=16), c4[:, :, 0, :], ALU.subtract)
                        ins.then_inc(sem["comb_ask"], 1)

                    def gated(j):
                        dve.wait_ge(sem["silu_done"], j + 1)
                        dve.wait_ge(sem["u_made"], j + 1)
                        if j >= 3:
                            dve.wait_ge(sem["down_made"], j - 2)
                        ins = V.tensor_tensor(hid[:, j % 3, :], sg[:, j % 2, :], bk[2][:, :], ALU.mult)
                        ins.then_inc(sem["act1_done"], 1)

                    def weighted(j):
                        dve.wait_ge(sem["act1_done"], j + 1)
                        if j:
                            dve.wait_ge(sem["c_made"], j)
                            V.tensor_tensor(hid[:, j % 3, :], hid[:, j % 3, :], bk[4][:, :], ALU.mult).then_inc(sem["hid_done"], 1)
                        else:
                            V.nop().then_inc(sem["hid_done"], 1)

                    def experts(j):
                        if j >= 1:
                            weighted(j - 1)
                        if j == 1:
                            dve.wait_ge(sem["comb_turned"], 1)
                            V.tensor_copy(combT, bk[4][:, :]).then_inc(sem["combT_done"], 1)
                        gated(j)

                    if B:
                        by = ask_y(laneB, 0)
                    if A:
                        dve.wait_ge(sem["x_in_"], 16)
                        ax = ask_x(laneA, x0)
                    if B:
                        V.memset(xin[:, :, 0:DC - 1], 0.0)
                        link(add_y(laneB, xB, xA, by))
                    if A:
                        norm_x(laneA, x0, ax)
                    if B:
                        bx = ask_x(laneB, xB)
                    if A:
                        keep_xT(laneA, 0)
                    if B:
                        norm_x(laneB, xB, bx)
                    if A:
                        keep_v(1)
                        keep_v(3)
                    if B:
                        keep_xT(laneB, 0)
                    if A:
                        keep_v(5)
                        keep_v(7)
                        begin_a()
                    for n in range(H):
                        if A:
                            head(n)
                        else:
                            for k in range(3 * n, 3 * n + 3):
                                slot(k)
                    if A:
                        keep_o(NP - 1)
                    if B:
                        gate_y()
                    if A:
                        ay = ask_y(laneA, 0)
                        link(add_y(laneA, xA, x0, ay))
                        ax = ask_x(laneA, xA)
                    if B:
                        by = ask_y(laneB, 1)
                    if A:
                        norm_x(laneA, xA, ax)
                    if B:
                        link(add_y(laneB, xB, xB, by))
                    if A:
                        keep_xT(laneA, 1)
                    if B:
                        b_turn[0] = ask_x(laneB, xB)
                    if A:
                        route()
                    for j in range(NJ):
                        if A:
                            experts(j)
                        step_b(j)
                    if A:
                        weighted(NJ - 1)

                @block.gpsimd
                def _(pool):
                    Q = nc.gpsimd
                    asked = [0]

                    def power(L):
                        asked[0] += 1
                        pool.wait_ge(sem["pow_ask"], asked[0])
                        Q.tensor_tensor(L.rstd[:, :], L.ve[:, :], half_neg[:, :], ALU.pow).then_inc(sem["pow_done"], 1)

                    def slot(k):
                        m = k - DECAY
                        if B and 0 <= m < NU:
                            s, i = divmod(m, NI)
                            if m == 0:
                                pool.wait_ge(sem["delta_done"], 1)
                            pool.wait_ge(sem["spread_kept"], 2 * s + 1)
                            if m >= 2:
                                pool.wait_ge(sem["scan_done"], m - 1)
                            Q.tensor_tensor(dBu[:, m % 2, :], du[:, i, :], Bs[:, s % 2, :], ALU.mult).then_inc(sem["dBu_done"], 1)

                    def rope_sum(m):
                        pool.wait_ge(sem["rope_terms"], 2 * m + 2)
                        a = ropeA[:, m % 2, :]
                        Q.tensor_tensor(a, a, ropeB, ALU.add).then_inc(sem["rope_sum"], 1)

                    def rope_low(m):
                        p = m // 2
                        pool.wait_ge(sem["rope_h_done"], m + 1)
                        hi, lo = (k_h, k_l) if m % 2 else (q_h, q_l)
                        Q.tensor_tensor(lo[:, p % 2, :], ropeA[:, m % 2, :], hi[:, p % 2, :].bitcast(F32), ALU.subtract)\
                         .then_inc(sem["rope_l_done"], 1)

                    def normalise(n):
                        pool.wait_ge(sem["rinv_done"], n + 1)
                        for qb in range(NT):
                            a = prob[:, n % 2, PROB_OFF[qb]:PROB_OFF[qb] + P * (qb + 1)]
                            c = 4 * (n % 2) + qb
                            Q.tensor_scalar(a, a, rinv[:, c:c + 1], 0.0, ALU.mult, ALU.add).then_inc(sem["norm_done"], 1)

                    def begin_a():
                        for m in range(4):
                            rope_sum(m)
                            rope_low(m)
                        normalise(0)

                    def head(n):
                        m = 2 * (n // 2 + 2) + n % 2
                        slot(3 * n)
                        slot(3 * n + 1)
                        if n + 1 < H:
                            normalise(n + 1)
                        slot(3 * n + 2)
                        if m < 2 * NP:
                            rope_sum(m)
                            rope_low(m)

                    if B:
                        power(laneB)
                    if A:
                        power(laneA)
                    if B:
                        power(laneB)
                    if A:
                        begin_a()
                    for n in range(H):
                        if A:
                            head(n)
                        else:
                            for k in range(3 * n, 3 * n + 3):
                                slot(k)
                    if A:
                        power(laneA)
                        power(laneA)
                    if B:
                        for _ in range(3):
                            power(laneB)
            nc.all_engine_barrier(sems_to_clear=range(first.num, last_sem.num + 1))

        turn(True, False, x_in[0:1], None)
        with nc.Fori(0, NB - 1) as b:
            turn(True, True, x_in[1:NB][bass.ds(b, 1)], out[0:NB - 1][bass.ds(b, 1)])
        turn(False, True, None, out[NB - 1:NB])


def kernel(**inputs):
    import numpy as np
    import concourse.bacc as bacc
    from concourse.bass_utils import run_bass_kernel_spmd as run

    a = {k: np.asarray(t) for k, t in inputs.items()}
    f32 = np.float32

    half = DK // 2
    theta = (f32(10000.0) ** (np.arange(0, DK, 2, dtype=f32) / f32(DK))).astype(f32)
    freqs = (np.arange(S, dtype=f32)[:, None] * (f32(1.0) / theta)[None, :]).astype(f32)
    emb = np.concatenate([freqs, freqs], axis=-1).T
    sign = np.where(np.arange(DK) % 2 == 0, f32(-1), f32(1))[:, None]
    cos, sin = np.tile(np.cos(emb), (2, 1)), np.tile(np.sin(emb) * sign, (2, 1))
    r = np.arange(P)
    sel = (np.arange(1024)[None, :] // 64 == (r % 16)[:, None]).astype(f32)
    small = {
        "ident": np.eye(P, dtype=f32), "eye": np.eye(P, dtype=f32), "mask": np.where(r[None, :] > r[:, None], f32(MASKED), f32(0)),
        "cos": cos, "sin": sin, "sel": sel,
        "i64": ((r % 32)[:, None] == np.arange(32)[None, :]).astype(f32),
    }

    swap = np.arange(H * DK) ^ 1

    def by_pair(w):
        return w.T.reshape(D, NP, P)

    wq, wk, bq, bk_ = a["L0_attn_wq"], a["L0_attn_wk"], a["L0_attn_bq"], a["L0_attn_bk"]
    wqk = np.stack([by_pair(w) for w in (wq, wq[swap], wk, wk[swap])], axis=2).reshape(D, NP * 4 * P)
    small["bqk"] = np.stack([t.reshape(NP, P).T for t in (bq, bq[swap], bk_, bk_[swap])], axis=2)
    small["bv"] = a["L0_attn_bv"].reshape(NP, P).T
    small["bo"] = a["L0_attn_bo"].reshape(D, 1)
    small["gbias"] = np.broadcast_to(a["L0_ffn_gate_bias"], (P, E))
    small["convw"] = a["L1_attn_conv_w"].reshape(NI, P, DC).transpose(1, 0, 2)
    small["convb"] = a["L1_attn_conv_b"].reshape(NI, P).T
    wx = a["L1_attn_W_xproj"]
    small["wx"] = np.concatenate([wx[1:], wx[:1]], axis=0).T.reshape(NI, P, 33).transpose(1, 0, 2)
    small["wdt"] = a["L1_attn_W_dt"].reshape(NI, P).T
    small["bdt"] = a["L1_attn_b_dt"].reshape(NI, P).T
    small["alog"] = a["L1_attn_A_log"].reshape(NI, P, DS).transpose(1, 0, 2)
    small["dskip"] = a["L1_attn_D"].reshape(NI, P).T
    small["wout"] = a["L1_attn_W_out"].T.reshape(NI, P, D).transpose(1, 0, 2)
    small["gate"] = a["L0_ffn_gate_w"].T
    small["wr"] = a["L1_ffn_Wr"]
    packed, packed_once = (np.concatenate([np.ascontiguousarray(small[n]).reshape(P, -1) for n in names], axis=1)
                           for names in (SMALL, ONCE))

    def up(shared, w):
        return np.concatenate([shared, w.transpose(2, 0, 1).reshape(D, -1)], axis=1)

    wd = np.concatenate([a["L0_ffn_sd_w"].T, a["L0_ffn_ed_w"].transpose(0, 2, 1).reshape(-1, D)], axis=0)
    w1 = np.concatenate([a["L1_ffn_Ws1"], np.zeros((D, 64), f32), a["L1_ffn_W1"].transpose(1, 0, 2).reshape(D, -1)], axis=1)
    w2 = np.concatenate([a["L1_ffn_Ws2"], np.zeros((64, D), f32), a["L1_ffn_W2"].reshape(-1, D)], axis=0)
    arrays = {
        "x": a["L0_attn_x"], "small": packed, "once": packed_once, "wqk": wqk, "wv": a["L0_attn_wv"].T,
        "wo": a["L0_attn_wo"].T.reshape(NP, P, D).transpose(1, 0, 2).reshape(P, NP * D),
        "wg": up(a["L0_ffn_sg_w"].T, a["L0_ffn_eg_w"]), "wu": up(a["L0_ffn_su_w"].T, a["L0_ffn_eu_w"]),
        "wd": wd.reshape(NJ, P, D).transpose(1, 0, 2).reshape(P, NJ * D),
        "win": a["L1_attn_W_in"].T, "w1": w1, "w2": w2.reshape(NJ2, P, D).transpose(1, 0, 2).reshape(P, NJ2 * D),
    }

    nc = bacc.Bacc("TRN2", target_bir_lowering=False, num_devices=1)
    feeds, args = {}, []
    for name, t in arrays.items():
        t = np.ascontiguousarray(t)
        feeds[f"in_{name}"] = t
        args.append(nc.dram_tensor(f"in_{name}", t.shape, mybir.dt.from_np(t.dtype), kind="ExternalInput").ap())
    args.append(nc.dram_tensor("out_x", (NB, S, D), F32, kind="ExternalOutput").ap())
    layers_kernel(nc, *args)
    r = run(nc, [feeds], core_ids=[0])
    return r.results[0]["out_x"]
```

```python
from contextlib import ExitStack

import concourse.bass as bass
from concourse import mybir

F32 = mybir.dt.float32
F32R = mybir.dt.float32r
ALU = mybir.AluOpType
ACT = mybir.ActivationFunctionType
AX = mybir.AxisListType

P = 128
NB = 8
S = 512
NT = S // P
D = 128
H = 16
DK = 64
NP = H // 2
E, G, TG, TK = 64, 8, 4, 6
NHID = 8
WUCH = 8
NJ = 1 + E // 2
DI, DS, DC = 256, 16, 4
NI = DI // P
E2 = 8
NJ2 = 1 + E2 // 2
EPS = 1e-5
MASKED = -1e30
TOP = 3e38
TAKEN = -3e38

def columns(parts):
    at, where = 0, {}
    for name, n in parts:
        where[name] = (at, at + n)
        at += n
    return where, at


SMALL, NSMALL = columns([
    ("cos", S), ("sin", S), ("bqk", NP * 4), ("bv", NP), ("bo", 1),
    ("gbias", E), ("convw", NI * DC), ("convb", NI), ("wx", NI * 64), ("wdt", NI), ("bdt", NI),
    ("alog", NI * DS), ("dskip", NI), ("wout", NI * D)])
ONCE, NONCE = columns([("eye", P), ("mask", P), ("sel", 1024), ("pick", 33), ("gate", E), ("wr", E2)])
PART_OFF = [0, 512, 1024, 896]
PROB_OFF = [0, 128, 384, 768]


def layers_kernel(nc, x_in, small_in, once_in, wqk_in, wv_in, wo_in, wg_in, wu_in, wd_in, win_in, w1_in, w2_in, out):
    ctx = ExitStack()
    with ctx:
        def sb(name, shape, dt=F32):
            return ctx.enter_context(nc.sbuf_tensor(name, shape, dt))

        small = sb("small", [P, NSMALL])

        def sm(name):
            a, b = SMALL[name]
            return small[:, a:b]

        wv_h, wv_l = sb("wv_h", [P, H * DK], F32R), sb("wv_l", [P, H * DK], F32R)
        wo_h, wo_l = sb("wo_h", [P, NP, D], F32R), sb("wo_l", [P, NP, D], F32R)
        wg_h = sb("wg_h", [P, NJ * P], F32R)
        wu_h = sb("wu_h", [P, NJ * P], F32R)
        win_h, win_l = sb("win_h", [P, 2 * DI], F32R), sb("win_l", [P, 2 * DI], F32R)
        w1_h, w1_l = sb("w1_h", [P, NJ2 * P], F32R), sb("w1_l", [P, NJ2 * P], F32R)
        w2 = sb("w2", [P, NJ2, D])
        gate_h, gate_l = sb("gate_h", [P, E], F32R), sb("gate_l", [P, E], F32R)
        wr_h, wr_l = sb("wr_h", [P, E2], F32R), sb("wr_l", [P, E2], F32R)
        ident_r, mask_r = sb("ident_r", [P, P], F32R), sb("mask_r", [P, P], F32R)
        pick_r = sb("pick_r", [P, 33], F32R)
        sel_r = sb("sel_r", [P, 1024], F32R)
        negA = sb("negA", [P, NI * DS])
        half_neg = sb("half_neg", [P, NT])
        ident = ident_r[:, :].bitcast(F32)

        x0, xA, xB = (sb(n, [P, NT, D]) for n in ("x0", "xA", "xB"))

        class Lane:
            def __init__(lane, n, bank):
                lane.name, lane.bank = n, bank
                lane.xn = sb("xn_" + n, [P, NT, D])
                lane.yT = lane.xn[:, :, :].rearrange("p a b -> p (a b)")
                lane.xT_h, lane.xT_l = sb("xT_h_" + n, [P, S], F32R), sb("xT_l_" + n, [P, S], F32R)
                lane.stats, lane.mv = sb("stats_" + n, [P, NT, 6]), sb("mv_" + n, [P, NT, 2])
                lane.ve, lane.rstd = sb("ve_" + n, [P, NT]), sb("rstd_" + n, [P, NT])

        bk = [ctx.enter_context(nc.psum_tensor(f"bank{i}", [P, S], F32)) for i in range(8)]
        laneA, laneB = Lane("a", bk[4]), Lane("b", bk[5])

        WORK, WORKR, WORKB, WORKBR = 12312, 2048 + 4224 + S, 10246, S
        spaces = {("A", F32): sb("work", [P, WORK]), ("A", F32R): sb("workr", [P, WORKR], F32R),
                  ("B", F32): sb("work_b", [P, WORKB]), ("B", F32R): sb("workr_b", [P, WORKBR], F32R)}
        sizes = {("A", F32): WORK, ("A", F32R): WORKR, ("B", F32): WORKB, ("B", F32R): WORKBR}
        at = {k: 0 for k in spaces}

        def piece(*dims, dt=F32, lane="A"):
            n = 1
            for d in dims:
                n *= d
            k = (lane, dt)
            assert at[k] + n <= sizes[k], (k, at[k], n)
            a = spaces[k][:, at[k]:at[k] + n]
            at[k] += n
            if len(dims) == 2:
                a = a.rearrange("p (a b) -> p a b", b=dims[1])
            if len(dims) == 3:
                a = a.rearrange("p (a b c) -> p a b c", b=dims[1], c=dims[2])
            return a

        def again(lane, f32=0, f32r=0):
            at[(lane, F32)], at[(lane, F32R)] = f32, f32r

        v = piece(NT, H * DK)
        wqk = piece(2, 2, 4 * P, dt=F32R)
        ropeA, ropeB = piece(S), piece(S)
        q_rot, k_rot = piece(2, S), piece(2, S)
        prob = piece(2, 1280)
        probT = piece(2, 1280)
        o_h, o_l = piece(S, dt=F32R), piece(S, dt=F32R)
        nmax, rsum, rinv = piece(8), piece(8), piece(8)
        again("A", 0, 2 * 2 * 4 * P)
        wd = piece(NJ, D)
        wg_l = piece(NJ * P, dt=F32R)
        wu_l = spaces[("A", F32R)][:, 0:2 * WUCH * P].rearrange("p (a b) -> p a b", b=WUCH * P)
        sg = piece(2, S)
        su = piece(S)
        hid = piece(NHID, S)
        sc = piece(NT, E)
        gm, gr = piece(NT, G + 4), piece(NT, G + 4)
        g8 = piece(NT, 8)
        gmask = piece(NT, G)
        ms, sr = piece(NT, E + 2), piece(NT, E + 2)
        s8 = piece(NT, 8)
        csum = piece(NT)
        comb = piece(NT, E)
        cs = piece(NT, P)
        combT = piece(S, dt=F32R)
        xin = piece(NI, S + DC - 1, lane="B")
        ca, cb, u, sz, xs, delta, du, dBu, Cs = (piece(NI, S, lane="B") for _ in range(9))
        y1 = laneB.yT
        bc_r = piece(S, dt=F32R, lane="B")
        Bs = spaces[("B", F32)][:, 0:NI * S].rearrange("p (a b) -> p a b", b=S)
        dA, hc, hs = xs, ca, cb
        again("B")
        r2, rp2, h2 = (piece(2, S, lane="B") for _ in range(3))
        lg = piece(NT, E2, lane="B")
        v8 = piece(NT, 8, lane="B")
        e2, gate2 = piece(NT, lane="B"), piece(NT, lane="B")
        pr2 = piece(NT, E2, lane="B")
        pT2 = piece(S, dt=F32R, lane="B")
        again("A")
        again("B")
        raw_wg, raw_wu = piece(NJ * P), piece(NJ * P)
        once = piece(NONCE)
        raw_wv, raw_qk, raw_wo = piece(H * DK, lane="B"), piece(NP * 4 * P, lane="B"), piece(H * DK, lane="B")
        raw_win, raw_w1 = piece(2 * DI, lane="B"), piece(NJ2 * P, lane="B")
        HALF = NJ * P // 2
        passing = [piece(HALF, dt=F32R) for _ in range(3)]

        def on(name):
            a, b = ONCE[name]
            return once[:, a:b]


        wqk_split = nc.dram_tensor("wqk_split", (NP, P, 2, 4 * P), F32, kind="Internal").ap()
        wg_low, wu_low = (nc.dram_tensor(n, (P, NJ * P), F32, kind="Internal").ap() for n in ("wg_low", "wu_low"))
        flat = "p a b -> p (a b)"
        SCALE = DK ** -0.5

        NQK = NP * 4 * P // 1024

        def pass_on(r):
            return passing[(r + 1) % 3]

        jobs = [(raw_wv, "wv", wv_h[:, :], wv_l[:, :], None)]
        jobs += [(raw_qk[:, 1024 * c:1024 * c + 1024], "qk", pass_on(c)[:, 0:1024], pass_on(c)[:, 1024:2048], c) for c in range(NQK)]
        jobs += [(raw_wo, "wo", wo_h[:, :, :].rearrange(flat), wo_l[:, :, :].rearrange(flat), None),
                 (raw_win, "win", win_h[:, :], win_l[:, :], None), (raw_w1, "w1", w1_h[:, :], w1_l[:, :], None)]
        for n, (name, raw, high) in enumerate((("wg", raw_wg, wg_h), ("wu", raw_wu, wu_h))):
            for c in range(2):
                w, r = slice(c * HALF, c * HALF + HALF), NQK + 2 * n + c
                jobs.append((raw[:, w], name, high[:, w], pass_on(r), r))
        s0 = {n: ctx.enter_context(nc.semaphore(n)) for n in
              ("small_in_", "once_in", "wv_in_", "qk_in_", "wo_in_", "win_in_", "w1_in_", "wg_in_", "wu_in_", "w2_in_",
               "split_h", "split_l", "negA_done")}
        stored = [ctx.enter_context(nc.semaphore(f"stored{r}")) for r in range(NQK + 4)]

        def wait_stored(eng, r):
            eng.wait_ge(stored[r], 64 if r < NQK else 16)

        with nc.Block() as block:
            @block.sync
            def _(sp):
                for dst, src, name in ((raw_wv, wv_in, "wv_in_"), (raw_qk, wqk_in, "qk_in_"), (small[:, :], small_in, "small_in_"),
                                       (once, once_in, "once_in"), (raw_wo, wo_in, "wo_in_"),
                                       (raw_win, win_in, "win_in_"), (raw_w1, w1_in, "w1_in_"), (raw_wg, wg_in, "wg_in_"),
                                       (raw_wu, wu_in, "wu_in_"), (w2[:, :, :].rearrange(flat), w2_in, "w2_in_")):
                    sp.dma_start(dst, src).then_inc(s0[name], 16)
                for n, (_, name, high, low, r) in enumerate(jobs):
                    if name == "qk":
                        sp.wait_ge(s0["split_l"], n + 1)
                        for h in range(2):
                            for part, src in ((0, high), (1, low)):
                                sp.dma_start(wqk_split[2 * r + h, :, part, :], src[:, 512 * h:512 * h + 512].bitcast(F32))\
                                    .then_inc(stored[r], 16)
                    elif r is not None:
                        sp.wait_ge(s0["split_l"], n + 1)
                        dst = wg_low if name == "wg" else wu_low
                        c = (r - NQK) % 2
                        sp.dma_start(dst[:, c * HALF:c * HALF + HALF], low.bitcast(F32)).then_inc(stored[r], 16)
                for r in range(NQK + 2):
                    wait_stored(sp, r)
                sp.wait_ge(s0["w2_in_"], 16)

            def wait_passed(eng, r):
                if r is not None and r >= 3:
                    wait_stored(eng, r - 3)

            @block.scalar
            def _(act):
                for raw, name, high, _, r in jobs:
                    act.wait_ge(s0[name + "_in_"], 16)
                    if name == "qk":
                        wait_passed(act, r)
                        th, tr = (w.rearrange("p (a k n) -> p a k n", k=2, n=2 * P) for w in (high, raw))
                        nc.scalar.activation(th[:, :, 0, :], tr[:, :, 0, :], ACT.Copy, scale=SCALE)
                        nc.scalar.activation(th[:, :, 1, :], tr[:, :, 1, :], ACT.Copy).then_inc(s0["split_h"], 1)
                    else:
                        nc.scalar.activation(high, raw, ACT.Copy).then_inc(s0["split_h"], 1)
                act.wait_ge(s0["small_in_"], 16)
                nc.scalar.activation(negA[:, :], sm("alog"), ACT.Exp).then_inc(s0["negA_done"], 1)
                act.wait_ge(s0["negA_done"], 1)
                nc.scalar.mul(negA[:, :], negA[:, :], -1.0)

            @block.vector
            def _(dve):
                for n, (raw, name, high, low, r) in enumerate(jobs):
                    dve.wait_ge(s0["split_h"], n + 1)
                    if name == "qk":
                        tl, tr, th = (w.rearrange("p (a k n) -> p a k n", k=2, n=2 * P) for w in (low, raw, high))
                        for k, factor in ((0, SCALE), (1, 1.0)):
                            ins = nc.vector.scalar_tensor_tensor(tl[:, :, k, :], tr[:, :, k, :], factor, th[:, :, k, :].bitcast(F32),
                                                                 ALU.mult, ALU.subtract)
                    else:
                        wait_passed(dve, r)
                        ins = nc.vector.tensor_tensor(low, raw, high.bitcast(F32), ALU.subtract)
                    ins.then_inc(s0["split_l"], 1)
                    if n == 0:
                        dve.wait_ge(s0["once_in"], 16)
                        for t, name in ((ident_r, "eye"), (mask_r, "mask"), (pick_r, "pick"), (sel_r, "sel"), (gate_h, "gate")):
                            nc.vector.tensor_copy(t[:, :], on(name))
                        nc.vector.tensor_copy(wr_h[:, :], on("wr")).then_inc(s0["once_in"], 1)
                        dve.wait_ge(s0["once_in"], 17)
                        nc.vector.tensor_tensor(gate_l[:, :], on("gate"), gate_h[:, :].bitcast(F32), ALU.subtract)
                        nc.vector.tensor_tensor(wr_l[:, :], on("wr"), wr_h[:, :].bitcast(F32), ALU.subtract)
                        dve.wait_ge(s0["small_in_"], 16)
                        bq = sm("bqk").rearrange("p (a k) -> p a k", k=4)[:, :, 0:2]
                        nc.vector.tensor_scalar(bq, bq, SCALE, None, ALU.mult)

            @block.gpsimd
            def _(pool):
                nc.gpsimd.memset(half_neg[:, :], -0.5)

        names = """x_in_ wv_in x_out out_done pow_ask pow_done xn_ready_a xn_turned_a xT_h_done_a xT_l_done_a y_copied_a y_turned_a
            xn_ready_b xn_turned_b xT_h_done_b xT_l_done_b y_copied_b y_turned_b
            dve_seq act_seq wqk0 wqk1 wg_low_in wu_low_in wd_in_ v_made v_kept proj_made rope_terms rope_sum
            s_made max_done exp_done rinv_done norm_done pt_made pt_kept pv_made o_h_done o_l_done wo_made
            x0_used lg_made lg_exp comb_turned comb_ask combT_done g_made u_made silu_done u_kept act1_done c_made hid_done down_made
            xz_made xin_done sz_done conv_done u_done xp_made bc_done dt_made xs_done sp_exp sp_w1 sp_ln delta_done
            spread_made spread_kept dA_done dBu_done scan_done hc_done y_made y1_done y2_done out_made
            l2_made l2_exp l2_ask p2_ask p2_turned pT2_done up2_made relu_done p2_made h2_done down2_made""".split()
        sem = {n: ctx.enter_context(nc.semaphore(n)) for n in names}
        first, last_sem = sem[names[0]], sem[names[-1]]
        NU = NI * DS
        SPREAD, DECAY, SCAN, READ, SUM = 7, 8, 9, 10, 11
        SUMMED = 42
        LC, LD = 5, 6
        B0 = 3
        NEXT = 31
        WCH = 11

        def turn(A, B, out_dst, x_src=None, x_next=None):
            def rope_bank(n):
                return bk[(2, 3, 4, 1, 4, 2, 3, 6)[n]] if n < 8 else bk[4]

            def value_bank(n):
                return bk[(0, 6, 2, 3)[n % 4]]

            def score_bank(n, qb):
                return bk[(3 * n + (0, 0, 1, 2)[qb]) % 2], P if qb == 1 else 0

            with nc.Block() as block:
                @block.sync
                def _(sp):
                    if A:
                        if x_src is not None:
                            sp.dma_start(x0[:, :, :], x_src.rearrange("o (t p) d -> (o p) t d", p=P)).then_inc(sem["x_in_"], 16)
                        for p in range(NP):
                            if p >= 2:
                                sp.wait_ge(sem["proj_made"], 4 * (p - 1))
                            sp.dma_start(wqk[:, p % 2, :, :].bitcast(F32), wqk_split[p]).then_inc(sem[f"wqk{p % 2}"], 16)

                        def load_wu(c):
                            w = slice(c * WUCH * P, min((c + 1) * WUCH, NJ) * P)
                            if c >= 2:
                                sp.wait_ge(sem["u_made"], WUCH * (c - 1))
                            sp.dma_start(wu_l[:, c % 2, 0:w.stop - w.start].bitcast(F32), wu_low[:, w]).then_inc(sem["wu_low_in"], 16)

                        sp.wait_ge(sem["proj_made"], 4 * NP)
                        if x_src is not None:
                            wait_stored(sp, NQK + 2)
                            wait_stored(sp, NQK + 3)
                        load_wu(0)
                        sp.wait_ge(sem["pv_made"], NP)
                        sp.wait_ge(sem["wo_made"], NP)
                        for c in range(NJ // WCH):
                            w = slice(c * WCH * P, (c + 1) * WCH * P)
                            sp.dma_start(wg_l[:, w].bitcast(F32), wg_low[:, w]).then_inc(sem["wg_low_in"], 16)
                            sp.wait_ge(sem["wg_low_in"], 16 * (c + 1))
                            sp.dma_start(wd[:, c * WCH:(c + 1) * WCH, :].rearrange(flat), wd_in[:, w]).then_inc(sem["wd_in_"], 16)
                            sp.wait_ge(sem["wd_in_"], 16 * (c + 1))
                            if c == 0:
                                sp.wait_ge(sem["wu_low_in"], 16)
                                load_wu(1)
                                if x_next is not None:
                                    if x_src is not None:
                                        sp.wait_ge(sem["x_in_"], 16)
                                    sp.wait_ge(sem["x0_used"], 1)
                                    sp.dma_start(x0[:, :, :], x_next.rearrange("o (t p) d -> (o p) t d", p=P)).then_inc(sem["x_in_"], 16)
                        for c in range(2, -(-NJ // WUCH)):
                            sp.wait_ge(sem["wu_low_in"], 16 * c)
                            load_wu(c)
                    if B:
                        sp.wait_ge(sem["x_out"], 1)
                        sp.dma_start(out_dst.rearrange("o (t p) d -> (o p) t d", p=P), xB[:, :, :]).then_inc(sem["out_done"], 16)
                        sp.wait_ge(sem["out_done"], 16)

                @block.tensor
                def _(pe):
                    mm = nc.tensor.matmul

                    def mm3(o, wh, wl, mh, ml, start=True, stop=True):
                        mm(o, wh, mh, start=start, stop=False)
                        mm(o, wh, ml, start=False, stop=False)
                        return mm(o, wl, mh, start=False, stop=stop)

                    def turn_xn(L, k):
                        if L is laneA and x_src is None:
                            k -= 1
                        if k >= 0:
                            pe.wait_ge(sem["xn_ready_" + L.name], k + 1)
                        for t in range(NT):
                            last = nc.tensor.transpose(L.bank[:, t * P:(t + 1) * P], L.xn[:, t, :], ident)
                        last.then_inc(sem["xn_turned_" + L.name], 1)

                    def turn_y(L, k):
                        if k:
                            pe.wait_ge(sem["y_copied_" + L.name], k)
                        for t in range(NT):
                            last = nc.tensor.transpose(L.bank[:, t * P:(t + 1) * P], L.yT[:, t * P:(t + 1) * P], ident)
                        last.then_inc(sem["y_turned_" + L.name], 1)

                    def wait_xT(L, k):
                        pe.wait_ge(sem["xT_h_done_" + L.name], k + 1)
                        pe.wait_ge(sem["xT_l_done_" + L.name], k + 1)

                    def xz(i):
                        if i == 0:
                            wait_xT(laneB, 0)
                        if i >= NI:
                            pe.wait_ge(sem["xin_done"], i - NI + 1)
                        c = slice(i * P, (i + 1) * P)
                        mm3(bk[(7, 5)[i % NI]][:, :], win_h[:, c], win_l[:, c], laneB.xT_h[:, :], laneB.xT_l[:, :])\
                            .then_inc(sem["xz_made"], 1)

                    def xproj():
                        wx = sm("wx").rearrange("p (i n) -> p i n", n=64)
                        pe.wait_ge(sem["sz_done"], 1)
                        pe.wait_ge(sem["u_done"], NI)
                        for i in range(NI):
                            last = mm(bk[7][0:64, :], wx[:, i, :], u[:, i, :], start=(i == 0), stop=(i == NI - 1))
                        last.then_inc(sem["xp_made"], 1)

                    def spread_row(row):
                        return mm(bk[5][:, :], pick_r[:, row:row + 1].broadcast_to([P, P]), bc_r[:, :], start=True, stop=True)

                    def spread_dt():
                        pe.wait_ge(sem["sz_done"], NI)
                        pe.wait_ge(sem["bc_done"], 2)
                        spread_row(2 * DS).then_inc(sem["dt_made"], 1)

                    def spread(m):
                        if m == 0:
                            pe.wait_ge(sem["xs_done"], NI)
                        else:
                            pe.wait_ge(sem["spread_kept"], m)
                        spread_row(m // 2 + (DS if m % 2 else 0)).then_inc(sem["spread_made"], 1)

                    def sum_states(s):
                        pe.wait_ge(sem["hc_done"], NI * s + 1)
                        mm(bk[7][:, :], ident, hc[:, 0, :], start=(s == 0), stop=(s == DS - 1)).then_inc(sem["y_made"], 1)

                    def slot(k):
                        if not B:
                            return
                        if k == 0:
                            xproj()
                        if k == 2:
                            spread_dt()
                        if k == SUMMED + 1:
                            out_proj()
                        if k == SUMMED + 3:
                            turn_y(laneB, 1)
                        if 0 <= k - SUM < NU and (k - SUM) % NI == 0:
                            sum_states((k - SUM) // NI)
                        if 0 <= k - SPREAD < NU:
                            spread(k - SPREAD)

                    def out_proj():
                        pe.wait_ge(sem["y2_done"], NI)
                        pe.wait_ge(sem["spread_kept"], NU)
                        wout = sm("wout").rearrange("p (i n) -> p i n", n=D)
                        for i in range(NI):
                            last = mm(bk[5][:, :], wout[:, i, :], ca[:, i, :], start=(i == 0), stop=(i == NI - 1))
                        last.then_inc(sem["out_made"], 1)

                    def logits2():
                        wait_xT(laneB, 1)
                        for t in range(NT):
                            tt = slice(t * P, (t + 1) * P)
                            last = mm3(bk[5][:, t * E2:(t + 1) * E2], laneB.xT_h[:, tt], laneB.xT_l[:, tt], wr_h[:, :], wr_l[:, :])
                        last.then_inc(sem["l2_made"], 1)

                    def turn_p2():
                        pe.wait_ge(sem["p2_ask"], 1)
                        for t in range(NT):
                            last = nc.tensor.transpose(bk[5][0:E2, t * P:(t + 1) * P], pr2[:, t, :], ident)
                        last.then_inc(sem["p2_turned"], 1)

                    def up2(j):
                        c = slice(j * P, (j + 1) * P)
                        if j == 0:
                            wait_xT(laneB, 1)
                        else:
                            pe.wait_ge(sem["relu_done"], j)
                        mm3(bk[3][:, :], w1_h[:, c], w1_l[:, c], laneB.xT_h[:, :], laneB.xT_l[:, :]).then_inc(sem["up2_made"], 1)
                        if j:
                            pe.wait_ge(sem["pT2_done"], 1)
                            if j >= 2:
                                pe.wait_ge(sem["h2_done"], j)
                            mm(bk[5][:, :], sel_r[0:E2, (j - 1) * P:j * P], pT2[0:E2, :], start=True, stop=True)\
                                .then_inc(sem["p2_made"], 1)

                    def down2(j):
                        pe.wait_ge(sem["h2_done"], j + 1)
                        k = P if j else 64
                        mm(bk[7][:, :], w2[0:k, j, :], h2[0:k, j % 2, :], start=(j == 0), stop=(j == NJ2 - 1))\
                            .then_inc(sem["down2_made"], 1)

                    def step_b(t):
                        if not B:
                            return
                        if t == 6:
                            down2(0)
                        if t == 7:
                            turn_p2()
                        for j in range(1, NJ2):
                            if t == 6 + 3 * j:
                                up2(j)
                            if t == 8 + 3 * j:
                                down2(j)
                        if t == 22:
                            turn_y(laneB, 2)

                    def values(n):
                        t, hf = divmod(n, 2)
                        if n in (2, 3):
                            pe.wait_ge(sem["rope_terms"], n - 1)
                        if n >= 4:
                            pe.wait_ge(sem["v_kept"], n - 3)
                        tt, cc = slice(t * P, (t + 1) * P), slice(hf * 512, hf * 512 + 512)
                        mm3(value_bank(n)[:, :], laneA.xT_h[:, tt], laneA.xT_l[:, tt], wv_h[:, cc], wv_l[:, cc]).then_inc(sem["v_made"], 1)

                    def project(p, kind):
                        n = 4 * p + kind
                        if kind == 0:
                            pe.wait_ge(sem[f"wqk{p % 2}"], 16 * (p // 2 + 1))
                        if n >= 4:
                            pe.wait_ge(sem["rope_terms"], n if n >= 8 else 4)
                        c = slice(kind * P, kind * P + P)
                        mm3(rope_bank(n)[:, :], wqk[:, p % 2, 0, c], wqk[:, p % 2, 1, c], laneA.xT_h[:, :], laneA.xT_l[:, :])\
                            .then_inc(sem["proj_made"], 1)

                    def scores(n, qb):
                        p, r = n // 2, slice(DK * (n % 2), DK * (n % 2) + DK)
                        un = 4 * n + qb
                        if qb == 0:
                            pe.wait_ge(sem["rope_sum"], 2 * p + 2)
                        read = {0: un - 1, 1: 0, 2: un - 2, 3: un - 1}[qb] if n or qb == 3 else 0
                        if read:
                            pe.wait_ge(sem["exp_done"], read)
                        rows, N = slice(qb * P, (qb + 1) * P), P * (qb + 1)
                        o, c0 = score_bank(n, qb)
                        o = o[:, c0:c0 + N]
                        mm(o, q_rot[r, p % 2, rows], k_rot[r, p % 2, 0:N], start=True, stop=False)
                        mm(o[:, qb * P:N], ident_r[:, :], mask_r[:, :], start=False, stop=True).then_inc(sem["s_made"], 1)

                    def turn_probs(n, g):
                        if g == 0:
                            pe.wait_ge(sem["norm_done"], 4 * (n + 1))
                        if n or g == 2:
                            pe.wait_ge(sem["pt_kept"], 3 * n + g - 1)
                        elif g == 0:
                            pe.wait_ge(sem["rope_terms"], 7)
                        o = bk[2 + (3 * n + g) % 2]
                        at = 0
                        for kb in ((0,), (1, 3), (2,))[g]:
                            for qb in range(kb, NT):
                                a = PROB_OFF[qb] + kb * P
                                last = nc.tensor.transpose(o[:, at:at + P], prob[:, n % 2, a:a + P], ident)
                                at += P
                        last.then_inc(sem["pt_made"], 1)

                    def weigh(p, terms):
                        pe.wait_ge(sem["pt_kept"], 6 * (p + 1))
                        pe.wait_ge(sem["rope_terms"], terms)
                        if p:
                            pe.wait_ge(sem["o_h_done"], p)
                            pe.wait_ge(sem["o_l_done"], p)
                        for kb in range(NT):
                            N = S - kb * P
                            for j in range(2):
                                n = 2 * p + j
                                last = mm(bk[4][DK * j:DK * j + DK, kb * P:S], v[:, kb, n * DK:n * DK + DK],
                                          probT[:, j, PART_OFF[kb]:PART_OFF[kb] + N], start=(kb == 0), stop=(kb == NT - 1),
                                          skip_group_check=True)
                        last.then_inc(sem["pv_made"], 1)

                    def project_out(p):
                        pe.wait_ge(sem["o_h_done"], p + 1)
                        pe.wait_ge(sem["o_l_done"], p + 1)
                        last = mm3(bk[6][:, :], wo_h[:, p, :], wo_l[:, p, :], o_h, o_l, start=(p == 0), stop=(p == NP - 1))
                        last.then_inc(sem["wo_made"], 1)

                    def begin_a():
                        pe.wait_ge(sem["v_kept"], 2 * NT)
                        for qb in range(3):
                            scores(0, qb)
                        for kind in range(4):
                            project(1, kind)
                        scores(0, 3)

                    def head(n):
                        pp = (n + 3) // 2
                        more = n % 2 == 1 and pp < NP
                        if n + 1 < H:
                            for qb in range(3):
                                scores(n + 1, qb)
                        if more:
                            if n > 1:
                                pe.wait_ge(sem["o_h_done"], n // 2)
                                pe.wait_ge(sem["o_l_done"], n // 2)
                            project(pp, 0)
                        slot(3 * n)
                        if n % 2 == 0 and n:
                            weigh(n // 2 - 1, 4 * min(NP, n // 2 + 2))
                        if n + 1 < H:
                            scores(n + 1, 3)
                        if more:
                            project(pp, 1)
                        turn_probs(n, 0)
                        turn_probs(n, 1)
                        slot(3 * n + 1)
                        turn_probs(n, 2)
                        if more:
                            project(pp, 2)
                        slot(3 * n + 2)
                        if more:
                            project(pp, 3)
                        if n % 2 == 0 and n:
                            project_out(n // 2 - 1)

                    def expert_logits():
                        wait_xT(laneA, 1)
                        for t in range(NT):
                            tt = slice(t * P, (t + 1) * P)
                            last = mm3(bk[4][:, t * E:(t + 1) * E], laneA.xT_h[:, tt], laneA.xT_l[:, tt], gate_h[:, :], gate_l[:, :])
                        last.then_inc(sem["lg_made"], 1)

                    def down(j):
                        if j:
                            pe.wait_ge(sem["hid_done"], j)
                        else:
                            pe.wait_ge(sem["act1_done"], 1)
                        if j % WCH == 0:
                            pe.wait_ge(sem["wd_in_"], 16 * (j // WCH + 1))
                        mm(bk[6][:, :], wd[:, j, :], hid[:, j % NHID, :], start=(j == 0), stop=(j == NJ - 1)).then_inc(sem["down_made"], 1)

                    def gate_up(j):
                        c = slice(j * P, (j + 1) * P)
                        if j >= 2:
                            pe.wait_ge(sem["silu_done"], j - 1)
                        if j % WCH == 0:
                            pe.wait_ge(sem["wg_low_in"], 16 * (j // WCH + 1))
                        mm3(bk[j % 2][:, :], wg_h[:, c], wg_l[:, c], laneA.xT_h[:, :], laneA.xT_l[:, :]).then_inc(sem["g_made"], 1)
                        if j:
                            pe.wait_ge(sem["u_kept"], j)
                        if j % WUCH == 0:
                            pe.wait_ge(sem["wu_low_in"], 16 * (j // WUCH + 1))
                        lo = slice(j % WUCH * P, (j % WUCH + 1) * P)
                        mm3(bk[2][:, :], wu_h[:, c], wu_l[:, j // WUCH % 2, lo], laneA.xT_h[:, :], laneA.xT_l[:, :]).then_inc(sem["u_made"], 1)

                    def weights(j):
                        if j == 1:
                            pe.wait_ge(sem["comb_ask"], 1)
                            for t in range(NT):
                                last = nc.tensor.transpose(bk[4][:, t * P:(t + 1) * P], cs[:, t, :], ident)
                            last.then_inc(sem["comb_turned"], 1)
                            pe.wait_ge(sem["combT_done"], 1)
                        else:
                            pe.wait_ge(sem["hid_done"], j - 1)
                        g, el = divmod(2 * (j - 1), 16)
                        rows = slice(32 * g, 32 * g + 32)
                        mm(bk[4][:, :], sel_r[rows, 64 * el:64 * el + P], combT[rows, :], start=True, stop=True,
                           tile_position=(32 * g, 0)).then_inc(sem["c_made"], 1)

                    def experts(t):
                        if t < NJ:
                            gate_up(t)
                        if 1 <= t - LC < NJ:
                            weights(t - LC)
                        if 0 <= t - LD < NJ:
                            down(t - LD)

                    if B:
                        turn_y(laneB, 0)
                    if A:
                        turn_xn(laneA, 0)
                        wait_xT(laneA, 0)
                        for kind in range(4):
                            project(0, kind)
                        for n in range(4):
                            values(n)
                    if B:
                        turn_xn(laneB, 0)
                    if A:
                        for n in range(4, 2 * NT):
                            values(n)
                    if B:
                        for i in range(2 * NI):
                            xz(i)
                    if A:
                        begin_a()
                    for n in range(H):
                        if A:
                            head(n)
                        else:
                            for k in range(3 * n, 3 * n + 3):
                                slot(k)
                    if A:
                        weigh(NP - 1, 4 * NP)
                        project_out(NP - 1)
                        turn_y(laneA, 1)
                    if B:
                        turn_xn(laneB, 1)
                        logits2()
                        up2(0)
                    if A:
                        turn_xn(laneA, 1)
                        expert_logits()
                    for j in range(NJ + LD):
                        if A:
                            experts(j)
                        step_b(j - B0)

                @block.scalar
                def _(act):
                    ac = nc.scalar.activation

                    def keep_xT(L, k):
                        act.wait_ge(sem["xn_turned_" + L.name], k + 1)
                        ac(L.xT_h[:, :], L.bank[:, :], ACT.Copy).then_inc(sem["xT_h_done_" + L.name], 1)

                    def keep_xin():
                        for i in range(NI):
                            act.wait_ge(sem["xz_made"], i + 1)
                            ac(xin[:, i, DC - 1:], bk[(7, 5)[i]][:, :], ACT.Copy).then_inc(sem["xin_done"], 1)

                    def silus():
                        for i in range(NI):
                            act.wait_ge(sem["xz_made"], NI + i + 1)
                            ac(sz[:, i, :], bk[(7, 5)[i]][:, :], ACT.Silu).then_inc(sem["sz_done"], 1)
                        for i in range(NI):
                            act.wait_ge(sem["conv_done"], i + 1)
                            ac(u[:, i, :], cb[:, i, :], ACT.Silu, bias=sm("convb")[:, i:i + 1]).then_inc(sem["u_done"], 1)

                    def slot(k):
                        if not B:
                            return
                        if k == 3:
                            act.wait_ge(sem["xs_done"], NI)
                            ac(ca, xs, ACT.Abs).then_inc(sem["act_seq"], 1)
                            act.wait_ge(sem["act_seq"], 1)
                            ac(cb, ca, ACT.Exp, scale=-1.0).then_inc(sem["sp_exp"], 1)
                        if k == 5:
                            act.wait_ge(sem["sp_w1"], 1)
                            ac(delta, ca, ACT.Ln).then_inc(sem["sp_ln"], 1)
                        if k == SUMMED + 2:
                            act.wait_ge(sem["out_made"], 1)
                            ac(laneB.yT, bk[5][:, :], ACT.Copy).then_inc(sem["y_copied_b"], 1)
                        m = k - SPREAD
                        if 0 <= m < NU:
                            s = m // 2
                            act.wait_ge(sem["spread_made"], m + 1)
                            if m % 2 == 0:
                                if s >= 2:
                                    act.wait_ge(sem["dBu_done"], NI * (s - 1))
                                if s == 0:
                                    act.wait_ge(sem["conv_done"], NI)
                                dst = Bs
                            else:
                                if s >= 2:
                                    act.wait_ge(sem["hc_done"], NI * (s - 1))
                                dst = Cs
                            ac(dst[:, s % 2, :], bk[5][:, :], ACT.Copy).then_inc(sem["spread_kept"], 1)
                        m = k - DECAY
                        if 0 <= m < NU:
                            s, i = divmod(m, NI)
                            if m == 0:
                                act.wait_ge(sem["delta_done"], 1)
                            if m >= 2:
                                act.wait_ge(sem["scan_done"], m - 1)
                            ac(dA[:, m % 2, :], delta[:, i, :], ACT.Exp, scale=negA[:, i * DS + s:i * DS + s + 1])\
                                .then_inc(sem["dA_done"], 1)

                    def step_b(t):
                        if not B:
                            return
                        if t == 5:
                            act.wait_ge(sem["l2_ask"], 1)
                            ac(gate2, e2, ACT.Exp).then_inc(sem["l2_exp"], 1)
                        for j in range(NJ2):
                            if t == (6 + 3 * j if j else 4):
                                act.wait_ge(sem["up2_made"], j + 1)
                                if j >= 2:
                                    act.wait_ge(sem["h2_done"], j - 1)
                                ac(r2[:, j % 2, :], bk[3][:, :], ACT.Relu).then_inc(sem["relu_done"], 1)
                        if t == 21:
                            act.wait_ge(sem["down2_made"], NJ2)
                            ac(laneB.yT, bk[7][:, :], ACT.Copy).then_inc(sem["y_copied_b"], 1)

                    def keep_v(n):
                        act.wait_ge(sem["v_made"], n + 1)
                        ac(v[:, n // 2, n % 2 * 512:n % 2 * 512 + 512], value_bank(n)[:, :], ACT.Copy).then_inc(sem["v_kept"], 1)

                    def exps(n, qbs):
                        for qb in qbs:
                            un = 4 * n + qb
                            N = P * (qb + 1)
                            if qb == 0 and n >= 2:
                                act.wait_ge(sem["pt_made"], 3 * (n - 1))
                                act.wait_ge(sem["rinv_done"], n - 1)
                            act.wait_ge(sem["max_done"], un + (2 if qb == 0 else 1))
                            o, c0 = score_bank(n, qb)
                            ac(prob[:, n % 2, PROB_OFF[qb]:PROB_OFF[qb] + N], o[:, c0:c0 + N], ACT.Exp,
                               bias=nmax[:, un % 8:un % 8 + 1], accum_out=rsum[:, un % 8:un % 8 + 1]).then_inc(sem["exp_done"], 1)

                    def keep_turned(n, g):
                        if n >= 2 and g == 0:
                            act.wait_ge(sem["pv_made"], n // 2)
                        act.wait_ge(sem["pt_made"], 3 * n + g + 1)
                        N = 512 if g < 2 else 256
                        ac(probT[:, n % 2, 512 * g:512 * g + N], bk[2 + (3 * n + g) % 2][:, 0:N], ACT.Copy).then_inc(sem["pt_kept"], 1)

                    def keep_o(p):
                        if p:
                            act.wait_ge(sem["wo_made"], p)
                        elif x_src is not None:
                            wait_stored(act, NQK + 2)
                        act.wait_ge(sem["pv_made"], p + 1)
                        ac(o_h, bk[4][:, :], ACT.Identity, bias=sm("bv")[:, p:p + 1]).then_inc(sem["o_h_done"], 1)

                    def head(n):
                        if n + 1 < H:
                            exps(n + 1, (0, 1, 2))
                        slot(3 * n)
                        if n % 2 == 0 and n:
                            keep_o(n // 2 - 1)
                        if n + 1 < H:
                            exps(n + 1, (3,))
                        keep_turned(n, 0)
                        keep_turned(n, 1)
                        slot(3 * n + 1)
                        keep_turned(n, 2)
                        slot(3 * n + 2)

                    if A:
                        keep_xT(laneA, 0)
                        for n in range(4):
                            keep_v(n)
                    if B:
                        keep_xT(laneB, 0)
                    if A:
                        for n in range(4, 2 * NT):
                            keep_v(n)
                    if B:
                        keep_xin()
                        silus()
                    if A:
                        exps(0, range(NT))
                    for n in range(H):
                        if A:
                            head(n)
                        else:
                            for k in range(3 * n, 3 * n + 3):
                                slot(k)
                    if A:
                        keep_o(NP - 1)
                    if A:
                        act.wait_ge(sem["wo_made"], NP)
                        ac(laneA.yT, bk[6][:, :], ACT.Identity, bias=sm("bo")).then_inc(sem["y_copied_a"], 1)
                    if B:
                        keep_xT(laneB, 1)
                    if A:
                        keep_xT(laneA, 1)
                        act.wait_ge(sem["lg_made"], 1)
                        ac(sc.rearrange(flat), bk[4][:, 0:NT * E], ACT.Exp, scale=-1.0).then_inc(sem["lg_exp"], 1)
                    for j in range(NJ + LD):
                        if A and j < NJ:
                            if j >= 2:
                                act.wait_ge(sem["act1_done"], j - 1)
                            act.wait_ge(sem["g_made"], j + 1)
                            ac(sg[:, j % 2, :], bk[j % 2][:, :], ACT.Silu).then_inc(sem["silu_done"], 1)
                            if j >= 1:
                                act.wait_ge(sem["act1_done"], j)
                            act.wait_ge(sem["u_made"], j + 1)
                            ac(su, bk[2][:, :], ACT.Copy).then_inc(sem["u_kept"], 1)
                        step_b(j - B0)
                    if A:
                        act.wait_ge(sem["down_made"], NJ)
                        if B:
                            act.wait_ge(sem["x_out"], 1)
                        ac(laneB.yT, bk[6][:, :], ACT.Copy).then_inc(sem["y_copied_a"], 1)

                @block.vector
                def _(dve):
                    V = nc.vector
                    seq = [0]

                    def link(ins):
                        seq[0] += 1
                        ins.then_inc(sem["dve_seq"], 1)
                        dve.wait_ge(sem["dve_seq"], seq[0])

                    asked = [0]

                    def ask_norm(L, rows):
                        for t in range(NT):
                            ins = V.bn_stats(L.stats[:, t, :], rows(t))
                        link(ins)
                        for t in range(NT):
                            ins = V.bn_aggr(L.mv[:, t, :], L.stats[:, t, :])
                        link(ins)
                        V.tensor_scalar(L.ve[:, :], L.mv[:, :, 1], EPS, None, ALU.add).then_inc(sem["pow_ask"], 1)
                        asked[0] += 1
                        return asked[0]

                    def ask_x(L, x):
                        return ask_norm(L, lambda t: x[:, t, :])

                    def norm_x(L, x, turn):
                        dve.wait_ge(sem["pow_done"], turn)
                        for t in range(NT):
                            ins = V.tensor_scalar(L.xn[:, t, :], x[:, t, :], L.mv[:, t, 0:1], L.rstd[:, t:t + 1], ALU.subtract, ALU.mult)
                        ins.then_inc(sem["xn_ready_" + L.name], 1)

                    def keep_xT(L, k):
                        dve.wait_ge(sem["xT_h_done_" + L.name], k + 1)
                        V.tensor_tensor(L.xT_l[:, :], L.bank[:, :], L.xT_h[:, :].bitcast(F32), ALU.subtract)\
                            .then_inc(sem["xT_l_done_" + L.name], 1)

                    def ask_y(L, k):
                        dve.wait_ge(sem["y_turned_" + L.name], k + 1)
                        return ask_norm(L, lambda t: L.bank[:, t * P:(t + 1) * P])

                    def add_y(L, dst, src, turn):
                        dve.wait_ge(sem["pow_done"], turn)
                        for t in range(NT):
                            ins = V.tensor_scalar(L.xn[:, t, :], L.bank[:, t * P:(t + 1) * P], L.mv[:, t, 0:1], L.rstd[:, t:t + 1],
                                                  ALU.subtract, ALU.mult)
                        link(ins)
                        return V.tensor_tensor(dst[:, :, :], src[:, :, :], L.xn[:, :, :], ALU.add)

                    b_turn = [0]
                    cw = sm("convw").rearrange("p (i c) -> p i c", c=DC)

                    def conv(c):
                        if c == 0:
                            dve.wait_ge(sem["xin_done"], NI)
                        src, dst = (ca, cb) if c % 2 else (cb, ca)
                        for i in range(NI):
                            if c == 0:
                                ins = V.tensor_scalar(ca[:, i, :], xin[:, i, 0:S], cw[:, i, 0:1], None, ALU.mult)
                            else:
                                ins = V.scalar_tensor_tensor(dst[:, i, :], xin[:, i, c:c + S], cw[:, i, c:c + 1], src[:, i, :],
                                                             ALU.mult, ALU.add)
                            if c == DC - 1:
                                ins.then_inc(sem["conv_done"], 1)
                        if c < DC - 1:
                            link(ins)

                    def slot(k):
                        if not B:
                            return
                        if k == 1:
                            dve.wait_ge(sem["xp_made"], 1)
                            V.tensor_copy(bc_r[0:64, :], bk[7][0:64, :]).then_inc(sem["bc_done"], 1)
                            dve.wait_ge(sem["bc_done"], 1)
                            V.tensor_tensor(bc_r[64:128, :], bk[7][0:64, :], bc_r[0:64, :].bitcast(F32), ALU.subtract).then_inc(sem["bc_done"], 1)
                        if k == 2:
                            dve.wait_ge(sem["dt_made"], 1)
                            for i in range(NI):
                                V.tensor_scalar(xs[:, i, :], bk[5][:, :], sm("wdt")[:, i:i + 1], sm("bdt")[:, i:i + 1], ALU.mult, ALU.add)\
                                 .then_inc(sem["xs_done"], 1)
                        if k == 4:
                            dve.wait_ge(sem["sp_exp"], 1)
                            V.tensor_scalar(ca, cb, 1.0, None, ALU.add).then_inc(sem["sp_w1"], 1)
                            dve.wait_ge(sem["sp_w1"], 1)
                            link(V.scalar_tensor_tensor(cb, ca, 1.0, cb, ALU.subtract, ALU.subtract))
                        if k == 6:
                            dve.wait_ge(sem["sp_ln"], 1)
                            link(V.tensor_tensor(delta, delta, cb, ALU.subtract))
                            link(V.scalar_tensor_tensor(delta, xs, 0.0, delta, ALU.max, ALU.add))
                            V.tensor_tensor(du, delta, u, ALU.mult).then_inc(sem["delta_done"], 1)
                        m = k - SCAN
                        if 0 <= m < NU:
                            dve.wait_ge(sem["dA_done"], m + 1)
                            dve.wait_ge(sem["dBu_done"], m + 1)
                            if m >= 2:
                                dve.wait_ge(sem["hc_done"], m - 1)
                            V.tensor_tensor_scan(hs[:, m % 2, :], dA[:, m % 2, :], dBu[:, m % 2, :], 0.0, ALU.mult, ALU.add)\
                             .then_inc(sem["scan_done"], 1)
                        m = k - READ
                        if 0 <= m < NU:
                            s, i = divmod(m, NI)
                            dve.wait_ge(sem["scan_done"], m + 1)
                            dve.wait_ge(sem["spread_kept"], 2 * s + 2)
                            if s:
                                dve.wait_ge(sem["y1_done" if i else "y_made"], s)
                            V.tensor_tensor(hc[:, i, :], hs[:, m % 2, :], Cs[:, s % 2, :], ALU.mult).then_inc(sem["hc_done"], 1)
                        m = k - SUM
                        if 0 <= m < NU and m % 2:
                            s = m // 2
                            dve.wait_ge(sem["hc_done"], m + 1)
                            if s:
                                dve.wait_ge(sem["y1_done"], s)
                                V.tensor_tensor(y1, y1, hc[:, 1, :], ALU.add).then_inc(sem["y1_done"], 1)
                            else:
                                V.tensor_copy(y1, hc[:, 1, :]).then_inc(sem["y1_done"], 1)
                        if k == SUMMED:
                            gate_y()
                        if k == SUMMED + 4:
                            b_turn[0] = ask_y(laneB, 1)
                        if k == SUMMED + 5:
                            link(add_y(laneB, xB, xB, b_turn[0]))
                            b_turn[0] = ask_x(laneB, xB)

                    def gate_y():
                        dve.wait_ge(sem["y_made"], DS)
                        dve.wait_ge(sem["y1_done"], DS)
                        for i in range(NI):
                            ins = V.scalar_tensor_tensor(cb[:, i, :], u[:, i, :], sm("dskip")[:, i:i + 1], y1 if i else bk[7][:, :], ALU.mult, ALU.add)
                        link(ins)
                        dve.wait_ge(sem["sz_done"], NI)
                        for i in range(NI):
                            V.tensor_tensor(ca[:, i, :], cb[:, i, :], sz[:, i, :], ALU.mult).then_inc(sem["y2_done"], 1)

                    def hidden2(j):
                        dve.wait_ge(sem["relu_done"], j + 1)
                        if j >= 2:
                            dve.wait_ge(sem["down2_made"], j - 1)
                        r = r2[:, j % 2, :]
                        if j:
                            dve.wait_ge(sem["p2_made"], j)
                            link(V.tensor_tensor(rp2[:, j % 2, :], r, bk[5][:, :], ALU.mult))
                            V.tensor_tensor(h2[:, j % 2, :], rp2[:, j % 2, :], r, ALU.mult).then_inc(sem["h2_done"], 1)
                        else:
                            V.tensor_tensor(h2[:, 0, :], r, r, ALU.mult).then_inc(sem["h2_done"], 1)

                    def step_b(t):
                        if not B:
                            return
                        if t == 4:
                            dve.wait_ge(sem["l2_made"], 1)
                            link(V.tensor_copy(lg.rearrange(flat), bk[5][:, 0:NT * E2]))
                            for i in range(NT):
                                ins = V.max(v8[:, i, :], lg[:, i, :])
                            link(ins)
                            V.tensor_tensor(e2, v8[:, :, 1], v8[:, :, 0], ALU.subtract).then_inc(sem["l2_ask"], 1)
                        if t == 5:
                            hidden2(0)
                        if t == 6:
                            dve.wait_ge(sem["l2_exp"], 1)
                            link(V.tensor_scalar(gate2, gate2, 1.0, None, ALU.add))
                            link(V.reciprocal(gate2, gate2))
                            link(V.tensor_scalar(gate2, gate2, 1.0, None, ALU.is_ge))
                            link(V.tensor_tensor(pr2, lg, v8[:, :, 0:1].broadcast_to([P, NT, E2]), ALU.is_equal))
                            V.tensor_tensor(pr2, pr2, gate2.rearrange("p (a o) -> p a o", o=1).broadcast_to([P, NT, E2]), ALU.mult)\
                             .then_inc(sem["p2_ask"], 1)
                        if t == 8:
                            dve.wait_ge(sem["p2_turned"], 1)
                            V.tensor_copy(pT2[0:E2, :], bk[5][0:E2, :]).then_inc(sem["pT2_done"], 1)
                        for j in range(1, NJ2):
                            if t == 7 + 3 * j:
                                hidden2(j)
                        if t == 23:
                            b_turn[0] = ask_y(laneB, 2)
                        if t == 24:
                            add_y(laneB, xB, xB, b_turn[0]).then_inc(sem["x_out"], 1)

                    def rope_term(p, kind):
                        n = 4 * p + kind
                        m = n // 2
                        dve.wait_ge(sem["proj_made"], n + 1)
                        tab = sm("sin" if kind % 2 else "cos")
                        bias = sm("bqk")[:, n:n + 1]
                        if m >= 1:
                            dve.wait_ge(sem["rope_sum"], m)
                        dst = ropeB if kind % 2 else ropeA
                        V.scalar_tensor_tensor(dst, rope_bank(n)[:, :], bias, tab, ALU.add, ALU.mult).then_inc(sem["rope_terms"], 1)

                    def row_max(n, qb):
                        un = 4 * n + qb
                        dve.wait_ge(sem["s_made"], un + (2 if qb == 0 else 1))
                        o, c0 = score_bank(n, qb)
                        V.tensor_reduce(nmax[:, un % 8:un % 8 + 1], o[:, c0:c0 + P * (qb + 1)], AX.X, ALU.max, negate=True)\
                         .then_inc(sem["max_done"], 1)

                    def row_inv(n):
                        dve.wait_ge(sem["exp_done"], 4 * (n + 1))
                        if n >= 2:
                            dve.wait_ge(sem["norm_done"], 4 * (n - 1))
                        a = 4 * (n % 2)
                        V.reciprocal(rinv[:, a:a + 4], rsum[:, a:a + 4]).then_inc(sem["rinv_done"], 1)

                    def keep_o(p):
                        dve.wait_ge(sem["o_h_done"], p + 1)
                        V.scalar_tensor_tensor(o_l, bk[4][:, :], sm("bv")[:, p:p + 1], o_h.bitcast(F32), ALU.add, ALU.subtract)\
                         .then_inc(sem["o_l_done"], 1)

                    def begin_a():
                        for qb in range(3):
                            row_max(0, qb)
                        for kind in range(4):
                            rope_term(1, kind)
                        row_max(0, 3)
                        row_inv(0)

                    def head(n):
                        pp = (n + 3) // 2
                        more = n % 2 == 1 and pp < NP
                        if n + 1 < H:
                            for qb in range(3):
                                row_max(n + 1, qb)
                        if more:
                            rope_term(pp, 0)
                        slot(3 * n)
                        if n + 1 < H:
                            row_max(n + 1, 3)
                        if n % 2 == 0 and n:
                            keep_o(n // 2 - 1)
                        if more:
                            rope_term(pp, 1)
                        slot(3 * n + 1)
                        if more:
                            rope_term(pp, 2)
                        if n + 1 < H:
                            row_inv(n + 1)
                        slot(3 * n + 2)
                        if more:
                            rope_term(pp, 3)

                    def route():
                        s2 = sc.rearrange(flat)
                        V.memset(gm[:, :, G:], TOP)
                        V.memset(ms[:, :, E:], TOP)
                        dve.wait_ge(sem["lg_exp"], 1)
                        link(V.tensor_scalar(s2, s2, 1.0, None, ALU.add))
                        link(V.reciprocal(s2, s2))
                        link(V.tensor_tensor(sc, sc, sm("gbias").rearrange("p (o e) -> p o e", o=1).broadcast_to([P, NT, E]), ALU.add))
                        link(V.tensor_reduce(gm[:, :, 0:G], sc.rearrange("p a (g e) -> p a g e", e=E // G), AX.X, ALU.max))
                        for t in range(NT):
                            ins = V.max(g8[:, t, :], gm[:, t, :])
                        link(ins)
                        for t in range(NT):
                            ins = V.match_replace(gr[:, t, :], g8[:, t, :], gm[:, t, :], TAKEN)
                        link(ins)
                        link(V.tensor_scalar(gmask, gr[:, :, 0:G], TAKEN, None, ALU.is_equal))
                        for t in range(NT):
                            ins = V.tensor_tensor(ms[:, t, 0:E].rearrange("p (g e) -> p g e", e=E // G),
                                                  sc[:, t, :].rearrange("p (g e) -> p g e", e=E // G),
                                                  gmask[:, t, :].rearrange("p (g o) -> p g o", o=1).broadcast_to([P, G, E // G]), ALU.mult)
                        link(ins)
                        for t in range(NT):
                            ins = V.max(s8[:, t, :], ms[:, t, :])
                        link(ins)
                        for t in range(NT):
                            ins = V.match_replace(sr[:, t, :], s8[:, t, :], ms[:, t, :], TAKEN)
                        link(ins)
                        link(V.scalar_tensor_tensor(comb, sr[:, :, 0:E], TAKEN, ms[:, :, 0:E], ALU.is_equal, ALU.mult))
                        link(V.tensor_reduce(csum, comb, AX.X, ALU.add))
                        link(V.tensor_scalar(csum, csum, 1e-8, None, ALU.add))
                        link(V.reciprocal(csum, csum))
                        link(V.tensor_tensor(comb, comb, csum.rearrange("p (a o) -> p a o", o=1).broadcast_to([P, NT, E]), ALU.mult))
                        for t in range(NT):
                            c4 = cs[:, t, :].rearrange("p (g h e) -> p g h e", h=2, e=16)
                            ins = V.tensor_copy(c4[:, :, 0, :].bitcast(F32R), comb[:, t, :].rearrange("p (g e) -> p g e", e=16))
                        link(ins)
                        for t in range(NT):
                            c4 = cs[:, t, :].rearrange("p (g h e) -> p g h e", h=2, e=16)
                            ins = V.tensor_tensor(c4[:, :, 1, :], comb[:, t, :].rearrange("p (g e) -> p g e", e=16), c4[:, :, 0, :], ALU.subtract)
                        ins.then_inc(sem["comb_ask"], 1)

                    def weighted(j):
                        if j == 1:
                            dve.wait_ge(sem["comb_turned"], 1)
                            V.tensor_copy(combT, bk[4][:, :]).then_inc(sem["combT_done"], 1)
                        dve.wait_ge(sem["act1_done"], j + 1)
                        dve.wait_ge(sem["c_made"], j)
                        V.tensor_tensor(hid[:, j % NHID, :], hid[:, j % NHID, :], bk[4][:, :], ALU.mult).then_inc(sem["hid_done"], 1)

                    if B:
                        by = ask_y(laneB, 0)
                        V.memset(xin[:, :, 0:DC - 1], 0.0)
                    if x_src is not None:
                        dve.wait_ge(sem["x_in_"], 16)
                        norm_x(laneA, x0, ask_x(laneA, x0))
                    if A:
                        keep_xT(laneA, 0)
                    if B:
                        link(add_y(laneB, xB, xA, by))
                        bx = ask_x(laneB, xB)
                    if A:
                        rope_term(0, 0)
                        rope_term(0, 1)
                    if B:
                        norm_x(laneB, xB, bx)
                    if A:
                        rope_term(0, 2)
                        rope_term(0, 3)
                    if B:
                        keep_xT(laneB, 0)
                        for c in range(DC):
                            conv(c)
                    if A:
                        begin_a()
                    for n in range(H):
                        if A:
                            head(n)
                        else:
                            for k in range(3 * n, 3 * n + 3):
                                slot(k)
                    if A:
                        keep_o(NP - 1)
                    if B:
                        norm_x(laneB, xB, b_turn[0])
                    if A:
                        ay = ask_y(laneA, 0)
                    if B:
                        keep_xT(laneB, 1)
                    if A:
                        ins = add_y(laneA, xA, x0, ay)
                        ins.then_inc(sem["x0_used"], 1)
                        dve.wait_ge(sem["x0_used"], 1)
                        ax = ask_x(laneA, xA)
                        norm_x(laneA, xA, ax)
                        keep_xT(laneA, 1)
                    if A:
                        route()
                    for j in range(NJ + LD):
                        if A and 1 <= j - LC < NJ:
                            weighted(j - LC)
                        step_b(j - B0)
                        if x_next is not None and j == NEXT:
                            dve.wait_ge(sem["x_in_"], 32 if x_src is not None else 16)
                            ax = ask_x(laneA, x0)
                        if x_next is not None and j == NEXT + 1:
                            norm_x(laneA, x0, ax)

                @block.gpsimd
                def _(pool):
                    Q = nc.gpsimd
                    asked = [0]

                    def power(L):
                        asked[0] += 1
                        pool.wait_ge(sem["pow_ask"], asked[0])
                        Q.tensor_tensor(L.rstd[:, :], L.ve[:, :], half_neg[:, :], ALU.pow).then_inc(sem["pow_done"], 1)

                    def slot(k):
                        if B and k in (SUMMED + 4, SUMMED + 5):
                            power(laneB)
                        m = k - DECAY
                        if B and 0 <= m < NU:
                            s, i = divmod(m, NI)
                            if m == 0:
                                pool.wait_ge(sem["delta_done"], 1)
                            pool.wait_ge(sem["spread_kept"], 2 * s + 1)
                            if m >= 2:
                                pool.wait_ge(sem["scan_done"], m - 1)
                            Q.tensor_tensor(dBu[:, m % 2, :], du[:, i, :], Bs[:, s % 2, :], ALU.mult).then_inc(sem["dBu_done"], 1)

                    def rope_sum(m):
                        p = m // 2
                        pool.wait_ge(sem["rope_terms"], 2 * m + 2)
                        if p >= 2:
                            pool.wait_ge(sem["s_made"], 8 * (p - 1))
                        Q.tensor_tensor((k_rot if m % 2 else q_rot)[:, p % 2, :], ropeA, ropeB, ALU.add).then_inc(sem["rope_sum"], 1)

                    def normalise(n):
                        pool.wait_ge(sem["rinv_done"], n + 1)
                        for qb in range(NT):
                            a = prob[:, n % 2, PROB_OFF[qb]:PROB_OFF[qb] + P * (qb + 1)]
                            c = 4 * (n % 2) + qb
                            Q.tensor_scalar(a, a, rinv[:, c:c + 1], 0.0, ALU.mult, ALU.add).then_inc(sem["norm_done"], 1)

                    def begin_a():
                        rope_sum(0)
                        rope_sum(1)
                        rope_sum(2)
                        rope_sum(3)
                        normalise(0)

                    def head(n):
                        pp = (n + 3) // 2
                        slot(3 * n)
                        if n and n % 2 == 0 and n // 2 + 1 < NP:
                            rope_sum(2 * (n // 2 + 1) + 1)
                        slot(3 * n + 1)
                        if n % 2 == 1 and pp < NP:
                            rope_sum(2 * pp)
                        if n + 1 < H:
                            normalise(n + 1)
                        slot(3 * n + 2)

                    def gated(j):
                        pool.wait_ge(sem["silu_done"], j + 1)
                        pool.wait_ge(sem["u_kept"], j + 1)
                        if j >= NHID:
                            pool.wait_ge(sem["down_made"], j - NHID + 1)
                        Q.tensor_tensor(hid[:, j % NHID, :], sg[:, j % 2, :], su, ALU.mult).then_inc(sem["act1_done"], 1)

                    if B:
                        power(laneB)
                    if x_src is not None:
                        power(laneA)
                    if B:
                        power(laneB)
                    if A:
                        begin_a()
                    for n in range(H):
                        if A:
                            head(n)
                        else:
                            for k in range(3 * n, 3 * n + 3):
                                slot(k)
                    if A:
                        power(laneA)
                        power(laneA)
                    for j in range(NJ + LD):
                        if A and j < NJ:
                            gated(j)
                        if B and j == B0 + 23:
                            power(laneB)
                        if x_next is not None and j == NEXT:
                            power(laneA)
            nc.all_engine_barrier(sems_to_clear=range(first.num, last_sem.num + 1))

        turn(True, False, None, x_src=x_in[0:1], x_next=x_in[1:2])
        with nc.Fori(0, NB - 2) as b:
            turn(True, True, out[0:NB - 2][bass.ds(b, 1)], x_next=x_in[2:NB][bass.ds(b, 1)])
        turn(True, True, out[NB - 2:NB - 1])
        turn(False, True, out[NB - 1:NB])


def kernel(**inputs):
    import numpy as np
    import concourse.bacc as bacc
    from concourse.bass_utils import run_bass_kernel_spmd as run

    a = {k: np.asarray(t) for k, t in inputs.items()}
    f32 = np.float32

    half = DK // 2
    theta = (f32(10000.0) ** (np.arange(0, DK, 2, dtype=f32) / f32(DK))).astype(f32)
    freqs = (np.arange(S, dtype=f32)[:, None] * (f32(1.0) / theta)[None, :]).astype(f32)
    emb = np.concatenate([freqs, freqs], axis=-1).T
    sign = np.where(np.arange(DK) % 2 == 0, f32(-1), f32(1))[:, None]
    cos, sin = np.tile(np.cos(emb), (2, 1)), np.tile(np.sin(emb) * sign, (2, 1))
    r = np.arange(P)
    sel = (np.arange(1024)[None, :] // 64 == (r % 16)[:, None]).astype(f32)
    small = {
        "eye": np.eye(P, dtype=f32), "mask": np.where(r[None, :] > r[:, None], f32(MASKED), f32(0)),
        "cos": cos, "sin": sin, "sel": sel,
        "pick": ((r % 64)[:, None] == np.arange(33)[None, :]).astype(f32),
    }

    swap = np.arange(H * DK) ^ 1

    def by_pair(w):
        return w.T.reshape(D, NP, P)

    wq, wk, bq, bk_ = a["L0_attn_wq"], a["L0_attn_wk"], a["L0_attn_bq"], a["L0_attn_bk"]
    wqk = np.stack([by_pair(w) for w in (wq, wq[swap], wk, wk[swap])], axis=2).reshape(D, NP * 4 * P)
    small["bqk"] = np.stack([t.reshape(NP, P).T for t in (bq, bq[swap], bk_, bk_[swap])], axis=2)
    small["bv"] = a["L0_attn_bv"].reshape(NP, P).T
    small["bo"] = a["L0_attn_bo"].reshape(D, 1)
    small["gbias"] = np.broadcast_to(a["L0_ffn_gate_bias"], (P, E))
    small["convw"] = a["L1_attn_conv_w"].reshape(NI, P, DC).transpose(1, 0, 2)
    small["convb"] = a["L1_attn_conv_b"].reshape(NI, P).T
    wx = a["L1_attn_W_xproj"]
    wx = np.concatenate([wx[1:], wx[:1], np.zeros((31, DI), f32)], axis=0)
    small["wx"] = wx.T.reshape(NI, P, 64).transpose(1, 0, 2)
    small["wdt"] = a["L1_attn_W_dt"].reshape(NI, P).T
    small["bdt"] = a["L1_attn_b_dt"].reshape(NI, P).T
    small["alog"] = a["L1_attn_A_log"].reshape(NI, P, DS).transpose(1, 0, 2)
    small["dskip"] = a["L1_attn_D"].reshape(NI, P).T
    small["wout"] = a["L1_attn_W_out"].T.reshape(NI, P, D).transpose(1, 0, 2)
    small["gate"] = a["L0_ffn_gate_w"].T
    small["wr"] = a["L1_ffn_Wr"]
    packed, packed_once = (np.concatenate([np.ascontiguousarray(small[n]).reshape(P, -1) for n in names], axis=1)
                           for names in (SMALL, ONCE))

    def up(shared, w):
        return np.concatenate([shared, w.transpose(2, 0, 1).reshape(D, -1)], axis=1)

    wd = np.concatenate([a["L0_ffn_sd_w"].T, a["L0_ffn_ed_w"].transpose(0, 2, 1).reshape(-1, D)], axis=0)
    w1 = np.concatenate([a["L1_ffn_Ws1"], np.zeros((D, 64), f32), a["L1_ffn_W1"].transpose(1, 0, 2).reshape(D, -1)], axis=1)
    w2 = np.concatenate([a["L1_ffn_Ws2"], np.zeros((64, D), f32), a["L1_ffn_W2"].reshape(-1, D)], axis=0)
    arrays = {
        "x": a["L0_attn_x"], "small": packed, "once": packed_once, "wqk": wqk, "wv": a["L0_attn_wv"].T,
        "wo": a["L0_attn_wo"].T.reshape(NP, P, D).transpose(1, 0, 2).reshape(P, NP * D),
        "wg": up(a["L0_ffn_sg_w"].T, a["L0_ffn_eg_w"]), "wu": up(a["L0_ffn_su_w"].T, a["L0_ffn_eu_w"]),
        "wd": wd.reshape(NJ, P, D).transpose(1, 0, 2).reshape(P, NJ * D),
        "win": a["L1_attn_W_in"].T, "w1": w1, "w2": w2.reshape(NJ2, P, D).transpose(1, 0, 2).reshape(P, NJ2 * D),
    }

    nc = bacc.Bacc("TRN2", target_bir_lowering=False, num_devices=1)
    feeds, args = {}, []
    for name, t in arrays.items():
        t = np.ascontiguousarray(t)
        feeds[f"in_{name}"] = t
        args.append(nc.dram_tensor(f"in_{name}", t.shape, mybir.dt.from_np(t.dtype), kind="ExternalInput").ap())
    args.append(nc.dram_tensor("out_x", (NB, S, D), F32, kind="ExternalOutput").ap())
    layers_kernel(nc, *args)
    r = run(nc, [feeds], core_ids=[0])
    return r.results[0]["out_x"]
```
